# Optimizing a Trainium2 kernel written in Bass

```python
import numpy as np
import jax
import jax.numpy as jnp

def _softmax(x, axis=-1):
    return jax.nn.softmax(x, axis=axis)

def _gelu(x):
    return jax.nn.gelu(x, approximate=True)

def _silu(x):
    return jax.nn.silu(x)

def _sigmoid(x):
    return jax.nn.sigmoid(x)

def _layernorm(x, axis=-1, eps=1e-05):
    m = jnp.mean(x, axis=axis, keepdims=True)
    v = jnp.var(x, axis=axis, keepdims=True)
    return (x - m) / jnp.sqrt(v + eps)

def _scatter_add(tgt, idx, src, axis=0):
    return tgt.at[idx].add(src)

def _segment_sum(src, seg, n):
    return jax.ops.segment_sum(src, seg, n)
kernel_name = 'mk_hybrid_d1_jaxref_r8_314518'

def setup_inputs(seed: int=0):
    np.random.seed(seed)
    _w = jnp.asarray

    def _L0_attn_a_setup():
        import jax, jax.numpy as jnp
        import numpy as np
        D_MODEL = 128
        NUM_HEADS = 16
        D_HEAD = 64
        N_CTX = 256
        BATCH = 4
        NEG_INF = -10000000000.0
        key = jax.random.key(seed)
        k1, k2, k3, k4, k5 = jax.random.split(key, 5)
        s = 1.0 / np.sqrt(D_MODEL).astype(np.float32)
        x = jax.random.normal(k1, (BATCH, N_CTX, D_MODEL), dtype=jnp.float32)
        W_K = jax.random.normal(k2, (NUM_HEADS, D_HEAD, D_MODEL), dtype=jnp.float32) * s
        W_Q = jax.random.normal(k3, (NUM_HEADS, D_HEAD, D_MODEL), dtype=jnp.float32) * s
        W_V = jax.random.normal(k4, (NUM_HEADS, D_HEAD, D_MODEL), dtype=jnp.float32) * s
        W_O = jax.random.normal(k5, (D_MODEL, NUM_HEADS * D_HEAD), dtype=jnp.float32) * s
        return {'x': x, 'W_K': W_K, 'W_Q': W_Q, 'W_V': W_V, 'W_O': W_O}
    _L0_attn_a_in = _L0_attn_a_setup()

    def _L0_attn_b_setup():
        import jax, jax.numpy as jnp
        import numpy as np
        B, T, C, H = (2, 128, 128, 16)
        D = C // H
        EPS = 1e-06
        key = jax.random.key(seed)
        k1, k2, k3, k4, k5 = jax.random.split(key, 5)
        s = 0.02
        return {'x': jax.random.normal(k1, (B, T, C), dtype=jnp.float32), 'w_qkv': jax.random.normal(k2, (3 * C, C), dtype=jnp.float32) * s, 'b_qkv': jax.random.normal(k3, (3 * C,), dtype=jnp.float32) * s, 'w_out': jax.random.normal(k4, (C, C), dtype=jnp.float32) * s, 'b_out': jax.random.normal(k5, (C,), dtype=jnp.float32) * s}
    _L0_attn_b_in = _L0_attn_b_setup()

    def _L0_ffn_setup():
        import jax, jax.numpy as jnp
        import numpy as np
        E, D, F, GATE_DIM = (8, 128, 512, 16)
        B, T = (2, 256)
        key = jax.random.key(seed)
        ks = jax.random.split(key, 7)
        s = 0.02
        return {'hidden_states': jax.random.normal(ks[0], (B, T, D), dtype=jnp.float32), 'w_red': jax.random.normal(ks[1], (D, GATE_DIM), dtype=jnp.float32) * s, 'wg': jax.random.normal(ks[2], (E, GATE_DIM), dtype=jnp.float32), 'w1': jax.random.normal(ks[3], (E, D, F), dtype=jnp.float32) * s, 'b1': jax.random.normal(ks[4], (E, F), dtype=jnp.float32) * s, 'w2': jax.random.normal(ks[5], (E, F, D), dtype=jnp.float32) * s, 'b2': jax.random.normal(ks[6], (E, D), dtype=jnp.float32) * s}
    _L0_ffn_in = _L0_ffn_setup()
    _d = {'L0_attn_a_x': _L0_attn_a_in['x'], 'L0_attn_a_W_K': _L0_attn_a_in['W_K'], 'L0_attn_a_W_Q': _L0_attn_a_in['W_Q'], 'L0_attn_a_W_V': _L0_attn_a_in['W_V'], 'L0_attn_a_W_O': _L0_attn_a_in['W_O'], 'L0_attn_b_w_qkv': _L0_attn_b_in['w_qkv'], 'L0_attn_b_b_qkv': _L0_attn_b_in['b_qkv'], 'L0_attn_b_w_out': _L0_attn_b_in['w_out'], 'L0_attn_b_b_out': _L0_attn_b_in['b_out'], 'L0_ffn_w_red': _L0_ffn_in['w_red'], 'L0_ffn_wg': _L0_ffn_in['wg'], 'L0_ffn_w1': _L0_ffn_in['w1'], 'L0_ffn_b1': _L0_ffn_in['b1'], 'L0_ffn_w2': _L0_ffn_in['w2'], 'L0_ffn_b2': _L0_ffn_in['b2']}
    _x0 = _d['L0_attn_a_x']
    _d['L0_attn_a_x'] = jax.random.normal(jax.random.fold_in(jax.random.key(seed), 1), (1, 2048, 128), dtype=_x0.dtype)
    del _x0
    return _d

def reference(L0_attn_a_x, L0_attn_a_W_K, L0_attn_a_W_Q, L0_attn_a_W_V, L0_attn_a_W_O, L0_attn_b_w_qkv, L0_attn_b_b_qkv, L0_attn_b_w_out, L0_attn_b_b_out, L0_ffn_w_red, L0_ffn_wg, L0_ffn_w1, L0_ffn_b1, L0_ffn_w2, L0_ffn_b2):

    def _L0_attn_a_ref(x, W_K, W_Q, W_V, W_O):
        import jax, jax.numpy as jnp
        import numpy as np
        D_MODEL = 128
        NUM_HEADS = 16
        D_HEAD = 64
        N_CTX = 256
        BATCH = 4
        NEG_INF = -10000000000.0
        b, q_len, d_model = x.shape
        d_head = W_K.shape[1]
        K = jnp.einsum('bpd,ihd->biph', x, W_K)
        Q = jnp.einsum('bpd,ihd->biph', x, W_Q)
        V = jnp.einsum('bpd,ihd->biph', x, W_V)
        scores = jnp.einsum('biph,biqh->biqp', K, Q)
        mask = jnp.tril(jnp.ones((q_len, q_len), dtype=bool))
        scores = jnp.where(mask[None, None, :, :], scores, NEG_INF)
        attn = jax.nn.softmax(scores / np.sqrt(d_head).astype(np.float32), axis=-1)
        z = jnp.einsum('biph,biqp->biqh', V, attn)
        z_flat = jnp.transpose(z, (0, 2, 1, 3)).reshape(b, q_len, -1)
        out = jnp.einsum('bqf,df->bqd', z_flat, W_O)
        return out

    def _L0_attn_b_ref(x, w_qkv, b_qkv, w_out, b_out):
        import jax, jax.numpy as jnp
        import numpy as np
        B, T, C, H = (2, 128, 128, 16)
        D = C // H
        EPS = 1e-06
        b, t, c = x.shape
        qkv = x @ w_qkv.T + b_qkv
        q, k, v = jnp.split(qkv, 3, axis=-1)

        def to_heads(u):
            return u.reshape(b, t, H, D).transpose(0, 2, 1, 3).astype(jnp.float32)
        q, k, v = (to_heads(q), to_heads(k), to_heads(v))
        q_prime = jax.nn.elu(q) + 1.0
        k_prime = jax.nn.elu(k) + 1.0
        kv_cumsum = jnp.cumsum(jnp.einsum('bhtd,bhte->bhtde', k_prime, v), axis=2)
        context = jnp.einsum('bhtd,bhtde->bhte', q_prime, kv_cumsum)
        norm = jnp.einsum('bhtd,bhtd->bht', q_prime, jnp.cumsum(k_prime, axis=2))
        out = context / (norm[..., None] + EPS)
        out = out.astype(x.dtype).transpose(0, 2, 1, 3).reshape(b, t, c)
        return out @ w_out.T + b_out

    def _L0_ffn_ref(hidden_states, w_red, wg, w1, b1, w2, b2):
        import jax, jax.numpy as jnp
        import numpy as np
        E, D, F, GATE_DIM = (8, 128, 512, 16)
        B, T = (2, 256)
        b, t, c = hidden_states.shape
        x = hidden_states.reshape(-1, c)
        red = x @ w_red
        wg_n = wg / jnp.maximum(jnp.linalg.norm(wg, axis=1, keepdims=True), 0.0001)
        logits = red @ wg_n.T
        gates = jax.nn.softmax(logits, axis=1)
        idx = jnp.argmax(gates, axis=1)
        scores = jnp.take_along_axis(gates, idx[:, None], axis=1)
        h = jax.nn.gelu(jnp.einsum('td,edf->etf', x, w1) + b1[:, None, :], approximate=False)
        y = jnp.einsum('etf,efd->etd', h, w2) + b2[:, None, :]
        out = jnp.take_along_axis(y, idx[None, :, None], axis=0)[0]
        out = out * scores
        return out.reshape(b, t, c)
    x = L0_attn_a_x
    x = x + _L0_attn_a_ref(_layernorm(x, axis=-1), L0_attn_a_W_K, L0_attn_a_W_Q, L0_attn_a_W_V, L0_attn_a_W_O)
    x = x + _L0_ffn_ref(_layernorm(x, axis=-1), L0_ffn_w_red, L0_ffn_wg, L0_ffn_w1, L0_ffn_b1, L0_ffn_w2, L0_ffn_b2)
    x = x + _L0_attn_b_ref(_layernorm(x, axis=-1), L0_attn_b_w_qkv, L0_attn_b_b_qkv, L0_attn_b_w_out, L0_attn_b_b_out)
    x = x + _L0_ffn_ref(_layernorm(x, axis=-1), L0_ffn_w_red, L0_ffn_wg, L0_ffn_w1, L0_ffn_b1, L0_ffn_w2, L0_ffn_b2)
    return x

_drawn_inputs = setup_inputs


def setup_inputs(seed=0):
    import zlib

    import numpy as np

    out = dict(_drawn_inputs(seed))
    spreads = {}
    factors = {'L0_attn_b_w_qkv': 6.649,
     'L0_attn_b_b_qkv': 8.0,
     'L0_attn_b_w_out': 6.869,
     'L0_attn_b_b_out': 3.005,
     'L0_ffn_w_red': 3.377,
     'L0_ffn_wg': 3.364,
     'L0_ffn_w1': 3.438,
     'L0_ffn_b1': 8.0,
     'L0_ffn_w2': 3.362,
     'L0_ffn_b2': 8.0}
    for name, (base, spread) in spreads.items():
        noise = np.random.default_rng([zlib.crc32(name.encode()), seed]).standard_normal(out[name].shape)
        drawn = base * np.exp(spread * noise) if base else spread * noise
        out[name] = jnp.asarray(drawn.astype(out[name].dtype))
    for name, factor in factors.items():
        out[name] = (out[name] * factor).astype(out[name].dtype)
    return out
```

```python
from contextlib import ExitStack

import concourse.bass as bass
from concourse import mybir

F32 = mybir.dt.float32
F32R = mybir.dt.float32r
BF16 = mybir.dt.bfloat16
I32 = mybir.dt.int32
U32 = mybir.dt.uint32
ALU = mybir.AluOpType
ACT = mybir.ActivationFunctionType
AX = mybir.AxisListType

P = 128
BANK = 512
MASKED = -1e30
LN_EPS = 1e-5


class Shapes:

    def __init__(self, x, w_k, w_g, w_1):
        self.T, self.D = x.shape[1], x.shape[2]
        self.H, self.DH = w_k.shape[0], w_k.shape[1]
        self.NT = self.T // P
        self.NC = self.T // BANK
        self.TPC = BANK // P
        self.PAIRS = self.H * self.DH // P
        self.HL = 16
        self.E, self.GD = w_g.shape
        self.FCH = w_1.shape[2] // P
        self.SLOTS = -(-(self.NT + self.E - 1) // 4) * 4


def make_identity(pool, tile, done, ready):
    pool.memset(tile, 0.0).then_inc(done, 1)
    pool.wait_ge(done, 1)
    pool.affine_select(out=tile, in_=tile, compare_op=ALU.not_equal, fill=1.0, base=0,
                       pattern=[[-1, P]], channel_multiplier=1).then_inc(ready, 1)


def attention(nc, shp, keep, x_in, w_k, w_q, w_v, w_o):
    T, D, DH, NT, NC, TPC, PAIRS = shp.T, shp.D, shp.DH, shp.NT, shp.NC, shp.TPC, shp.PAIRS
    x, ident = keep["x"], keep["ident"]
    SCALE = float(DH) ** -0.5
    ROWS = range(NT)
    RING = 5

    def chunks(r):
        return r // TPC + 1

    def width(r, c):
        return min(BANK, (r + 1) * P - c * BANK)

    first_chunk, first_group = {}, {}
    n = g = 0
    for r in ROWS:
        first_group[r] = g
        g += chunks(r)
        for h in range(2):
            first_chunk[r, h] = n
            n += chunks(r)
    N_SC, N_GR = n, g
    N_PJ = 3 * NC
    N_V = NC

    def merged(front, back):
        out, nf, nb = [], len(front), len(back)
        i = j = 0
        while i < nf or j < nb:
            if j >= nb or (i < nf and i * nb <= j * nf):
                out.append(front[i])
                i += 1
            else:
                out.append(back[j])
                j += 1
        return out

    def back_of(r):
        items = []
        for c in range(chunks(r)):
            items += [("turn", r, 0, c), ("turn", r, 1, c)]
            if c:
                items.append(("value", r, c - 1))
        return items + [("value", r, chunks(r) - 1)]

    order = []
    for s in range(NT + 1):
        if s < NT:
            front = [("score", s, h, c) for h in range(2) for c in range(chunks(s))]
        else:
            front = [("project", j) for j in range(N_PJ)]
        body = merged(front, back_of(s - 1) if s else [])
        if s >= 2:
            body = [("out", s - 2), body[0], ("out2", s - 2)] + body[1:]
        order += body
    values = [("vproject", m) for m in range(N_V)]
    order += values + [("out", NT - 1), ("out2", NT - 1)]
    opening = [("project", j) for j in range(N_PJ)] + values

    with ExitStack() as ctx:
        def sb(name, shape, dt=F32):
            return ctx.enter_context(nc.sbuf_tensor("at_" + name, shape, dt))

        sems = []

        def sem(name):
            sems.append(nc.alloc_semaphore("at_" + name))
            return sems[-1]

        ps = [ctx.enter_context(nc.psum_tensor(f"at_ps{i}", [P, BANK], F32)) for i in range(8)]
        ring = ps[:RING]
        turn_ps = ps[RING:RING + 2]
        zo_ps = ps[RING + 2]
        z_ps, o_ps = zo_ps[:, 0:P], zo_ps[:, P:3 * P]

        stats = sb("stats", [P, NT, 6])
        mv = sb("mv", [P, NT, 2])
        rstd = sb("rstd", [P, NT])
        xn = sb("xn", [P, NT, D])
        xnT = sb("xnT", [D, T])
        wnat = {n: sb("wnat_" + n, [P, PAIRS, P]) for n in "qkv"}
        wnat_o = sb("wnat_o", [D, PAIRS * P])
        wT = {n: sb("wT_" + n, [P, PAIRS + 1, P]) for n in "qkv"}
        wo_bd = sb("wo_bd", [P, PAIRS, 2, D])
        wq_fix = sb("wq_fix", [D, 2, 2, DH])
        wk_fix = sb("wk_fix", [D, P])
        k_st = [sb(f"k_st{h}", [P, T], F32R) for h in range(2)]
        q_hi = [sb(f"q_hi{h}", [P, T], F32R) for h in range(2)]
        q_lo = [sb(f"q_lo{h}", [P, T], F32R) for h in range(2)]
        v = sb("v", [P, NT, P])
        prob = [[sb(f"prob{k}{h}", [P, T]) for h in range(2)] for k in range(2)]
        probT = [[sb(f"probT{h}{k}", [P, BANK]) for k in range(2)] for h in range(2)]
        zT = [sb(f"zT{k}", [P, P]) for k in range(2)]
        cmax = sb("cmax", [P, 2, 2, NC])
        nmax = sb("nmax", [P, 2, 2])
        esum = sb("esum", [P, 2, 2, NC])
        rsum = sb("rsum", [P, 2, 2])
        rinv = sb("rinv", [P, 2, 2])
        identb = sb("identb", [P, P], BF16)
        maskb = sb("maskb", [P, P], BF16)

        s_xin, s_win = sem("s_xin"), [sem(f"s_win{i}") for i in range(4)]
        s_c0, s_c1, s_c2, s_const = sem("s_c0"), sem("s_c1"), sem("s_c2"), sem("s_const")
        s_stat, s_aggr, s_std, s_rstd, s_xn = (sem(n) for n in ("s_stat", "s_aggr", "s_std", "s_rstd", "s_xn"))
        s_setT, s_setcp = sem("s_setT"), sem("s_setcp")
        s_wfix = sem("s_wfix")
        s_proj, s_hi, s_lo = sem("s_proj"), sem("s_hi"), sem("s_lo")
        s_vproj, s_v = sem("s_vproj"), sem("s_v")
        s_score, s_cmax, s_nmax, s_exp = sem("s_score"), sem("s_cmax"), sem("s_nmax"), sem("s_exp")
        s_turn = [sem(f"s_turn{h}") for h in range(2)]
        s_probT = [sem(f"s_probT{h}") for h in range(2)]
        s_z, s_zT, s_o = sem("s_z"), sem("s_zT"), sem("s_o")
        s_rsum, s_rinv, s_acc1, s_acc2 = sem("s_rsum"), sem("s_rinv"), sem("s_acc1"), sem("s_acc2")

        N_SET = 4 * PAIRS // TPC + NC

        with nc.Block() as block:

            @block.sync
            def _(sp):
                sp.dma_start(x[:, :, :], x_in[0].rearrange("(t p) d -> p t d", p=P)).then_inc(s_xin, 16)
                for i, (n, w) in enumerate((("q", w_q), ("k", w_k), ("v", w_v))):
                    sp.dma_start(wnat[n][:, :, :],
                                 w.rearrange("h f d -> (h f) d").rearrange("(a p) d -> p a d", p=P)).then_inc(s_win[i], 16)
                sp.dma_start(wnat_o[:, :], w_o).then_inc(s_win[3], 16)

            @block.gpsimd
            def _(pool):
                pool.sem_inc(s_probT[0], 1)
                pool.sem_inc(s_probT[1], 1)
                pool.sem_inc(s_acc2, 1)
                make_identity(pool, ident[:, :], s_c0, s_const)
                make_identity(pool, identb[:, :], s_c1, s_const)
                pool.memset(maskb[:, :], 0.0).then_inc(s_c2, 1)
                pool.wait_ge(s_c2, 1)
                pool.affine_select(out=maskb[:, :], in_=maskb[:, :], compare_op=ALU.is_ge, fill=MASKED, base=0,
                                   pattern=[[-1, P]], channel_multiplier=1).then_inc(s_const, 1)
                for n in "qkv":
                    pool.memset(wT[n][:, PAIRS, :], 0.0).then_inc(s_const, 1)
                pool.memset(wo_bd[:, :, :, :], 0.0).then_inc(s_const, 1)
                pool.wait_ge(s_const, 7)
                pool.wait_ge(s_setcp, N_SET - NC)

                def projection_weights(pair):
                    cols = wT["q"][:, bass.ds(pair, 1), :].rearrange("d a (h f) -> d (a h) f", h=2)
                    for copy in range(2):
                        pool.tensor_copy(wq_fix[:, :, copy, :], cols)
                    pool.tensor_copy(wk_fix[:, :], wT["k"][:, bass.ds(pair, 1), :]
                                     .rearrange("d a f -> d (a f)")).then_inc(s_wfix, 1)

                projection_weights(0)
                with pool.Fori(0, PAIRS) as pair:
                    pool.wait_ge(s_proj, N_PJ * (pair + 1))
                    projection_weights(pair + 1)

            @block.vector
            def _(dve):
                dve.wait_ge(s_xin, 16)
                for t in range(NT):
                    dve.bn_stats(stats[:, t, :], x[:, t, :]).then_inc(s_stat, 1)
                for t in range(NT):
                    dve.wait_ge(s_stat, t + 1)
                    dve.bn_aggr(mv[:, t, :], stats[:, t, :]).then_inc(s_aggr, 1)
                dve.wait_ge(s_std, 1)
                dve.reciprocal(rstd[:, :], rstd[:, :]).then_inc(s_rstd, 1)
                dve.wait_ge(s_rstd, 1)
                for t in range(NT):
                    dve.tensor_scalar(xn[:, t, :], x[:, t, :], mv[:, t, 0:1], rstd[:, t:t + 1],
                                      ALU.subtract, ALU.mult).then_inc(s_xn, 1)

                def low_parts(j, made):
                    kind, c = divmod(j, NC)
                    cols = slice(c * BANK, (c + 1) * BANK)
                    bank = ring[(N_SC + j) % RING]
                    dve.wait_ge(s_hi, N_PJ * made + j + 1)
                    if kind == 0:
                        for h in range(2):
                            here, there = slice(DH * h, DH * (h + 1)), slice(DH * (1 - h), DH * (2 - h))
                            last = dve.tensor_tensor(k_st[h][there, cols], bank[here, :],
                                                     k_st[h][here, cols].bitcast(F32), ALU.subtract)
                    else:
                        last = dve.scalar_tensor_tensor(q_lo[kind - 1][:, cols], bank[:, :], SCALE,
                                                        q_hi[kind - 1][:, cols].bitcast(F32), ALU.mult, ALU.subtract)
                    last.then_inc(s_lo, 1)

                def run(items, pair, made):
                    for it in items:
                        if it[0] == "score":
                            _, r, h, c = it
                            k = first_chunk[r, h] + c
                            bank = ring[k % RING][:, 0:width(r, c)]
                            dve.wait_ge(s_score, N_SC * pair + k + 1)
                            if chunks(r) == 1:
                                dve.tensor_reduce(nmax[:, r % 2, h:h + 1], bank, AX.X, ALU.max, negate=True).then_inc(s_nmax, 1)
                                continue
                            dve.tensor_reduce(cmax[:, r % 2, h, c:c + 1], bank, AX.X, ALU.max).then_inc(s_cmax, 1)
                            if c == chunks(r) - 1:
                                dve.wait_ge(s_cmax, (N_SC - first_chunk[TPC, 0]) * pair + k + 1 - first_chunk[TPC, 0])
                                dve.tensor_reduce(nmax[:, r % 2, h:h + 1], cmax[:, r % 2, h, 0:c + 1], AX.X, ALU.max,
                                                  negate=True).then_inc(s_nmax, 1)
                        elif it[0] == "turn" and it[2] == 1:
                            _, r, h, c = it
                            g = first_group[r] + c
                            w = width(r, c)
                            dve.wait_ge(s_turn[1], N_GR * pair + g + 1)
                            dve.tensor_copy(probT[1][g % 2][:, 0:w], turn_ps[1][:, 0:w]).then_inc(s_probT[1], 1)
                            if c == 0:
                                dve.wait_ge(s_exp, N_SC * pair + first_chunk[r, 1] + chunks(r))
                                dve.tensor_reduce(rsum[:, r % 2, :], esum[:, r % 2, :, 0:chunks(r)], AX.X, ALU.add).then_inc(s_rsum, 1)
                        elif it[0] == "out":
                            r = it[1]
                            dve.wait_ge(s_rsum, NT * pair + r + 1)
                            dve.reciprocal(rinv[:, r % 2, :], rsum[:, r % 2, :]).then_inc(s_rinv, 1)
                            dve.wait_ge(s_o, NT * pair + r + 1)
                            dve.wait_ge(s_rinv, NT * pair + r + 1)
                            dve.scalar_tensor_tensor(x[:, r, :], o_ps[:, 0:D], rinv[:, r % 2, 0:1], x[:, r, :],
                                                     ALU.mult, ALU.add).then_inc(s_acc1, 1)
                        elif it[0] == "out2":
                            r = it[1]
                            dve.wait_ge(s_acc1, NT * pair + r + 1)
                            dve.scalar_tensor_tensor(x[:, r, :], o_ps[:, D:2 * D], rinv[:, r % 2, 1:2], x[:, r, :],
                                                     ALU.mult, ALU.add).then_inc(s_acc2, 1)
                        elif it[0] == "project":
                            low_parts(it[1], made)

                run(opening, 0, 0)
                with dve.Fori(0, PAIRS) as pair:
                    run(order, pair, pair + 1)

            @block.scalar
            def _(act):
                act.wait_ge(s_aggr, NT)
                act.activation(rstd[:, :], mv[:, :, 1], ACT.Sqrt, bias=keep["eps"][:, 0:1]).then_inc(s_std, 1)
                W_GROUPS = PAIRS // TPC
                dst = [wT[n][:, TPC * i:TPC * (i + 1), :] for n in "qkv" for i in range(W_GROUPS)]
                dst = [d.rearrange("p a f -> p (a f)") for d in dst]
                act.wait_ge(s_const, 7)
                for i in range(N_SET):
                    act.wait_ge(s_setT, i + 1)
                    if i < 3 * W_GROUPS:
                        last = act.activation(dst[i], ps[i % 8][:, :], ACT.Copy)
                    elif i < 4 * W_GROUPS:
                        pairs = slice(TPC * (i - 3 * W_GROUPS), TPC * (i - 3 * W_GROUPS + 1))
                        for h in range(2):
                            rows = slice(DH * h, DH * (h + 1))
                            last = act.activation(wo_bd[rows, pairs, h, :],
                                                  ps[i % 8][rows, :].rearrange("p (a d) -> p a d", d=D), ACT.Copy)
                    else:
                        c = i - 4 * W_GROUPS
                        last = act.activation(xnT[:, c * BANK:(c + 1) * BANK], ps[i % 8][:, :], ACT.Copy)
                    last.then_inc(s_setcp, 1)

                def run(items, pair, made):
                    for it in items:
                        if it[0] == "score":
                            _, r, h, c = it
                            if c < chunks(r) - 1:
                                continue
                            act.wait_ge(s_nmax, 2 * NT * pair + 2 * r + h + 1)
                            for c in range(chunks(r)):
                                k, w = first_chunk[r, h] + c, width(r, c)
                                act.activation(prob[r % 2][h][:, c * BANK:c * BANK + w], ring[k % RING][:, 0:w], ACT.Exp,
                                               bias=nmax[:, r % 2, h:h + 1],
                                               accum_out=esum[:, r % 2, h, c:c + 1]).then_inc(s_exp, 1)
                        elif it[0] == "turn" and it[2] == 0:
                            _, r, h, c = it
                            g = first_group[r] + c
                            w = width(r, c)
                            act.wait_ge(s_turn[0], N_GR * pair + g + 1)
                            act.activation(probT[0][g % 2][:, 0:w], turn_ps[0][:, 0:w], ACT.Copy).then_inc(s_probT[0], 1)
                        elif it[0] == "value" and it[2] == chunks(it[1]) - 1:
                            r = it[1]
                            act.wait_ge(s_z, NT * pair + r + 1)
                            act.activation(zT[r % 2][:, :], z_ps, ACT.Copy).then_inc(s_zT, 1)
                        elif it[0] == "project":
                            kind, c = divmod(it[1], NC)
                            cols = slice(c * BANK, (c + 1) * BANK)
                            bank = ring[(N_SC + it[1]) % RING]
                            act.wait_ge(s_proj, N_PJ * made + it[1] + 1)
                            if kind == 0:
                                for h in range(2):
                                    rows = slice(DH * h, DH * (h + 1))
                                    last = act.activation(k_st[h][rows, cols], bank[rows, :], ACT.Copy)
                            else:
                                last = act.activation(q_hi[kind - 1][:, cols], bank[:, :], ACT.Copy, scale=SCALE)
                            last.then_inc(s_hi, 1)
                        elif it[0] == "vproject":
                            m = it[1]
                            act.wait_ge(s_vproj, N_V * made + m + 1)
                            act.activation(v[:, TPC * m:TPC * (m + 1), :].rearrange("p t f -> p (t f)"),
                                           ring[(N_SC + N_PJ + m) % RING][:, :], ACT.Copy).then_inc(s_v, 1)

                run(opening, 0, 0)
                with act.Fori(0, PAIRS) as pair:
                    run(order, pair, pair + 1)

            @block.tensor
            def _(pe):
                pe.wait_ge(s_const, 3)
                src = []
                for i, n in enumerate("qkv"):
                    src += [(s_win[i], 16, wnat[n][:, a, :]) for a in range(PAIRS)]
                src += [(s_win[3], 16, wnat_o[:, a * P:(a + 1) * P]) for a in range(PAIRS)]
                src += [(s_xn, t + 1, xn[:, t, :]) for t in range(NT)]
                for i, (ready, count, tile) in enumerate(src):
                    grp, k = divmod(i, TPC)
                    if k == 0 and grp >= 8:
                        pe.wait_ge(s_setcp, grp - 7)
                    pe.wait_ge(ready, count)
                    last = pe.transpose(ps[grp % 8][:, k * P:(k + 1) * P], tile, ident[:, :])
                    if k == TPC - 1:
                        last.then_inc(s_setT, 1)
                pe.wait_ge(s_setcp, N_SET)

                def free_bank(use, pair, made):
                    before = use - RING
                    if before < 0:
                        uses, made = N_SC + N_PJ + N_V, made - 1
                        before = max(u for u in range(uses) if u % RING == use % RING)
                    if before >= N_SC + N_PJ:
                        pe.wait_ge(s_v, N_V * made + before - N_SC - N_PJ + 1)
                    elif before >= N_SC:
                        pe.wait_ge(s_lo, N_PJ * made + before - N_SC + 1)
                    else:
                        pe.wait_ge(s_exp, N_SC * pair + before + 1)

                def run(items, pair, made, first):
                    for it in items:
                        if it[0] == "score":
                            _, r, h, c = it
                            if r == 0 and h == 0:
                                pe.wait_ge(s_lo, N_PJ * made)
                            k, w = first_chunk[r, h] + c, width(r, c)
                            free_bank(k, pair, made)
                            bank = ring[k % RING]
                            keys = k_st[h][:, c * BANK:c * BANK + w]
                            pe.matmul(bank[:, 0:w], q_hi[h][:, r * P:(r + 1) * P], keys, start=True, stop=False)
                            if c == chunks(r) - 1:
                                pe.matmul(bank[:, w - P:w], identb[:, :], maskb[:, :], start=False, stop=False)
                            last = pe.matmul(bank[:, 0:w], q_lo[h][:, r * P:(r + 1) * P], keys, start=False, stop=True)
                            last.then_inc(s_score, 1)
                        elif it[0] == "turn":
                            _, r, h, c = it
                            g = first_group[r] + c
                            pe.wait_ge(s_exp, N_SC * pair + first_chunk[r, h] + c + 1)
                            pe.wait_ge(s_probT[h], N_GR * pair + g + 1)
                            for b in range(width(r, c) // P):
                                cols = slice(c * BANK + b * P, c * BANK + (b + 1) * P)
                                last = pe.transpose(turn_ps[h][:, b * P:(b + 1) * P], prob[r % 2][h][:, cols], ident[:, :])
                            last.then_inc(s_turn[h], 1)
                        elif it[0] == "value":
                            _, r, c = it
                            g = first_group[r] + c
                            if r == 0:
                                pe.wait_ge(s_v, N_V * made)
                            if c == 0:
                                pe.wait_ge(s_acc2, NT * pair + r + 1)
                            for h in range(2):
                                pe.wait_ge(s_probT[h], N_GR * pair + g + 2)
                            for b in range(width(r, c) // P):
                                t = c * TPC + b
                                for h in range(2):
                                    rows = slice(DH * h, DH * (h + 1))
                                    last = pe.matmul(z_ps[rows, :], v[:, t, rows], probT[h][g % 2][:, b * P:(b + 1) * P],
                                                     start=t == 0, stop=t == r)
                            if c == chunks(r) - 1:
                                last.then_inc(s_z, 1)
                        elif it[0] == "out":
                            r = it[1]
                            pe.wait_ge(s_zT, NT * pair + r + 1)
                            pe.matmul(o_ps, zT[r % 2][:, :], wo_bd[:, bass.ds(pair, 1), :, :].rearrange("f a h d -> f (a h d)"),
                                      start=True, stop=True).then_inc(s_o, 1)
                        elif it[0] == "project":
                            j = it[1]
                            kind, c = divmod(j, NC)
                            if j == 0:
                                pe.wait_ge(s_wfix, made + 1)
                            if not first or j >= RING:
                                free_bank(N_SC + j, pair, made)
                            w = wk_fix[:, :] if kind == 0 else wq_fix[:, kind - 1, :, :].rearrange("d a f -> d (a f)")
                            pe.matmul(ring[(N_SC + j) % RING][:, :], w, xnT[:, c * BANK:(c + 1) * BANK],
                                      start=True, stop=True).then_inc(s_proj, 1)
                        elif it[0] == "vproject":
                            m = it[1]
                            free_bank(N_SC + N_PJ + m, pair, made)
                            bank = ring[(N_SC + N_PJ + m) % RING]
                            wv = wT["v"][:, bass.ds(made, 1), :].rearrange("d a f -> d (a f)")
                            for b in range(TPC):
                                t = m * TPC + b
                                last = pe.matmul(bank[:, b * P:(b + 1) * P], xnT[:, t * P:(t + 1) * P], wv, start=True, stop=True)
                            last.then_inc(s_vproj, 1)

                run(opening, 0, 0, True)
                with pe.Fori(0, PAIRS) as pair:
                    run(order, pair, pair + 1, False)

        nc.clear_and_free_semaphores(sems)
        nc.all_engine_barrier()


def layernorm_steps(keep, shp, stats, mv, rstd, s_stat, s_aggr, s_std, s_rstd):
    x = keep["x"]

    def on_vector(dve):
        for t in range(shp.NT):
            dve.bn_stats(stats[:, t, :], x[:, t, :]).then_inc(s_stat, 1)
        for t in range(shp.NT):
            dve.wait_ge(s_stat, t + 1)
            dve.bn_aggr(mv[:, t, :], stats[:, t, :]).then_inc(s_aggr, 1)
        dve.wait_ge(s_std, 1)
        dve.reciprocal(rstd[:, :], rstd[:, :]).then_inc(s_rstd, 1)
        dve.wait_ge(s_rstd, 1)

    def on_scalar(act):
        act.wait_ge(s_aggr, shp.NT)
        act.activation(rstd[:, :], mv[:, :, 1], ACT.Sqrt, bias=keep["eps"][:, 0:1]).then_inc(s_std, 1)

    return on_vector, on_scalar


def skewed(eng, tiles, ring, offsets, emit):
    deepest = max(offsets.values())
    head = -(-(deepest + ring) // ring) * ring

    def peeled(steps):
        for n in steps:
            for stage, off in offsets.items():
                if 0 <= n - off < tiles:
                    emit(stage, 0, n - off)

    peeled(range(head))
    with eng.Fori(head // ring, tiles // ring) as turn:
        for phase in range(ring):
            for stage, off in offsets.items():
                emit(stage, turn, phase - off)
    peeled(range(tiles, tiles + deepest))


def static_tile(turn, c):
    return c if isinstance(turn, int) else None


def ffn(nc, shp, keep, tag, w_red, w_g, scratch_in, scratch_out):
    T, D, NT, NC, TPC = shp.T, shp.D, shp.NT, shp.NC, shp.TPC
    E, GD, FCH, SLOTS = shp.E, shp.GD, shp.FCH, shp.SLOTS
    x, ident, wall = keep["x"], keep["ident"], keep["wall"]
    W1, W2, B1, B2 = keep["wall_cols"]
    WCOLS = keep["wall"].shape[2]
    U = 4

    with ExitStack() as ctx:
        def sb(name, shape, dt=F32):
            return ctx.enter_context(nc.sbuf_tensor(tag + name, shape, dt))

        sems = []

        def sem(name):
            sems.append(nc.alloc_semaphore(tag + name))
            return sems[-1]

        ps = [ctx.enter_context(nc.psum_tensor(f"{tag}ps{i}", [P, BANK], F32)) for i in range(8)]
        stats, mv, rstd = sb("stats", [P, NT, 6]), sb("mv", [P, NT, 2]), sb("rstd", [P, NT])
        xn, xnT = sb("xn", [P, NT, D]), sb("xnT", [D, T])
        wred, wg = sb("wred", [D, GD]), sb("wg", [E, GD])
        wg2, wgs, wgr, wgn, wgnT = sb("wg2", [E, GD]), sb("wgs", [E, 1]), sb("wgr", [E, 1]), sb("wgn", [E, GD]), sb("wgnT", [GD, E])
        redT = sb("redT", [GD, T])
        lmax, sub, ex = sb("lmax", [P, NT]), sb("sub", [P, NT, E]), sb("ex", [P, NT, E])
        prio, best = sb("prio", [P, NT, E]), sb("best", [P, NT])
        onehot = sb("onehot", [P, E, NT], BF16)
        den, score = sb("den", [P, NT]), sb("score", [P, NT])
        cnt, incl, excl = sb("cnt", [P, E, NT]), sb("incl", [P, E, NT]), sb("excl", [P, E, NT])
        over, tiles, ends, starts = sb("over", [P, E, NT]), sb("tiles", [P, E]), sb("ends", [P, E]), sb("starts", [P, E])
        place, pos, pos_u = sb("place", [P, E, NT]), sb("pos", [P, NT]), sb("pos_u", [P, NT], U32)
        passed, slot_f, slot_e = sb("passed", [1, SLOTS, E]), sb("slot_f", [1, SLOTS]), sb("slot_e", [1, SLOTS], I32)
        xs = [sb(f"xs{k}", [P, D]) for k in range(U)]
        xsT = [sb(f"xsT{k}", [D, P]) for k in range(U)]
        wfix = [sb(f"wfix{k}", [P, WCOLS]) for k in range(U)]
        hT = [sb(f"hT{k}", [P, FCH, P]) for k in range(U)]
        ys = [sb(f"ys{k}", [P, D]) for k in range(U)]
        got = sb("got", [P, NT, D])

        s_stat, s_aggr, s_std, s_rstd = sem("s_stat"), sem("s_aggr"), sem("s_std"), sem("s_rstd")
        s_gin, s_xn, s_xnTp, s_xnT = sem("s_gin"), sem("s_xn"), sem("s_xnTp"), sem("s_xnT")
        s_wg, s_wgsq, s_wgn, s_wgTp, s_wgT = sem("s_wg"), sem("s_wgsq"), sem("s_wgn"), sem("s_wgTp"), sem("s_wgT")
        s_red, s_redT, s_lg, s_sub, s_ex = sem("s_red"), sem("s_redT"), sem("s_lg"), sem("s_sub"), sem("s_ex")
        s_hot, s_rank, s_chain, s_pos, s_slot = sem("s_hot"), sem("s_rank"), sem("s_chain"), sem("s_pos"), sem("s_slot")
        s_scat = sem("s_scat")
        s_xs = [sem(f"s_xs{k}") for k in range(U)]
        s_xsTp, s_xsT, s_w, s_h, s_gelu, s_y, s_ys = (sem(n) for n in ("s_xsTp", "s_xsT", "s_w", "s_h", "s_gelu", "s_y", "s_ys"))
        s_store = [sem(f"s_store{k}") for k in range(U)]
        s_got = [sem(f"s_got{c}") for c in range(NC)]
        ln_vector, ln_scalar = layernorm_steps(keep, shp, stats, mv, rstd, s_stat, s_aggr, s_std, s_rstd)

        lg_ps, rank_ps = ps[6], ps[7]
        lg = lg_ps[:, 0:NT * E].rearrange("p (t e) -> p t e", e=E)
        wgT_ps = lg_ps[0:GD, BANK - E:BANK]
        rank = rank_ps[:, 0:E * NT].rearrange("p (e t) -> p e t", t=NT)
        count = rank_ps[:, E * NT:2 * E * NT].rearrange("p (e t) -> p e t", t=NT)

        def by_tile(ap):
            return ap.rearrange("p e t -> p t e")

        with nc.Block() as block:

            @block.sync
            def _(sp):
                sp.dma_start(wred[:, :], w_red).then_inc(s_gin, 16)
                sp.dma_start(wg[:, :], w_g).then_inc(s_wg, 16)
                sp.wait_ge(s_scat, 16 * NT)

                def emit(stage, turn, c):
                    s, k, n = U * turn + c, c % U, turn + c // U
                    if stage == "load":
                        if static_tile(turn, c) is None or c >= U:
                            sp.wait_ge(s_xsTp, s - U + 1)
                        sp.dma_start(xs[k][:, :], scratch_in[bass.ds(s * P, P), :]).then_inc(s_xs[k], 16)
                    else:
                        sp.wait_ge(s_ys, s + 1)
                        sp.dma_start(scratch_out[bass.ds(s * P, P), :], ys[k][:, :]).then_inc(s_store[k], 16)

                skewed(sp, SLOTS, U, {"load": 0, "store": U}, emit)
                for k in range(U):
                    sp.wait_ge(s_store[k], 16 * (SLOTS // U))

            @block.gpsimd
            def _(pool):
                pool.wait_ge(s_pos, 1)
                for t in range(NT):
                    pool.indirect_dma_start(scratch_in[:, :], bass.IndirectOffsetOnAxis(ap=pos_u[:, t:t + 1], axis=0),
                                            xn[:, t, :], None).then_inc(s_scat, 16)
                pool.wait_ge(s_slot, 1)

                def emit(stage, turn, c):
                    s, k = U * turn + c, c % U
                    if static_tile(turn, c) is None or c >= U:
                        pool.wait_ge(s_ys, s - U + 1)
                    e = pool.value_load(slot_e[0:1, bass.ds(s, 1)], min_val=0, max_val=E - 1)
                    pool.tensor_copy(wfix[k][:, :], wall[:, bass.ds(e, 1), :].rearrange("p a n -> p (a n)")).then_inc(s_w, 1)

                skewed(pool, SLOTS, U, {"weights": 0}, emit)
                for k in range(U):
                    pool.wait_ge(s_store[k], 16 * (SLOTS // U))
                for t in range(NT):
                    pool.indirect_dma_start(got[:, t, :], None, scratch_out[:, :],
                                            bass.IndirectOffsetOnAxis(ap=pos_u[:, t:t + 1], axis=0)).then_inc(s_got[t // TPC], 16)

            @block.vector
            def _(dve):
                links = [0]

                def link(ins):
                    links[0] += 1
                    ins.then_inc(s_chain, 1)
                    dve.wait_ge(s_chain, links[0])

                dve.wait_ge(s_wg, 16)
                link(dve.tensor_tensor(wg2[:, :], wg[:, :], wg[:, :], ALU.mult))
                dve.tensor_reduce(wgs[:, :], wg2[:, :], AX.X, ALU.add).then_inc(s_wgsq, 1)
                ln_vector(dve)
                for t in range(NT):
                    dve.tensor_scalar(xn[:, t, :], x[:, t, :], mv[:, t, 0:1], rstd[:, t:t + 1],
                                      ALU.subtract, ALU.mult).then_inc(s_xn, 1)
                dve.wait_ge(s_std, 2)
                link(dve.tensor_scalar(wgr[:, :], wgr[:, :], 1e-4, None, ALU.max))
                link(dve.reciprocal(wgr[:, :], wgr[:, :]))
                dve.tensor_scalar(wgn[:, :], wg[:, :], wgr[:, 0:1], None, ALU.mult).then_inc(s_wgn, 1)
                dve.wait_ge(s_wgTp, 1)
                dve.tensor_copy(wgnT[:, :], wgT_ps).then_inc(s_wgT, 1)
                for c in range(NC):
                    dve.wait_ge(s_red, c + 1)
                    dve.tensor_copy(redT[:, c * BANK:(c + 1) * BANK], ps[4 + c % 2][0:GD, :]).then_inc(s_redT, 1)

                dve.wait_ge(s_lg, 1)
                link(dve.tensor_reduce(lmax[:, :], lg, AX.X, ALU.max))
                dve.tensor_tensor(sub[:, :, :], lg, lmax[:, :].unsqueeze(2).to_broadcast([P, NT, E]), ALU.subtract).then_inc(s_sub, 1)
                dve.wait_ge(s_sub, 1)
                link(dve.scalar_tensor_tensor(prio[:, :, :], sub[:, :, :], 0.0, keep["prio"][:, :, :], ALU.is_ge, ALU.mult))
                link(dve.tensor_reduce(best[:, :], prio[:, :, :], AX.X, ALU.max))
                dve.tensor_tensor(by_tile(onehot[:, :, :]), prio[:, :, :], best[:, :].unsqueeze(2).to_broadcast([P, NT, E]),
                                  ALU.is_equal).then_inc(s_hot, 1)
                dve.wait_ge(s_ex, 1)
                link(dve.tensor_reduce(den[:, :], ex[:, :, :], AX.X, ALU.add))
                link(dve.reciprocal(score[:, :], den[:, :]))

                dve.wait_ge(s_rank, 1)
                link(dve.tensor_copy(cnt[:, :, :], count))
                flat = [a[:, :, :].rearrange("p e t -> p (e t)") for a in (incl, keep["restart"], cnt)]
                link(dve.tensor_tensor_scan(flat[0], flat[1], flat[2], 0.0, ALU.mult, ALU.add))
                dve.tensor_tensor(excl[:, :, :], incl[:, :, :], cnt[:, :, :], ALU.subtract)
                link(dve.tensor_tensor(over[:, :, :], incl[:, :, NT - 1:NT].to_broadcast([P, E, NT]), keep["full"][:, :, :], ALU.is_gt))
                link(dve.tensor_reduce(tiles[:, :], over[:, :, :], AX.X, ALU.add))
                link(dve.tensor_tensor_scan(ends[:, :], keep["ones8"][:, :], tiles[:, :], 0.0, ALU.mult, ALU.add))
                link(dve.tensor_tensor(starts[:, :], ends[:, :], tiles[:, :], ALU.subtract))
                link(dve.scalar_tensor_tensor(place[:, :, :], starts[:, :].unsqueeze(2).to_broadcast([P, E, NT]), float(P), excl[:, :, :],
                                              ALU.mult, ALU.add))
                link(dve.tensor_tensor(place[:, :, :], rank, place[:, :, :], ALU.add))
                link(dve.tensor_tensor(place[:, :, :], place[:, :, :], onehot[:, :, :], ALU.mult))
                link(dve.tensor_reduce(pos[:, :], by_tile(place[:, :, :]), AX.X, ALU.add))
                dve.tensor_copy(pos_u[:, :], pos[:, :]).then_inc(s_pos, 1)
                link(dve.tensor_tensor(passed[:, :, :], keep["slots"][:, :, :], ends[0:1, :].unsqueeze(1).to_broadcast([1, SLOTS, E]), ALU.is_ge))
                link(dve.tensor_reduce(slot_f[:, :], passed[:, :, :], AX.X, ALU.add))
                dve.tensor_scalar(slot_e[:, :], slot_f[:, :], float(E - 1), None, ALU.min).then_inc(s_slot, 1)

                def emit(stage, turn, c):
                    s, k = U * turn + c, c % U
                    if stage == "xT":
                        dve.wait_ge(s_xsTp, s + 1)
                        dve.tensor_copy(xsT[k][:, :], ps[c % 2][:, 0:P]).then_inc(s_xsT, 1)
                    else:
                        dve.wait_ge(s_y, s + 1)
                        if static_tile(turn, c) is None or c >= U:
                            dve.wait_ge(s_store[k], 16 * (turn + c // U))
                        dve.tensor_tensor(ys[k][:, :], ps[4 + c % 2][:, 0:D], wfix[k][:, B2], ALU.add).then_inc(s_ys, 1)

                skewed(dve, SLOTS, U, {"xT": 0, "y": 2}, emit)
                for t in range(NT):
                    dve.wait_ge(s_got[t // TPC], 16 * TPC)
                    dve.scalar_tensor_tensor(x[:, t, :], got[:, t, :], score[:, t:t + 1], x[:, t, :], ALU.mult, ALU.add)

            @block.scalar
            def _(act):
                ln_scalar(act)
                act.wait_ge(s_wgsq, 1)
                act.activation(wgr[:, :], wgs[:, :], ACT.Sqrt).then_inc(s_std, 1)
                for c in range(NC):
                    act.wait_ge(s_xnTp, c + 1)
                    act.activation(xnT[:, c * BANK:(c + 1) * BANK], ps[c][:, :], ACT.Copy).then_inc(s_xnT, 1)
                act.wait_ge(s_sub, 1)
                act.activation(ex[:, :, :], sub[:, :, :], ACT.Exp).then_inc(s_ex, 1)

                def emit(stage, turn, c):
                    s, k = U * turn + c, c % U
                    act.wait_ge(s_w, s + 1)
                    act.wait_ge(s_h, s + 1)
                    for f in range(FCH):
                        last = act.activation(hT[k][:, f, :], ps[2 + c % 2][:, f * P:(f + 1) * P], ACT.Gelu,
                                              bias=wfix[k][:, B1.start + f:B1.start + f + 1])
                    last.then_inc(s_gelu, 1)

                skewed(act, SLOTS, U, {"gelu": 1}, emit)

            @block.tensor
            def _(pe):
                for t in range(NT):
                    pe.wait_ge(s_xn, t + 1)
                    last = pe.transpose(ps[t // TPC][:, t % TPC * P:(t % TPC + 1) * P], xn[:, t, :], ident[:, :])
                    if t % TPC == TPC - 1:
                        last.then_inc(s_xnTp, 1)
                pe.wait_ge(s_wgn, 1)
                pe.transpose(wgT_ps, wgn[:, :], ident[0:E, 0:E]).then_inc(s_wgTp, 1)
                pe.wait_ge(s_gin, 16)
                for c in range(NC):
                    pe.wait_ge(s_xnT, c + 1)
                    if c >= 2:
                        pe.wait_ge(s_redT, c - 1)
                    pe.matmul(ps[4 + c % 2][0:GD, :], wred[:, :], xnT[:, c * BANK:(c + 1) * BANK],
                              start=True, stop=True).then_inc(s_red, 1)
                pe.wait_ge(s_wgT, 1)
                for t in range(NT):
                    pe.wait_ge(s_redT, t // TPC + 1)
                    last = pe.matmul(lg[:, t, :], redT[:, t * P:(t + 1) * P], wgnT[:, :], start=True, stop=True)
                last.then_inc(s_lg, 1)
                pe.wait_ge(s_hot, 1)
                hot = onehot[:, :, :].rearrange("p e t -> p (e t)")
                pe.matmul(rank_ps[:, 0:E * NT], keep["before"][:, :], hot, start=True, stop=True)
                pe.matmul(rank_ps[:, E * NT:2 * E * NT], keep["all"][:, :], hot, start=True, stop=True).then_inc(s_rank, 1)

                def emit(stage, turn, c):
                    s, k = U * turn + c, c % U
                    first = static_tile(turn, c) is not None and c < 2
                    if stage == "xT":
                        pe.wait_ge(s_xs[k], 16 * (turn + c // U + 1))
                        if not first:
                            pe.wait_ge(s_xsT, s - 1)
                        pe.transpose(ps[c % 2][:, 0:P], xs[k][:, :], ident[:, :]).then_inc(s_xsTp, 1)
                    elif stage == "h":
                        pe.wait_ge(s_xsT, s + 1)
                        pe.wait_ge(s_w, s + 1)
                        if not first:
                            pe.wait_ge(s_gelu, s - 1)
                        for f in range(FCH):
                            last = pe.matmul(ps[2 + c % 2][:, f * P:(f + 1) * P], wfix[k][:, f * P:(f + 1) * P], xsT[k][:, :],
                                             start=True, stop=True)
                        last.then_inc(s_h, 1)
                    else:
                        pe.wait_ge(s_gelu, s + 1)
                        if not first:
                            pe.wait_ge(s_ys, s - 1)
                        for f in range(FCH):
                            last = pe.matmul(ps[4 + c % 2][:, 0:D], hT[k][:, f, :], wfix[k][:, W2.start + f * D:W2.start + (f + 1) * D],
                                             start=f == 0, stop=f == FCH - 1)
                        last.then_inc(s_y, 1)

                skewed(pe, SLOTS, U, {"xT": 0, "h": 1, "y": 2}, emit)

        nc.clear_and_free_semaphores(sems)
        nc.all_engine_barrier()


def linear_attention(nc, shp, keep, w_qkv, b_qkv, w_out, b_out):
    D, NT = shp.D, shp.NT
    HL, DL = shp.HL, D // shp.HL
    VX = HL * (DL + 1)
    OUTER = D * (DL + 1)
    EPS = 1e-6
    U = 2
    x, ident = keep["x"], keep["ident"]

    with ExitStack() as ctx:
        def sb(name, shape, dt=F32):
            return ctx.enter_context(nc.sbuf_tensor("li_" + name, shape, dt))

        def pair(name, shape):
            return [sb(f"{name}{k}", shape) for k in range(U)]

        sems = []

        def sem(name):
            sems.append(nc.alloc_semaphore("li_" + name))
            return sems[-1]

        sums_ps = ctx.enter_context(nc.psum_tensor("li_sums", [P, 3 * BANK], F32))
        xT_ps, z_ps, qT_ps, st_ps, y_ps = (ctx.enter_context(nc.psum_tensor("li_" + n, [P, BANK], F32))
                                           for n in ("xTp", "zp", "qTp", "stp", "yp"))
        delta, inter = st_ps[:, 0:VX], st_ps[:, VX:2 * VX]
        oT_ps, out_ps = y_ps[:, 0:P], y_ps[:, P:P + D]

        stats, mv, rstd = sb("stats", [P, NT, 6]), sb("mv", [P, NT, 2]), sb("rstd", [P, NT])
        w_nat, wo_nat = sb("w_nat", [P, 3, D]), sb("wo_nat", [P, D])
        wT = sb("wT", [P, 4, P])
        b_row, bo_all = sb("b_row", [1, 3 * D]), sb("bo_all", [P, D])
        ones = sb("ones", [1, P])
        upto = sb("upto", [P, P])
        block_mask = sb("block_mask", [P, HL, DL + 1])
        xn, xT = pair("xn", [P, D]), pair("xT", [D, P])
        neg, ex = pair("neg", [P, 2 * D]), pair("ex", [P, 2 * D])
        qk, v1 = pair("qk", [P, 2 * D]), pair("v1", [P, HL, DL + 1])
        outer, prod = pair("outer", [P, HL, DL, DL + 1]), sb("prod", [P, D, DL + 1])
        qT, fresh, state = pair("qT", [D, P]), pair("fresh", [P, VX]), pair("state", [P, VX])
        own, tot = sb("own", [P, HL, DL + 1]), sb("tot", [P, HL, DL + 1])
        den, o, oT = sb("den", [P, HL]), pair("o", [P, HL, DL]), pair("oT", [P, P])

        s_in, s_bias, s_bout = sem("s_in"), sem("s_bias"), sem("s_bout")
        s_c, s_const, s_init = sem("s_c"), sem("s_const"), sem("s_init")
        s_stat, s_aggr, s_std, s_rstd = sem("s_stat"), sem("s_aggr"), sem("s_std"), sem("s_rstd")
        s_wTp, s_wT = sem("s_wTp"), sem("s_wT")
        s_xn, s_xTp, s_xT, s_z, s_neg, s_ex, s_v, s_qk = (sem(n) for n in ("s_xn", "s_xTp", "s_xT", "s_z", "s_neg", "s_ex", "s_v", "s_qk"))
        s_outer, s_sums, s_prod, s_delta, s_fresh, s_state, s_inter = (
            sem(n) for n in ("s_outer", "s_sums", "s_prod", "s_delta", "s_fresh", "s_state", "s_inter"))
        s_qTp, s_qT, s_own, s_tot, s_den, s_rden, s_o, s_oTp, s_oT, s_out, s_xb, s_x = (
            sem(n) for n in ("s_qTp", "s_qT", "s_own", "s_tot", "s_den", "s_rden", "s_o", "s_oTp", "s_oT", "s_out", "s_xb", "s_x"))
        ln_vector, ln_scalar = layernorm_steps(keep, shp, stats, mv, rstd, s_stat, s_aggr, s_std, s_rstd)

        def first(turn, c):
            return static_tile(turn, c) == 0

        with nc.Block() as block:

            @block.sync
            def _(sp):
                sp.dma_start(w_nat[:, :, :], w_qkv.rearrange("(a p) d -> p a d", p=P)).then_inc(s_in, 16)
                sp.dma_start(wo_nat[:, :], w_out).then_inc(s_in, 16)
                sp.dma_start(b_row[:, :], b_qkv.unsqueeze(0)).then_inc(s_bias, 16)
                sp.dma_start(bo_all[:, :], b_out.unsqueeze(0).to_broadcast([P, D])).then_inc(s_bout, 16)

            @block.gpsimd
            def _(pool):
                pool.memset(upto[:, :], 1.0).then_inc(s_c, 1)
                pool.memset(block_mask[:, :, :], 1.0).then_inc(s_c, 1)
                pool.memset(ones[:, :], 1.0).then_inc(s_const, 1)
                for k in range(U):
                    pool.memset(v1[k][:, :, DL:DL + 1], 1.0).then_inc(s_const, 1)
                    pool.memset(state[k][:, :], 0.0).then_inc(s_const, 1)
                pool.wait_ge(s_c, 2)
                pool.affine_select(out=upto[:, :], in_=upto[:, :], compare_op=ALU.is_ge, fill=0.0, base=0,
                                   pattern=[[1, P]], channel_multiplier=-1).then_inc(s_const, 1)
                pool.affine_select(out=block_mask[:, :, :], in_=block_mask[:, :, :], compare_op=ALU.is_ge, fill=0.0, base=0,
                                   pattern=[[-DL, HL], [0, DL + 1]], channel_multiplier=1).then_inc(s_c, 1)
                pool.wait_ge(s_c, 3)
                pool.affine_select(out=block_mask[:, :, :], in_=block_mask[:, :, :], compare_op=ALU.is_ge, fill=0.0, base=DL - 1,
                                   pattern=[[DL, HL], [0, DL + 1]], channel_multiplier=-1).then_inc(s_const, 1)
                pool.wait_ge(s_const, 2 * U + 3)
                pool.wait_ge(s_bout, 16)

                def emit(stage, turn, c):
                    t, k = U * turn + c, c % U
                    if stage == "bias":
                        pool.wait_ge(s_xn, t + 1)
                        rows = x[:, bass.ds(t, 1), :].rearrange("p a d -> p (a d)")
                        pool.tensor_tensor(rows, rows, bo_all[:, :], ALU.add).then_inc(s_xb, 1)
                    elif stage == "state":
                        pool.wait_ge(s_fresh, t + 1)
                        if not first(turn, c):
                            pool.wait_ge(s_state, t)
                        pool.tensor_tensor(state[k][:, :], state[1 - k][:, :], fresh[k][:, :], ALU.add).then_inc(s_state, 1)
                    else:
                        pool.wait_ge(s_qk, t + 1)
                        pool.wait_ge(s_v, t + 1)
                        kk = qk[k][:, D:2 * D].rearrange("p (h d) -> p h d", d=DL).unsqueeze(3).to_broadcast([P, HL, DL, DL + 1])
                        vv = v1[k][:, :, :].unsqueeze(2).to_broadcast([P, HL, DL, DL + 1])
                        pool.tensor_tensor(outer[k][:, :, :, :], kk, vv, ALU.mult).then_inc(s_outer, 1)

                skewed(pool, NT, U, {"bias": 0, "state": 2, "outer": 1}, emit)

            @block.vector
            def _(dve):
                ln_vector(dve)
                dve.wait_ge(s_const, 2 * U + 3)

                def emit(stage, turn, c):
                    t, k = U * turn + c, c % U
                    if stage == "norm":
                        rows = x[:, bass.ds(t, 1), :].rearrange("p a d -> p (a d)")
                        mean = mv[:, bass.ds(t, 1), 0:1].rearrange("p a b -> p (a b)")
                        dve.tensor_scalar(xn[k][:, :], rows, mean, rstd[:, bass.ds(t, 1)], ALU.subtract, ALU.mult).then_inc(s_xn, 1)
                    elif stage == "y":
                        dve.wait_ge(s_out, t + 1)
                        dve.wait_ge(s_xb, t + 1)
                        rows = x[:, bass.ds(t, 1), :].rearrange("p a d -> p (a d)")
                        dve.tensor_tensor(rows, out_ps, rows, ALU.add).then_inc(s_x, 1)
                    elif stage == "sums":
                        dve.wait_ge(s_delta, t + 1)
                        dve.tensor_tensor(fresh[k][:, :], delta, block_mask[:, :, :].rearrange("p h e -> p (h e)"), ALU.mult).then_inc(s_fresh, 1)
                        dve.wait_ge(s_sums, t + 1)
                        dve.tensor_tensor(prod[:, :, :], sums_ps[:, 0:OUTER].rearrange("p (c e) -> p c e", e=DL + 1),
                                          qk[k][:, 0:D].unsqueeze(2).to_broadcast([P, D, DL + 1]), ALU.mult).then_inc(s_prod, 1)
                    elif stage == "features":
                        dve.wait_ge(s_ex, t + 1)
                        dve.scalar_tensor_tensor(qk[k][:, :], z_ps[:, 0:2 * D], 0.0, ex[k][:, :], ALU.max, ALU.add).then_inc(s_qk, 1)
                    else:
                        dve.wait_ge(s_prod, t + 1)
                        dve.tensor_reduce(own[:, :, :], prod[:, :, :].rearrange("p (h d) e -> p h e d", d=DL), AX.X, ALU.add).then_inc(s_own, 1)
                        dve.wait_ge(s_inter, t + 1)
                        dve.wait_ge(s_own, t + 1)
                        dve.tensor_tensor(tot[:, :, :], inter.rearrange("p (h e) -> p h e", e=DL + 1), own[:, :, :], ALU.add).then_inc(s_tot, 1)
                        dve.wait_ge(s_tot, t + 1)
                        dve.tensor_scalar(den[:, :].unsqueeze(2), tot[:, :, DL:DL + 1], EPS, None, ALU.add).then_inc(s_den, 1)
                        dve.wait_ge(s_den, t + 1)
                        dve.reciprocal(den[:, :], den[:, :]).then_inc(s_rden, 1)
                        dve.wait_ge(s_rden, t + 1)
                        dve.tensor_tensor(o[k][:, :, :], tot[:, :, 0:DL], den[:, :].unsqueeze(2).to_broadcast([P, HL, DL]), ALU.mult).then_inc(s_o, 1)

                skewed(dve, NT, U, {"norm": 0, "y": 4, "sums": 2, "features": 1, "heads": 2}, emit)

            @block.scalar
            def _(act):
                act.wait_ge(s_const, 2 * U + 3)
                ln_scalar(act)
                act.wait_ge(s_wTp, 1)
                act.activation(wT[:, :, :].rearrange("p a f -> p (a f)"), sums_ps[:, 0:BANK], ACT.Copy).then_inc(s_wT, 1)

                def emit(stage, turn, c):
                    t, k = U * turn + c, c % U
                    if stage == "qT":
                        act.wait_ge(s_qTp, t + 1)
                        act.activation(qT[k][:, :], qT_ps[:, 0:P], ACT.Copy).then_inc(s_qT, 1)
                    elif stage == "xT":
                        act.wait_ge(s_xTp, t + 1)
                        act.activation(xT[k][:, :], xT_ps[:, 0:P], ACT.Copy).then_inc(s_xT, 1)
                    elif stage == "z":
                        act.wait_ge(s_z, t + 1)
                        act.activation(neg[k][:, :], z_ps[:, 0:2 * D], ACT.Relu, scale=-1.0).then_inc(s_neg, 1)
                        act.activation(v1[k][:, :, 0:DL], z_ps[:, 2 * D:3 * D].rearrange("p (h e) -> p h e", e=DL), ACT.Copy).then_inc(s_v, 1)
                        act.wait_ge(s_neg, t + 1)
                        act.activation(ex[k][:, :], neg[k][:, :], ACT.Exp, scale=-1.0).then_inc(s_ex, 1)
                    else:
                        act.wait_ge(s_oTp, t + 1)
                        act.activation(oT[k][:, :], oT_ps, ACT.Copy).then_inc(s_oT, 1)

                skewed(act, NT, U, {"qT": 2, "xT": 0, "z": 1, "oT": 3}, emit)

            @block.tensor
            def _(pe):
                pe.wait_ge(s_in, 32)
                for a in range(3):
                    pe.transpose(sums_ps[:, a * P:(a + 1) * P], w_nat[:, a, :], ident[:, :])
                pe.transpose(sums_ps[:, 3 * P:4 * P], wo_nat[:, :], ident[:, :]).then_inc(s_wTp, 1)
                pe.wait_ge(s_const, 2 * U + 3)
                pe.wait_ge(s_bias, 16)
                pe.wait_ge(s_wT, 1)

                def emit(stage, turn, c):
                    t, k = U * turn + c, c % U
                    if stage == "y":
                        pe.wait_ge(s_oT, t + 1)
                        pe.matmul(out_ps, oT[k][:, :], wT[:, 3, :], start=True, stop=True).then_inc(s_out, 1)
                    elif stage == "sums":
                        pe.wait_ge(s_qk, t + 1)
                        if not first(turn, c):
                            pe.wait_ge(s_qT, t)
                        pe.transpose(qT_ps[:, 0:P], qk[k][:, 0:D], ident[:, :]).then_inc(s_qTp, 1)
                        pe.wait_ge(s_v, t + 1)
                        if not first(turn, c):
                            pe.wait_ge(s_tot, t)
                        pe.matmul(delta, qk[k][:, D:2 * D], v1[k][:, :, :].rearrange("p h e -> p (h e)"),
                                  start=True, stop=True).then_inc(s_delta, 1)
                        pe.wait_ge(s_outer, t + 1)
                        if not first(turn, c):
                            pe.wait_ge(s_prod, t)
                        flat = outer[k][:, :, :, :].rearrange("p h d e -> p (h d e)")
                        for a in range(0, OUTER, BANK):
                            b = min(a + BANK, OUTER)
                            last = pe.matmul(sums_ps[:, a:b], upto[:, :], flat[:, a:b], start=True, stop=True)
                        last.then_inc(s_sums, 1)
                        pe.wait_ge(s_qT, t + 1)
                        pe.wait_ge(s_fresh, t + 1)
                        if not first(turn, c):
                            pe.wait_ge(s_state, t)
                        pe.matmul(inter, qT[k][:, :], state[1 - k][:, :], start=True, stop=True).then_inc(s_inter, 1)
                    elif stage == "xT":
                        pe.wait_ge(s_xn, t + 1)
                        if not first(turn, c):
                            pe.wait_ge(s_xT, t)
                        pe.transpose(xT_ps[:, 0:P], xn[k][:, :], ident[:, :]).then_inc(s_xTp, 1)
                    elif stage == "z":
                        pe.wait_ge(s_xT, t + 1)
                        if not first(turn, c):
                            pe.wait_ge(s_qk, t)
                            pe.wait_ge(s_v, t)
                        pe.matmul(z_ps[:, 0:3 * D], xT[k][:, :], wT[:, 0:3, :].rearrange("p a f -> p (a f)"), start=True, stop=False)
                        pe.matmul(z_ps[:, 0:3 * D], ones[:, :], b_row[:, :], start=False, stop=True).then_inc(s_z, 1)
                    else:
                        pe.wait_ge(s_o, t + 1)
                        if not first(turn, c):
                            pe.wait_ge(s_x, t)
                        pe.transpose(oT_ps, o[k][:, :, :].rearrange("p h e -> p (h e)"), ident[:, :]).then_inc(s_oTp, 1)

                skewed(pe, NT, U, {"y": 4, "sums": 2, "xT": 0, "z": 1, "oT": 3}, emit)

        nc.clear_and_free_semaphores(sems)
        nc.all_engine_barrier()


def prepare(nc, shp, keep, f_w1, f_b1, f_w2, f_b2, scratch_in):
    E, FCH, D, NT, SLOTS = shp.E, shp.FCH, shp.D, shp.NT, shp.SLOTS
    W1, W2, B1, B2 = keep["wall_cols"]
    wall = keep["wall"]
    s_z, s_c = keep["s_z"], keep["s_c"]
    with nc.Block() as block:

        @block.vector
        def _(dve):
            dve.memset(keep["eps"][:, :], LN_EPS)
            dve.memset(keep["zeros"][:, :], 0.0).then_inc(s_z, 1)
            dve.memset(keep["ones8"][:, :], 1.0)
            dve.memset(keep["all"][:, :], 1.0)
            dve.wait_ge(s_c, 1)
            dve.tensor_scalar(keep["restart"][:, :, :], keep["restart"][:, :, :], 1.0, None, ALU.min)

        @block.gpsimd
        def _(pool):
            pool.iota(keep["restart"][:, :, :], pattern=[[0, E], [1, NT]], base=0, channel_multiplier=0,
                      allow_small_or_imprecise_dtypes=True).then_inc(s_c, 1)
            pool.iota(keep["full"][:, :, :], pattern=[[0, E], [P, NT]], base=0, channel_multiplier=0,
                      allow_small_or_imprecise_dtypes=True)
            pool.iota(keep["prio"][:, :, :], pattern=[[0, NT], [-1, E]], base=E, channel_multiplier=0,
                      allow_small_or_imprecise_dtypes=True)
            pool.iota(keep["slots"][:, :, :], pattern=[[1, SLOTS], [0, E]], base=0, channel_multiplier=0,
                      allow_small_or_imprecise_dtypes=True)
            pool.memset(keep["before"][:, :], 1.0).then_inc(s_c, 1)
            pool.wait_ge(s_c, 2)
            pool.affine_select(out=keep["before"][:, :], in_=keep["before"][:, :], compare_op=ALU.is_gt, fill=0.0, base=0,
                               pattern=[[1, P]], channel_multiplier=-1)

        @block.sync
        def _(sp):
            sp.wait_ge(s_z, 1)
            sp.dma_start(scratch_in.rearrange("(s p) d -> p s d", p=P),
                         keep["zeros"][:, :].unsqueeze(1).to_broadcast([P, SLOTS, D])).then_inc(keep["s_scratch"], 16)
            sp.dma_start(wall[:, :, W1], f_w1.rearrange("e d f -> d e f")).then_inc(keep["s_wall"], 16)
            for f in range(FCH):
                sp.dma_start(wall[:, :, W2.start + f * D:W2.start + (f + 1) * D],
                             f_w2[:, f * P:(f + 1) * P, :].rearrange("e p d -> p e d")).then_inc(keep["s_wall"], 16)
                sp.dma_start(wall[:, :, B1.start + f:B1.start + f + 1],
                             f_b1[:, f * P:(f + 1) * P].rearrange("e (p a) -> p e a", a=1), allow_slow_non_contiguous=True).then_inc(keep["s_wall"], 16)
            sp.dma_start(wall[:, :, B2], f_b2.unsqueeze(0).to_broadcast([P, E, D])).then_inc(keep["s_wall"], 16)
            sp.wait_ge(keep["s_scratch"], 16)
            sp.wait_ge(keep["s_wall"], 16 * (2 * FCH + 2))


def bass_hybrid_layers(nc, a_x, w_k, w_q, w_v, w_o, b_wqkv, b_bqkv, b_wout, b_bout,
                       f_wred, f_wg, f_w1, f_b1, f_w2, f_b2, out):
    shp = Shapes(a_x, w_k, f_wg, f_w1)
    NT, D, E = shp.NT, shp.D, shp.E
    hid = shp.FCH * P
    scratch_in = nc.dram_tensor("slots_in", (shp.SLOTS * P, D), F32).ap()
    scratch_out = nc.dram_tensor("slots_out", (shp.SLOTS * P, D), F32).ap()
    with ExitStack() as ctx:
        def sb(name, shape, dt=F32):
            return ctx.enter_context(nc.sbuf_tensor(name, shape, dt))

        keep = {
            "x": sb("x", [P, NT, D]), "ident": sb("ident", [P, P]), "eps": sb("eps", [P, 1]), "zeros": sb("zeros", [P, D]),
            "wall": sb("wall", [P, E, 2 * hid + shp.FCH + D]),
            "wall_cols": (slice(0, hid), slice(hid, 2 * hid), slice(2 * hid, 2 * hid + shp.FCH),
                          slice(2 * hid + shp.FCH, 2 * hid + shp.FCH + D)),
            "restart": sb("restart", [P, E, NT]), "full": sb("full", [P, E, NT]), "prio": sb("prio", [P, NT, E]),
            "slots": sb("slots", [1, shp.SLOTS, E]), "ones8": sb("ones8", [P, E]),
            "before": sb("before", [P, P], BF16), "all": sb("all", [P, P], BF16),
        }
        for n in ("s_z", "s_c", "s_scratch", "s_wall"):
            keep[n] = ctx.enter_context(nc.semaphore(n))
        s_out = ctx.enter_context(nc.semaphore("s_out"))
        prepare(nc, shp, keep, f_w1, f_b1, f_w2, f_b2, scratch_in)
        attention(nc, shp, keep, a_x, w_k, w_q, w_v, w_o)
        ffn(nc, shp, keep, "f0_", f_wred, f_wg, scratch_in, scratch_out)
        linear_attention(nc, shp, keep, b_wqkv, b_bqkv, b_wout, b_bout)
        ffn(nc, shp, keep, "f1_", f_wred, f_wg, scratch_in, scratch_out)

        with nc.Block() as block:
            @block.sync
            def _(sp):
                sp.dma_start(out[0].rearrange("(t p) d -> p t d", p=P), keep["x"][:, :, :]).then_inc(s_out, 16)
                sp.wait_ge(s_out, 16)


_INS = ['L0_attn_a_x', 'L0_attn_a_W_K', 'L0_attn_a_W_Q', 'L0_attn_a_W_V', 'L0_attn_a_W_O',
        'L0_attn_b_w_qkv', 'L0_attn_b_b_qkv', 'L0_attn_b_w_out', 'L0_attn_b_b_out',
        'L0_ffn_w_red', 'L0_ffn_wg', 'L0_ffn_w1', 'L0_ffn_b1', 'L0_ffn_w2', 'L0_ffn_b2']
_OUTS = [((1, 2048, 128), 'float32')]


def kernel(**inputs):
    import numpy as _np
    import concourse.bacc as _bacc
    from concourse import mybir as _mybir
    from concourse.bass_utils import run_bass_kernel_spmd as _run

    nc = _bacc.Bacc("TRN2", target_bir_lowering=False, num_devices=1)
    arrays, args = {}, []
    for name in _INS:
        a = _np.ascontiguousarray(inputs[name])
        arrays[f"in_{name}_dram"] = a
        args.append(nc.dram_tensor(f"in_{name}_dram", a.shape, _mybir.dt.from_np(a.dtype), kind="ExternalInput").ap())
    for i, (shape, dtype) in enumerate(_OUTS):
        dt = _mybir.dt.from_np(_np.dtype(dtype))
        args.append(nc.dram_tensor(f"out_{i}_dram", shape, dt, kind="ExternalOutput").ap())
    bass_hybrid_layers(nc, *args)
    r = _run(nc, [arrays], core_ids=[0])
    got = tuple(r.results[0][f"out_{i}_dram"] for i in range(len(_OUTS)))
    return got[0]
```

```python
from contextlib import ExitStack

import concourse.bass as bass
from concourse import mybir

F32 = mybir.dt.float32
F32R = mybir.dt.float32r
BF16 = mybir.dt.bfloat16
I32 = mybir.dt.int32
U32 = mybir.dt.uint32
ALU = mybir.AluOpType
ACT = mybir.ActivationFunctionType
AX = mybir.AxisListType

P = 128
BANK = 512
MASKED = -1e30
LN_EPS = 1e-5


class Shapes:

    def __init__(self, x, w_k, w_g, w_1):
        self.T, self.D = x.shape[1], x.shape[2]
        self.H, self.DH = w_k.shape[0], w_k.shape[1]
        self.NT = self.T // P
        self.NC = self.T // BANK
        self.TPC = BANK // P
        self.PAIRS = self.H * self.DH // P
        self.HL = 16
        self.E, self.GD = w_g.shape
        self.FCH = w_1.shape[2] // P
        self.SLOTS = -(-(self.NT + self.E - 1) // 4) * 4


def make_identity(pool, tile, done, ready):
    pool.memset(tile, 0.0).then_inc(done, 1)
    pool.wait_ge(done, 1)
    pool.affine_select(out=tile, in_=tile, compare_op=ALU.not_equal, fill=1.0, base=0,
                       pattern=[[-1, P]], channel_multiplier=1).then_inc(ready, 1)


def attention(nc, shp, keep, x_in, w_k, w_q, w_v, w_o, fetch):
    T, D, DH, NT, NC, TPC, PAIRS = shp.T, shp.D, shp.DH, shp.NT, shp.NC, shp.TPC, shp.PAIRS
    x, ident = keep["x"], keep["ident"]
    SCALE = float(DH) ** -0.5
    RING = 5
    STEPS = NT // 2
    UNITS = 4 * STEPS
    SLOTS = 8

    def row(u):
        return u // 4 * 2 + u % 4 // 2

    def chunks(u):
        return row(u) // TPC + 1

    def width(u, c):
        return min(BANK, (row(u) + 1) * P - c * BANK)

    first_chunk = [sum(chunks(b) for b in range(u)) for u in range(UNITS + 1)]
    N_SC = first_chunk[UNITS]
    first_group = [j * (j + 1) // 2 for j in range(STEPS + 1)]
    N_GR = first_group[STEPS]
    N_PJ = 2 * NC
    N_V = NC
    V_FIRST = N_SC + N_PJ
    V_BANKS = [RING - 2, RING - 1] * (N_V // 2)
    BANKS = [use % RING for use in range(V_FIRST)] + V_BANKS

    def back_of(j):
        items = []
        for g in range(j + 1):
            items += [("turn", j, 0, g), ("turn", j, 1, g)]
            if g:
                items += [("value", j, g - 1, 0), ("value", j, g - 1, 1)]
        return items + [("value", j, j, 0), ("value", j, j, 1), ("leave", j)]

    def spread(items, weights):
        ends = [round(len(items) * sum(weights[:i]) / sum(weights)) for i in range(len(weights) + 1)]
        return [items[a:b] for a, b in zip(ends, ends[1:])]

    def slot_weights(n, opens):
        w = [1] * n
        return [0] * ((n + 1) // 2) + w[(n + 1) // 2:] if opens and n > 1 else w

    def exp_slot(c, ne):
        return max(c - 1, 0)

    LATE = 4

    def issue_order(projections):
        order, rest = [], []
        for w in range(UNITS + 1):
            ns = chunks(w) if w < UNITS else 0
            ne = chunks(w - 1) if w else 0
            opens = w % 4 == 1 and w > 4
            fill = []
            if opens:
                j = w // 4 - 1
                lens = [max(chunks(u) if u < UNITS else 0, chunks(u - 1)) for u in range(w, w + 4)]
                items = back_of(j)
                fill = [rest[:2], rest[2:3], rest[3:4], rest[4:]] if len(rest) > 2 else [rest]
                if j < STEPS - 2 and chunks(4 * (j + 2)) == NC:
                    items, rest = items[:-LATE], items[-LATE:]
                else:
                    rest = []
                rest = rest + [("out", j), ("add", j)]
                dealt = spread(items, [v for i, n in enumerate(lens) for v in slot_weights(n, i == 0)])
            for k in range(max(ns, ne)):
                if k < ns:
                    order.append(("score", w, k))
                if opens and k == 0:
                    order.append(("sums", j))
                order += fill.pop(0) if fill else []
                order += dealt.pop(0) if w > 4 else []
                order += [("exp", w - 1, c) for c in range(ne) if exp_slot(c, ne) == k]
        j = STEPS - 1
        if not projections:
            return order + [("sums", j), ("out", j - 1), ("add", j - 1)] + back_of(j) + [("out", j), ("add", j)]
        order += [("project", 0), ("sums", j), ("project", 1), ("out", j - 1), ("add", j - 1), ("low", 0)]
        for i, items in enumerate(spread(back_of(j), [1] * (N_PJ - 2))):
            order += [("project", i + 2)] + items + [("low", i + 1)]
        values = [("vproject", m) for m in range(N_V)]
        return order + values[:1] + [("low", N_PJ - 1)] + values[1:2] + [("out", j), ("add", j)] + values[2:]

    order, last_order = issue_order(True), issue_order(False)
    opening = [(step, i) for i in range(N_PJ) for step in ("project", "low")] + [("vproject", m) for m in range(N_V)]

    with ExitStack() as ctx:
        def sb(name, shape, dt=F32):
            return ctx.enter_context(nc.sbuf_tensor("at_" + name, shape, dt))

        sems = []

        def sem(name):
            sems.append(nc.alloc_semaphore("at_" + name))
            return sems[-1]

        ps = [ctx.enter_context(nc.psum_tensor(f"at_ps{i}", [P, BANK], F32)) for i in range(8)]
        ring = ps[:RING]
        turn_ps = ps[RING:RING + 2]
        z_ps = ps[RING + 2][:, 0:2 * P]
        o_ps = [ps[RING + 2][:, 2 * D:4 * D], ps[RING + 2][:, 0:2 * D]]

        stats = sb("stats", [P, NT, 6])
        mv = sb("mv", [P, NT, 2])
        rstd = sb("rstd", [P, NT])
        xnT = sb("xnT", [D, T])
        wT = {n: sb("wT_" + n, [P, PAIRS, P]) for n in "qkv"}
        wo_bd = sb("wo_bd", [P, PAIRS, 2, D])
        wq_fix, wk_fix = sb("wq_fix", [D, P]), sb("wk_fix", [D, P])
        k_st = [sb(f"k_st{h}", [P, T], F32R) for h in range(2)]
        q_parts = [sb(f"q_parts{h}", [P, 2, T], F32R) for h in range(2)]
        q_hi, q_lo = ([q[:, i, :] for q in q_parts] for i in range(2))
        v = sb("v", [P, NT, P])
        prob = [[sb(f"prob{k}{i}", [P, T - P * (i < 2)]) for i in range(4)] for k in range(2)]
        wnat = {n: prob[0][i][:, 0:PAIRS * P].rearrange("p (a f) -> p a f", f=P) for i, n in enumerate("qkv")}
        wnat_o = prob[0][3][:, 0:PAIRS * P]
        xn = prob[1][2][:, 0:NT * D].rearrange("p (t d) -> p t d", d=D)
        probT = [[sb(f"probT{h}{k}", [P, BANK]) for k in range(2)] for h in range(2)]
        zT = [sb(f"zT{k}", [P, 2 * P]) for k in range(2)]
        cmax = sb("cmax", [P, SLOTS, NC])
        nmax = sb("nmax", [P, SLOTS])
        esum = sb("esum", [P, 2, 4, NC])
        rsum, rinv = sb("rsum", [P, 2, 4]), sb("rinv", [P, 2, 4])
        identb = sb("identb", [P, P], BF16)
        maskb = sb("maskb", [P, P], BF16)

        s_xin, s_win = sem("s_xin"), [sem(f"s_win{i}") for i in range(4)]
        s_c0, s_c1, s_c2, s_const = sem("s_c0"), sem("s_c1"), sem("s_c2"), sem("s_const")
        s_stat, s_aggr, s_std, s_rstd, s_xn = (sem(n) for n in ("s_stat", "s_aggr", "s_std", "s_rstd", "s_xn"))
        s_setT, s_setcp = sem("s_setT"), sem("s_setcp")
        s_wfix = sem("s_wfix")
        s_dup = [sem(f"s_dup{c}") for c in range(NC)]
        s_proj, s_hi, s_lo = sem("s_proj"), sem("s_hi"), sem("s_lo")
        s_vproj, s_v = sem("s_vproj"), sem("s_v")
        s_score, s_cmax, s_nmax, s_exp = sem("s_score"), sem("s_cmax"), sem("s_nmax"), sem("s_exp")
        s_turn = [sem(f"s_turn{h}") for h in range(2)]
        s_probT = [sem(f"s_probT{h}") for h in range(2)]
        s_z, s_zT, s_o = sem("s_z"), sem("s_zT"), sem("s_o")
        s_rsum, s_rinv, s_acc1, s_acc2 = sem("s_rsum"), sem("s_rinv"), sem("s_acc1"), sem("s_acc2")

        N_SET = 4 * PAIRS // TPC + NC
        FIRST_MANY = next(u for u in range(UNITS) if chunks(u) > 1)
        N_CMAX = N_SC - first_chunk[FIRST_MANY]
        FIRST_SUMS = FIRST_MANY // 4
        N_RSUM = STEPS - FIRST_SUMS

        with nc.Block() as block:

            @block.sync
            def _(sp):
                sp.dma_start(x[:, :, :], x_in[0].rearrange("(t p) d -> p t d", p=P)).then_inc(s_xin, 16)
                for i, (n, w) in enumerate((("q", w_q), ("k", w_k), ("v", w_v))):
                    sp.dma_start(wnat[n], w.rearrange("h f d -> (h f) d").rearrange("(a p) d -> p a d", p=P)).then_inc(s_win[i], 16)
                sp.dma_start(wnat_o, w_o).then_inc(s_win[3], 16)

                def second_copies(made):
                    for c in range(NC):
                        cols = slice(c * BANK, (c + 1) * BANK)
                        sp.wait_ge(s_lo, N_PJ * made + NC + c + 1)
                        for h in range(2):
                            here, there = slice(DH * h, DH * (h + 1)), slice(DH * (1 - h), DH * (2 - h))
                            sp.dma_start(q_parts[h][there, :, cols].bitcast(F32), q_parts[h][here, :, cols].bitcast(F32)).then_inc(s_dup[c], 16)

                second_copies(0)
                fetch(sp)
                with sp.Fori(0, PAIRS - 1) as pair:
                    second_copies(pair + 1)

            @block.gpsimd
            def _(pool):
                pool.sem_inc(s_probT[0], 1)
                pool.sem_inc(s_probT[1], 1)
                pool.sem_inc(s_acc2, 1)
                make_identity(pool, ident[:, :], s_c0, s_const)
                make_identity(pool, identb[:, :], s_c1, s_const)
                pool.memset(maskb[:, :], 0.0).then_inc(s_c2, 1)
                pool.wait_ge(s_c2, 1)
                pool.affine_select(out=maskb[:, :], in_=maskb[:, :], compare_op=ALU.is_ge, fill=MASKED, base=0,
                                   pattern=[[-1, P]], channel_multiplier=1).then_inc(s_const, 1)
                pool.memset(wo_bd[:, :, :, :], 0.0).then_inc(s_const, 1)
                pool.wait_ge(s_setcp, N_SET - NC)

                def projection_weights(pair):
                    for fix, n in ((wk_fix, "k"), (wq_fix, "q")):
                        last = pool.tensor_copy(fix[:, :], wT[n][:, bass.ds(pair, 1), :].rearrange("d a f -> d (a f)"))
                    last.then_inc(s_wfix, 1)

                projection_weights(0)
                with pool.Fori(0, PAIRS - 1) as pair:
                    pool.wait_ge(s_proj, N_PJ * (pair + 1))
                    projection_weights(pair + 1)

            @block.vector
            def _(dve):
                dve.wait_ge(s_xin, 16)
                for t in range(NT):
                    dve.bn_stats(stats[:, t, :], x[:, t, :]).then_inc(s_stat, 1)
                for t in range(NT):
                    dve.wait_ge(s_stat, t + 1)
                    dve.bn_aggr(mv[:, t, :], stats[:, t, :]).then_inc(s_aggr, 1)
                dve.wait_ge(s_std, 1)
                dve.reciprocal(rstd[:, :], rstd[:, :]).then_inc(s_rstd, 1)
                dve.wait_ge(s_rstd, 1)
                for t in range(NT):
                    dve.tensor_scalar(xn[:, t, :], x[:, t, :], mv[:, t, 0:1], rstd[:, t:t + 1],
                                      ALU.subtract, ALU.mult).then_inc(s_xn, 1)

                def run(items, pair, made):
                    for it in items:
                        if it[0] == "score":
                            _, u, c = it
                            k = first_chunk[u] + c
                            bank = ring[k % RING][:, 0:width(u, c)]
                            dve.wait_ge(s_score, N_SC * pair + k + 1)
                            if chunks(u) == 1:
                                dve.tensor_reduce(nmax[:, u % SLOTS:u % SLOTS + 1], bank, AX.X, ALU.max, negate=True).then_inc(s_nmax, 1)
                                continue
                            dve.tensor_reduce(cmax[:, u % SLOTS, c:c + 1], bank, AX.X, ALU.max).then_inc(s_cmax, 1)
                            if c == chunks(u) - 1:
                                dve.wait_ge(s_cmax, N_CMAX * pair + k + 1 - first_chunk[FIRST_MANY])
                                dve.tensor_reduce(nmax[:, u % SLOTS:u % SLOTS + 1], cmax[:, u % SLOTS, 0:c + 1], AX.X, ALU.max,
                                                  negate=True).then_inc(s_nmax, 1)
                        elif it[0] == "turn" and it[2] == 1:
                            _, j, h, g = it
                            n, w = first_group[j] + g, (4 if g < j else 3) * P
                            dve.wait_ge(s_turn[1], N_GR * pair + n + 1)
                            dve.tensor_copy(probT[1][n % 2][:, 0:w], turn_ps[1][:, 0:w]).then_inc(s_probT[1], 1)
                        elif it[0] == "sums":
                            j = it[1]
                            n, k = chunks(4 * j), j % 2
                            dve.wait_ge(s_exp, N_SC * pair + first_chunk[4 * j + 4])
                            if n == 1:
                                dve.reciprocal(rinv[:, k, :].unsqueeze(2), esum[:, k, :, 0:1]).then_inc(s_rinv, 1)
                                continue
                            dve.tensor_reduce(rsum[:, k, :], esum[:, k, :, 0:n], AX.X, ALU.add).then_inc(s_rsum, 1)
                            dve.wait_ge(s_rsum, N_RSUM * pair + j + 1 - FIRST_SUMS)
                            dve.reciprocal(rinv[:, k, :], rsum[:, k, :]).then_inc(s_rinv, 1)
                        elif it[0] == "add":
                            j = it[1]
                            dve.wait_ge(s_rinv, STEPS * pair + j + 1)
                            dve.wait_ge(s_o, STEPS * pair + j + 1)
                            for h, done in enumerate((s_acc1, s_acc2)):
                                if h:
                                    dve.wait_ge(s_acc1, STEPS * pair + j + 1)
                                for i in range(2):
                                    last = dve.scalar_tensor_tensor(x[:, 2 * j + i, :], o_ps[i][:, h * D:(h + 1) * D],
                                                                    rinv[:, j % 2, 2 * i + h:2 * i + h + 1], x[:, 2 * j + i, :],
                                                                    ALU.mult, ALU.add)
                                last.then_inc(done, 1)
                        elif it[0] == "low":
                            kind, c = divmod(it[1], NC)
                            cols = slice(c * BANK, (c + 1) * BANK)
                            bank = ring[(N_SC + it[1]) % RING]
                            dve.wait_ge(s_hi, N_PJ * made + it[1] + 1)
                            for h in range(2):
                                here, there = slice(DH * h, DH * (h + 1)), slice(DH * (1 - h), DH * (2 - h))
                                if kind == 0:
                                    last = dve.tensor_tensor(k_st[h][there, cols], bank[here, :],
                                                             k_st[h][here, cols].bitcast(F32), ALU.subtract)
                                    continue
                                last = dve.scalar_tensor_tensor(q_lo[h][here, cols], bank[here, :], SCALE,
                                                                q_hi[h][here, cols].bitcast(F32), ALU.mult, ALU.subtract)
                            last.then_inc(s_lo, 1)

                run(opening, 0, 0)
                with dve.Fori(0, PAIRS - 1) as pair:
                    run(order, pair, pair + 1)
                run(last_order, PAIRS - 1, PAIRS)

            @block.scalar
            def _(act):
                act.wait_ge(s_aggr, NT)
                act.activation(rstd[:, :], mv[:, :, 1], ACT.Sqrt, bias=keep["eps"][:, 0:1]).then_inc(s_std, 1)
                W_GROUPS = PAIRS // TPC
                dst = [wT[n][:, TPC * i:TPC * (i + 1), :] for n in "qkv" for i in range(W_GROUPS)]
                dst = [d.rearrange("p a f -> p (a f)") for d in dst]
                act.wait_ge(s_const, 4)
                for i in range(N_SET):
                    act.wait_ge(s_setT, i + 1)
                    if i < 3 * W_GROUPS:
                        last = act.activation(dst[i], ps[i % 8][:, :], ACT.Copy)
                    elif i < 4 * W_GROUPS:
                        pairs = slice(TPC * (i - 3 * W_GROUPS), TPC * (i - 3 * W_GROUPS + 1))
                        for h in range(2):
                            rows = slice(DH * h, DH * (h + 1))
                            last = act.activation(wo_bd[rows, pairs, h, :],
                                                  ps[i % 8][rows, :].rearrange("p (a d) -> p a d", d=D), ACT.Copy)
                    else:
                        c = i - 4 * W_GROUPS
                        last = act.activation(xnT[:, c * BANK:(c + 1) * BANK], ps[i % 8][:, :], ACT.Copy)
                    last.then_inc(s_setcp, 1)

                def run(items, pair, made):
                    for it in items:
                        if it[0] == "exp":
                            _, u, c = it
                            j, h, k, w = u // 4, u % 2, first_chunk[u] + c, width(u, c)
                            if c == 0:
                                act.wait_ge(s_nmax, UNITS * pair + u + 1)
                                if j >= 2 and u % 4 < 2:
                                    act.wait_ge(s_turn[h], N_GR * pair + first_group[j - 1])
                            act.activation(prob[j % 2][u % 4][:, c * BANK:c * BANK + w], ring[k % RING][:, 0:w], ACT.Exp,
                                           bias=nmax[:, u % SLOTS:u % SLOTS + 1],
                                           accum_out=esum[:, j % 2, u % 4, c:c + 1]).then_inc(s_exp, 1)
                        elif it[0] == "turn" and it[2] == 0:
                            _, j, h, g = it
                            n, w = first_group[j] + g, (4 if g < j else 3) * P
                            act.wait_ge(s_turn[0], N_GR * pair + n + 1)
                            act.activation(probT[0][n % 2][:, 0:w], turn_ps[0][:, 0:w], ACT.Copy).then_inc(s_probT[0], 1)
                        elif it[0] == "leave":
                            j = it[1]
                            act.wait_ge(s_z, STEPS * pair + j + 1)
                            act.activation(zT[j % 2][:, :], z_ps, ACT.Copy).then_inc(s_zT, 1)
                        elif it[0] == "project":
                            kind, c = divmod(it[1], NC)
                            cols = slice(c * BANK, (c + 1) * BANK)
                            bank = ring[(N_SC + it[1]) % RING]
                            act.wait_ge(s_proj, N_PJ * made + it[1] + 1)
                            for h in range(2):
                                here, there = slice(DH * h, DH * (h + 1)), slice(DH * (1 - h), DH * (2 - h))
                                if kind == 0:
                                    last = act.activation(k_st[h][here, cols], bank[here, :], ACT.Copy)
                                    continue
                                last = act.activation(q_hi[h][here, cols], bank[here, :], ACT.Copy, scale=SCALE)
                            last.then_inc(s_hi, 1)
                        elif it[0] == "vproject":
                            m = it[1]
                            act.wait_ge(s_vproj, N_V * made + m + 1)
                            act.activation(v[:, TPC * m:TPC * (m + 1), :].rearrange("p t f -> p (t f)"),
                                           ring[BANKS[V_FIRST + m]][:, :], ACT.Copy).then_inc(s_v, 1)

                act.activation(zT[0][:, 0:1], keep["eps"][:, 0:1], ACT.Exp)
                run(opening, 0, 0)
                with act.Fori(0, PAIRS - 1) as pair:
                    run(order, pair, pair + 1)
                run(last_order, PAIRS - 1, PAIRS)

            @block.tensor
            def _(pe):
                pe.wait_ge(s_const, 3)
                src = []
                for i, n in enumerate("qkv"):
                    src += [(s_win[i], 16, wnat[n][:, a, :]) for a in range(PAIRS)]
                src += [(s_win[3], 16, wnat_o[:, a * P:(a + 1) * P]) for a in range(PAIRS)]
                src += [(s_xn, t + 1, xn[:, t, :]) for t in range(NT)]
                for i, (ready, count, tile) in enumerate(src):
                    grp, k = divmod(i, TPC)
                    if k == 0 and grp >= 8:
                        pe.wait_ge(s_setcp, grp - 7)
                    pe.wait_ge(ready, count)
                    last = pe.transpose(ps[grp % 8][:, k * P:(k + 1) * P], tile, ident[:, :])
                    if k == TPC - 1:
                        last.then_inc(s_setT, 1)
                pe.wait_ge(s_setcp, N_SET)

                def free_bank(use, pair, made):
                    same = [u for u in range(len(BANKS)) if BANKS[u] == BANKS[use]]
                    before = max([u for u in same if u < use], default=None)
                    if before is None:
                        before, made = max(same), made - 1
                    if before >= V_FIRST:
                        pe.wait_ge(s_v, N_V * made + before - V_FIRST + 1)
                    elif before >= N_SC:
                        pe.wait_ge(s_lo, N_PJ * made + before - N_SC + 1)
                    else:
                        pe.wait_ge(s_exp, N_SC * pair + before + 1)

                def run(items, pair, made, first):
                    for it in items:
                        if it[0] == "score":
                            _, u, c = it
                            r, h = row(u), u % 2
                            if r % TPC == 0 and u % 4 == 0:
                                pe.wait_ge(s_lo, N_PJ * (made - 1) + r // TPC + 1)
                                pe.wait_ge(s_dup[r // TPC], 32 * made)
                            k, w = first_chunk[u] + c, width(u, c)
                            free_bank(k, pair, made)
                            bank = ring[k % RING]
                            keys = k_st[h][:, c * BANK:c * BANK + w]
                            pe.matmul(bank[:, 0:w], q_hi[h][:, r * P:(r + 1) * P], keys, start=True, stop=False)
                            if c == chunks(u) - 1:
                                pe.matmul(bank[:, w - P:w], identb[:, :], maskb[:, :], start=False, stop=False)
                            last = pe.matmul(bank[:, 0:w], q_lo[h][:, r * P:(r + 1) * P], keys, start=False, stop=True)
                            last.then_inc(s_score, 1)
                        elif it[0] == "turn":
                            _, j, h, g = it
                            n = first_group[j] + g
                            if g == 0:
                                pe.wait_ge(s_exp, N_SC * pair + first_chunk[4 * j + 3 + h])
                            pe.wait_ge(s_probT[h], N_GR * pair + n + 1)
                            tiles = [(t, i) for t in (2 * g, 2 * g + 1) for i in range(2) if t <= 2 * j + i]
                            for b, (t, i) in enumerate(tiles):
                                last = pe.transpose(turn_ps[h][:, b * P:(b + 1) * P],
                                                    prob[j % 2][2 * i + h][:, t * P:(t + 1) * P], ident[:, :])
                            last.then_inc(s_turn[h], 1)
                        elif it[0] == "value":
                            _, j, g, b = it
                            n, t = first_group[j] + g, 2 * g + b
                            if b == 0:
                                if j == 0:
                                    pe.wait_ge(s_v, N_V * made)
                                if g == 0:
                                    pe.wait_ge(s_acc2, STEPS * pair + j + 1)
                                for h in range(2):
                                    pe.wait_ge(s_probT[h], N_GR * pair + n + 2)
                            last_tile = t == 2 * j + 1
                            to, w = (P, P) if last_tile else (0, 2 * P)
                            for h in range(2):
                                rows = slice(DH * h, DH * (h + 1))
                                last = pe.matmul(z_ps[rows, to:to + w], v[:, t, rows], probT[h][n % 2][:, 2 * P * b:2 * P * b + w],
                                                 start=t == 0, stop=last_tile)
                            if last_tile:
                                last.then_inc(s_z, 1)
                        elif it[0] == "out":
                            j = it[1]
                            pe.wait_ge(s_zT, STEPS * pair + j + 1)
                            for i in range(2):
                                last = pe.matmul(o_ps[i], zT[j % 2][:, i * P:(i + 1) * P],
                                                 wo_bd[:, bass.ds(pair, 1), :, :].rearrange("f a h d -> f (a h d)"),
                                                 start=True, stop=True)
                            last.then_inc(s_o, 1)
                        elif it[0] == "project":
                            i = it[1]
                            kind, c = divmod(i, NC)
                            if i == 0:
                                pe.wait_ge(s_wfix, made + 1)
                            if not first or i >= RING:
                                free_bank(N_SC + i, pair, made)
                            pe.matmul(ring[(N_SC + i) % RING][:, :], (wk_fix, wq_fix)[kind][:, :], xnT[:, c * BANK:(c + 1) * BANK],
                                      start=True, stop=True).then_inc(s_proj, 1)
                        elif it[0] == "vproject":
                            m = it[1]
                            free_bank(V_FIRST + m, pair, made)
                            bank = ring[BANKS[V_FIRST + m]]
                            wv = wT["v"][:, bass.ds(made, 1), :].rearrange("d a f -> d (a f)")
                            for b in range(TPC):
                                t = m * TPC + b
                                last = pe.matmul(bank[:, b * P:(b + 1) * P], xnT[:, t * P:(t + 1) * P], wv, start=True, stop=True)
                            last.then_inc(s_vproj, 1)

                run(opening, 0, 0, True)
                with pe.Fori(0, PAIRS - 1) as pair:
                    run(order, pair, pair + 1, False)
                run(last_order, PAIRS - 1, PAIRS, False)

        nc.clear_and_free_semaphores(sems)
        nc.all_engine_barrier()


def layernorm_steps(keep, shp, stats, mv, rstd, s_stat, s_aggr, s_std, s_rstd):
    x = keep["x"]

    def on_vector(dve):
        for t in range(shp.NT):
            dve.bn_stats(stats[:, t, :], x[:, t, :]).then_inc(s_stat, 1)
        for t in range(shp.NT):
            dve.wait_ge(s_stat, t + 1)
            dve.bn_aggr(mv[:, t, :], stats[:, t, :]).then_inc(s_aggr, 1)
        dve.wait_ge(s_std, 1)
        dve.reciprocal(rstd[:, :], rstd[:, :]).then_inc(s_rstd, 1)
        dve.wait_ge(s_rstd, 1)

    def on_scalar(act):
        act.wait_ge(s_aggr, shp.NT)
        act.activation(rstd[:, :], mv[:, :, 1], ACT.Sqrt, bias=keep["eps"][:, 0:1]).then_inc(s_std, 1)

    return on_vector, on_scalar


def skewed(eng, tiles, ring, offsets, emit):
    deepest = max(offsets.values())
    head = -(-(deepest + ring) // ring) * ring

    def peeled(steps):
        for n in steps:
            for stage, off in offsets.items():
                if 0 <= n - off < tiles:
                    emit(stage, 0, n - off)

    peeled(range(head))
    with eng.Fori(head // ring, tiles // ring) as turn:
        for phase in range(ring):
            for stage, off in offsets.items():
                emit(stage, turn, phase - off)
    peeled(range(tiles, tiles + deepest))


def static_tile(turn, c):
    return c if isinstance(turn, int) else None


def ffn(nc, shp, keep, tag, w_red, w_g, scratch_in, scratch_out):
    T, D, NT, NC, TPC = shp.T, shp.D, shp.NT, shp.NC, shp.TPC
    E, GD, FCH, SLOTS = shp.E, shp.GD, shp.FCH, shp.SLOTS
    x, ident, wall = keep["x"], keep["ident"], keep["wall"]
    W1, W2, B1, B2 = keep["wall_cols"]
    WCOLS = keep["wall"].shape[2]
    U = 4

    with ExitStack() as ctx:
        def sb(name, shape, dt=F32):
            return ctx.enter_context(nc.sbuf_tensor(tag + name, shape, dt))

        sems = []

        def sem(name):
            sems.append(nc.alloc_semaphore(tag + name))
            return sems[-1]

        ps = [ctx.enter_context(nc.psum_tensor(f"{tag}ps{i}", [P, BANK], F32)) for i in range(8)]
        stats, mv, rstd = sb("stats", [P, NT, 6]), sb("mv", [P, NT, 2]), sb("rstd", [P, NT])
        xn, xnT = sb("xn", [P, NT, D]), sb("xnT", [D, T])
        wred, wg = sb("wred", [D, GD]), sb("wg", [E, GD])
        wg2, wgs, wgr, wgn, wgnT = sb("wg2", [E, GD]), sb("wgs", [E, 1]), sb("wgr", [E, 1]), sb("wgn", [E, GD]), sb("wgnT", [GD, E])
        redT = sb("redT", [GD, T])
        lmax, sub, ex = sb("lmax", [P, NT]), sb("sub", [P, NT, E]), sb("ex", [P, NT, E])
        prio, best = sb("prio", [P, NT, E]), sb("best", [P, NT])
        onehot = sb("onehot", [P, E, NT], BF16)
        den, score = sb("den", [P, NT]), sb("score", [P, NT])
        cnt, incl, excl = sb("cnt", [P, E, NT]), sb("incl", [P, E, NT]), sb("excl", [P, E, NT])
        over, tiles, ends, starts = sb("over", [P, E, NT]), sb("tiles", [P, E]), sb("ends", [P, E]), sb("starts", [P, E])
        place, pos, pos_u = sb("place", [P, E, NT]), sb("pos", [P, NT]), sb("pos_u", [P, NT], U32)
        passed, slot_f, slot_e = sb("passed", [1, SLOTS, E]), sb("slot_f", [1, SLOTS]), sb("slot_e", [1, SLOTS], I32)
        xs = [sb(f"xs{k}", [P, D]) for k in range(U)]
        xsT = [sb(f"xsT{k}", [D, P]) for k in range(U)]
        wfix = [sb(f"wfix{k}", [P, WCOLS]) for k in range(U)]
        hT = [sb(f"hT{k}", [P, FCH, P]) for k in range(U)]
        ys = [sb(f"ys{k}", [P, D]) for k in range(U)]
        got = sb("got", [P, NT, D])

        s_stat, s_aggr, s_std, s_rstd = sem("s_stat"), sem("s_aggr"), sem("s_std"), sem("s_rstd")
        s_gin, s_xn, s_xnTp, s_xnT = sem("s_gin"), sem("s_xn"), sem("s_xnTp"), sem("s_xnT")
        s_wg, s_wgsq, s_wgn, s_wgTp, s_wgT = sem("s_wg"), sem("s_wgsq"), sem("s_wgn"), sem("s_wgTp"), sem("s_wgT")
        s_red, s_redT, s_lg, s_sub, s_ex = sem("s_red"), sem("s_redT"), sem("s_lg"), sem("s_sub"), sem("s_ex")
        s_hot, s_rank, s_chain, s_pos, s_slot = sem("s_hot"), sem("s_rank"), sem("s_chain"), sem("s_pos"), sem("s_slot")
        s_scat = sem("s_scat")
        s_xs = [sem(f"s_xs{k}") for k in range(U)]
        s_xsTp, s_xsT, s_w, s_h, s_gelu, s_y, s_ys = (sem(n) for n in ("s_xsTp", "s_xsT", "s_w", "s_h", "s_gelu", "s_y", "s_ys"))
        s_store = [sem(f"s_store{k}") for k in range(U)]
        s_got = [sem(f"s_got{c}") for c in range(NC)]
        ln_vector, ln_scalar = layernorm_steps(keep, shp, stats, mv, rstd, s_stat, s_aggr, s_std, s_rstd)

        lg_ps, rank_ps = ps[6], ps[7]
        lg = lg_ps[:, 0:NT * E].rearrange("p (t e) -> p t e", e=E)
        wgT_ps = lg_ps[0:GD, BANK - E:BANK]
        rank = rank_ps[:, 0:E * NT].rearrange("p (e t) -> p e t", t=NT)
        count = rank_ps[:, E * NT:2 * E * NT].rearrange("p (e t) -> p e t", t=NT)

        def by_tile(ap):
            return ap.rearrange("p e t -> p t e")

        with nc.Block() as block:

            @block.sync
            def _(sp):
                sp.dma_start(wred[:, :], w_red).then_inc(s_gin, 16)
                sp.dma_start(wg[:, :], w_g).then_inc(s_wg, 16)
                sp.wait_ge(s_scat, 16 * NT)

                def emit(stage, turn, c):
                    s, k, n = U * turn + c, c % U, turn + c // U
                    if stage == "load":
                        if static_tile(turn, c) is None or c >= U:
                            sp.wait_ge(s_xsTp, s - U + 1)
                        sp.dma_start(xs[k][:, :], scratch_in[bass.ds(s * P, P), :]).then_inc(s_xs[k], 16)
                    else:
                        sp.wait_ge(s_ys, s + 1)
                        sp.dma_start(scratch_out[bass.ds(s * P, P), :], ys[k][:, :]).then_inc(s_store[k], 16)

                skewed(sp, SLOTS, U, {"load": 0, "store": U}, emit)
                for k in range(U):
                    sp.wait_ge(s_store[k], 16 * (SLOTS // U))

            @block.gpsimd
            def _(pool):
                pool.wait_ge(keep["s_scratch"], 16)
                pool.wait_ge(s_pos, 1)
                for t in range(NT):
                    pool.indirect_dma_start(scratch_in[:, :], bass.IndirectOffsetOnAxis(ap=pos_u[:, t:t + 1], axis=0),
                                            xn[:, t, :], None).then_inc(s_scat, 16)
                for k in range(U):
                    pool.wait_ge(s_store[k], 16 * (SLOTS // U))
                for t in range(NT):
                    pool.indirect_dma_start(got[:, t, :], None, scratch_out[:, :],
                                            bass.IndirectOffsetOnAxis(ap=pos_u[:, t:t + 1], axis=0)).then_inc(s_got[t // TPC], 16)

            @block.vector
            def _(dve):
                links = [0]

                def link(ins):
                    links[0] += 1
                    ins.then_inc(s_chain, 1)
                    dve.wait_ge(s_chain, links[0])

                dve.wait_ge(s_wg, 16)
                link(dve.tensor_tensor(wg2[:, :], wg[:, :], wg[:, :], ALU.mult))
                dve.tensor_reduce(wgs[:, :], wg2[:, :], AX.X, ALU.add).then_inc(s_wgsq, 1)
                ln_vector(dve)
                for t in range(NT):
                    dve.tensor_scalar(xn[:, t, :], x[:, t, :], mv[:, t, 0:1], rstd[:, t:t + 1],
                                      ALU.subtract, ALU.mult).then_inc(s_xn, 1)
                dve.wait_ge(s_std, 2)
                link(dve.tensor_scalar(wgr[:, :], wgr[:, :], 1e-4, None, ALU.max))
                link(dve.reciprocal(wgr[:, :], wgr[:, :]))
                dve.tensor_scalar(wgn[:, :], wg[:, :], wgr[:, 0:1], None, ALU.mult).then_inc(s_wgn, 1)
                dve.wait_ge(s_wgTp, 1)
                dve.tensor_copy(wgnT[:, :], wgT_ps).then_inc(s_wgT, 1)
                for c in range(NC):
                    dve.wait_ge(s_red, c + 1)
                    dve.tensor_copy(redT[:, c * BANK:(c + 1) * BANK], ps[4 + c % 2][0:GD, :]).then_inc(s_redT, 1)

                dve.wait_ge(s_lg, 1)
                link(dve.tensor_reduce(lmax[:, :], lg, AX.X, ALU.max))
                dve.tensor_tensor(sub[:, :, :], lg, lmax[:, :].unsqueeze(2).to_broadcast([P, NT, E]), ALU.subtract).then_inc(s_sub, 1)
                dve.wait_ge(s_sub, 1)
                link(dve.scalar_tensor_tensor(prio[:, :, :], sub[:, :, :], 0.0, keep["prio"][:, :, :], ALU.is_ge, ALU.mult))
                link(dve.tensor_reduce(best[:, :], prio[:, :, :], AX.X, ALU.max))
                dve.tensor_tensor(by_tile(onehot[:, :, :]), prio[:, :, :], best[:, :].unsqueeze(2).to_broadcast([P, NT, E]),
                                  ALU.is_equal).then_inc(s_hot, 1)
                dve.wait_ge(s_ex, 1)
                link(dve.tensor_reduce(den[:, :], ex[:, :, :], AX.X, ALU.add))
                link(dve.reciprocal(score[:, :], den[:, :]))

                dve.wait_ge(s_rank, 1)
                link(dve.tensor_copy(cnt[:, :, :], count))
                flat = [a[:, :, :].rearrange("p e t -> p (e t)") for a in (incl, keep["restart"], cnt)]
                link(dve.tensor_tensor_scan(flat[0], flat[1], flat[2], 0.0, ALU.mult, ALU.add))
                dve.tensor_tensor(excl[:, :, :], incl[:, :, :], cnt[:, :, :], ALU.subtract)
                link(dve.tensor_tensor(over[:, :, :], incl[:, :, NT - 1:NT].to_broadcast([P, E, NT]), keep["full"][:, :, :], ALU.is_gt))
                link(dve.tensor_reduce(tiles[:, :], over[:, :, :], AX.X, ALU.add))
                link(dve.tensor_tensor_scan(ends[:, :], keep["ones8"][:, :], tiles[:, :], 0.0, ALU.mult, ALU.add))
                link(dve.tensor_tensor(starts[:, :], ends[:, :], tiles[:, :], ALU.subtract))
                link(dve.scalar_tensor_tensor(place[:, :, :], starts[:, :].unsqueeze(2).to_broadcast([P, E, NT]), float(P), excl[:, :, :],
                                              ALU.mult, ALU.add))
                link(dve.tensor_tensor(place[:, :, :], rank, place[:, :, :], ALU.add))
                link(dve.tensor_tensor(place[:, :, :], place[:, :, :], onehot[:, :, :], ALU.mult))
                link(dve.tensor_reduce(pos[:, :], by_tile(place[:, :, :]), AX.X, ALU.add))
                dve.tensor_copy(pos_u[:, :], pos[:, :]).then_inc(s_pos, 1)
                link(dve.tensor_tensor(passed[:, :, :], keep["slots"][:, :, :], ends[0:1, :].unsqueeze(1).to_broadcast([1, SLOTS, E]), ALU.is_ge))
                link(dve.tensor_reduce(slot_f[:, :], passed[:, :, :], AX.X, ALU.add))
                dve.tensor_scalar(slot_e[:, :], slot_f[:, :], float(E - 1), None, ALU.min).then_inc(s_slot, 1)

                dve.wait_ge(keep["s_wall"], 16 * (2 * FCH + 2))
                dve.wait_ge(s_slot, 1)

                def emit(stage, turn, c):
                    s, k = U * turn + c, c % U
                    if stage == "weights":
                        if static_tile(turn, c) is None or c >= U:
                            dve.wait_ge(s_ys, s - U + 1)
                        e = dve.value_load(slot_e[0:1, bass.ds(s, 1)], min_val=0, max_val=E - 1)
                        dve.tensor_copy(wfix[k][:, :], wall[:, bass.ds(e, 1), :].rearrange("p a n -> p (a n)")).then_inc(s_w, 1)
                    elif stage == "xT":
                        dve.wait_ge(s_xsTp, s + 1)
                        dve.tensor_copy(xsT[k][:, :], ps[c % 2][:, 0:P]).then_inc(s_xsT, 1)
                    else:
                        dve.wait_ge(s_y, s + 1)
                        if static_tile(turn, c) is None or c >= U:
                            dve.wait_ge(s_store[k], 16 * (turn + c // U))
                        dve.tensor_tensor(ys[k][:, :], ps[4 + c % 2][:, 0:D], wfix[k][:, B2], ALU.add).then_inc(s_ys, 1)

                skewed(dve, SLOTS, U, {"weights": 0, "xT": 0, "y": 2}, emit)
                for t in range(NT):
                    dve.wait_ge(s_got[t // TPC], 16 * TPC)
                    dve.scalar_tensor_tensor(x[:, t, :], got[:, t, :], score[:, t:t + 1], x[:, t, :], ALU.mult, ALU.add)

            @block.scalar
            def _(act):
                ln_scalar(act)
                act.wait_ge(s_wgsq, 1)
                act.activation(wgr[:, :], wgs[:, :], ACT.Sqrt).then_inc(s_std, 1)
                for c in range(NC):
                    act.wait_ge(s_xnTp, c + 1)
                    act.activation(xnT[:, c * BANK:(c + 1) * BANK], ps[c][:, :], ACT.Copy).then_inc(s_xnT, 1)
                act.wait_ge(s_sub, 1)
                act.activation(ex[:, :, :], sub[:, :, :], ACT.Exp).then_inc(s_ex, 1)

                def emit(stage, turn, c):
                    s, k = U * turn + c, c % U
                    act.wait_ge(s_w, s + 1)
                    act.wait_ge(s_h, s + 1)
                    for f in range(FCH):
                        last = act.activation(hT[k][:, f, :], ps[2 + c % 2][:, f * P:(f + 1) * P], ACT.Gelu,
                                              bias=wfix[k][:, B1.start + f:B1.start + f + 1])
                    last.then_inc(s_gelu, 1)

                skewed(act, SLOTS, U, {"gelu": 1}, emit)

            @block.tensor
            def _(pe):
                for t in range(NT):
                    pe.wait_ge(s_xn, t + 1)
                    last = pe.transpose(ps[t // TPC][:, t % TPC * P:(t % TPC + 1) * P], xn[:, t, :], ident[:, :])
                    if t % TPC == TPC - 1:
                        last.then_inc(s_xnTp, 1)
                pe.wait_ge(s_wgn, 1)
                pe.transpose(wgT_ps, wgn[:, :], ident[0:E, 0:E]).then_inc(s_wgTp, 1)
                pe.wait_ge(s_gin, 16)
                for c in range(NC):
                    pe.wait_ge(s_xnT, c + 1)
                    if c >= 2:
                        pe.wait_ge(s_redT, c - 1)
                    pe.matmul(ps[4 + c % 2][0:GD, :], wred[:, :], xnT[:, c * BANK:(c + 1) * BANK],
                              start=True, stop=True).then_inc(s_red, 1)
                pe.wait_ge(s_wgT, 1)
                for t in range(NT):
                    pe.wait_ge(s_redT, t // TPC + 1)
                    last = pe.matmul(lg[:, t, :], redT[:, t * P:(t + 1) * P], wgnT[:, :], start=True, stop=True)
                last.then_inc(s_lg, 1)
                pe.wait_ge(s_hot, 1)
                hot = onehot[:, :, :].rearrange("p e t -> p (e t)")
                pe.matmul(rank_ps[:, 0:E * NT], keep["before"][:, :], hot, start=True, stop=True)
                pe.matmul(rank_ps[:, E * NT:2 * E * NT], keep["all"][:, :], hot, start=True, stop=True).then_inc(s_rank, 1)

                def emit(stage, turn, c):
                    s, k = U * turn + c, c % U
                    first = static_tile(turn, c) is not None and c < 2
                    if stage == "xT":
                        pe.wait_ge(s_xs[k], 16 * (turn + c // U + 1))
                        if not first:
                            pe.wait_ge(s_xsT, s - 1)
                        pe.transpose(ps[c % 2][:, 0:P], xs[k][:, :], ident[:, :]).then_inc(s_xsTp, 1)
                    elif stage == "h":
                        pe.wait_ge(s_xsT, s + 1)
                        pe.wait_ge(s_w, s + 1)
                        if not first:
                            pe.wait_ge(s_gelu, s - 1)
                        for f in range(FCH):
                            last = pe.matmul(ps[2 + c % 2][:, f * P:(f + 1) * P], wfix[k][:, f * P:(f + 1) * P], xsT[k][:, :],
                                             start=True, stop=True)
                        last.then_inc(s_h, 1)
                    else:
                        pe.wait_ge(s_gelu, s + 1)
                        if not first:
                            pe.wait_ge(s_ys, s - 1)
                        for f in range(FCH):
                            last = pe.matmul(ps[4 + c % 2][:, 0:D], hT[k][:, f, :], wfix[k][:, W2.start + f * D:W2.start + (f + 1) * D],
                                             start=f == 0, stop=f == FCH - 1)
                        last.then_inc(s_y, 1)

                skewed(pe, SLOTS, U, {"xT": 0, "h": 1, "y": 2}, emit)

        nc.clear_and_free_semaphores(sems)
        nc.all_engine_barrier()


def linear_attention(nc, shp, keep, w_qkv, b_qkv, w_out, b_out):
    D, NT = shp.D, shp.NT
    HL, DL = shp.HL, D // shp.HL
    VX = HL * (DL + 1)
    OUTER = D * (DL + 1)
    EPS = 1e-6
    U = 2
    x, ident = keep["x"], keep["ident"]

    with ExitStack() as ctx:
        def sb(name, shape, dt=F32):
            return ctx.enter_context(nc.sbuf_tensor("li_" + name, shape, dt))

        def pair(name, shape):
            return [sb(f"{name}{k}", shape) for k in range(U)]

        sems = []

        def sem(name):
            sems.append(nc.alloc_semaphore("li_" + name))
            return sems[-1]

        sums_ps = ctx.enter_context(nc.psum_tensor("li_sums", [P, 3 * BANK], F32))
        xT_ps, z_ps, qT_ps, st_ps, y_ps = (ctx.enter_context(nc.psum_tensor("li_" + n, [P, BANK], F32))
                                           for n in ("xTp", "zp", "qTp", "stp", "yp"))
        delta, inter = qT_ps[:, P:P + VX], st_ps[:, 0:VX]
        oT_ps, out_ps = y_ps[:, 0:P], y_ps[:, P:P + D]

        stats, mv, rstd = sb("stats", [P, NT, 6]), sb("mv", [P, NT, 2]), sb("rstd", [P, NT])
        w_nat, wo_nat = sb("w_nat", [P, 3, D]), sb("wo_nat", [P, D])
        wT = sb("wT", [P, 4, P])
        b_row, bo_all = sb("b_row", [1, 3 * D]), sb("bo_all", [P, D])
        ones = sb("ones", [1, P])
        upto = sb("upto", [P, P])
        block_mask = sb("block_mask", [P, HL, DL + 1])
        xn, xT = pair("xn", [P, D]), pair("xT", [D, P])
        neg, ex = pair("neg", [P, 2 * D]), pair("ex", [P, 2 * D])
        qk, v1 = pair("qk", [P, 2 * D]), pair("v1", [P, HL, DL + 1])
        outer, prod = pair("outer", [P, HL, DL, DL + 1]), sb("prod", [P, D, DL + 1])
        qT, fresh, state = pair("qT", [D, P]), pair("fresh", [P, VX]), pair("state", [P, VX])
        own, tot = sb("own", [P, HL, DL + 1]), sb("tot", [P, HL, DL + 1])
        den, o, oT = sb("den", [P, HL]), pair("o", [P, HL, DL]), pair("oT", [P, P])

        s_in, s_bias, s_bout = sem("s_in"), sem("s_bias"), sem("s_bout")
        s_c, s_const, s_init = sem("s_c"), sem("s_const"), sem("s_init")
        s_stat, s_aggr, s_std, s_rstd = sem("s_stat"), sem("s_aggr"), sem("s_std"), sem("s_rstd")
        s_wTp, s_wT = sem("s_wTp"), sem("s_wT")
        s_xn, s_xTp, s_xT, s_z, s_neg, s_ex, s_v, s_qk = (sem(n) for n in ("s_xn", "s_xTp", "s_xT", "s_z", "s_neg", "s_ex", "s_v", "s_qk"))
        s_outer, s_sums, s_prod, s_delta, s_fresh, s_state, s_inter = (
            sem(n) for n in ("s_outer", "s_sums", "s_prod", "s_delta", "s_fresh", "s_state", "s_inter"))
        s_qTp, s_qT, s_own, s_tot, s_den, s_rden, s_o, s_oTp, s_oT, s_out, s_xb, s_x = (
            sem(n) for n in ("s_qTp", "s_qT", "s_own", "s_tot", "s_den", "s_rden", "s_o", "s_oTp", "s_oT", "s_out", "s_xb", "s_x"))
        ln_vector, ln_scalar = layernorm_steps(keep, shp, stats, mv, rstd, s_stat, s_aggr, s_std, s_rstd)

        def first(turn, c):
            return static_tile(turn, c) == 0

        with nc.Block() as block:

            @block.sync
            def _(sp):
                sp.dma_start(w_nat[:, :, :], w_qkv.rearrange("(a p) d -> p a d", p=P)).then_inc(s_in, 16)
                sp.dma_start(wo_nat[:, :], w_out).then_inc(s_in, 16)
                sp.dma_start(b_row[:, :], b_qkv.unsqueeze(0)).then_inc(s_bias, 16)
                sp.dma_start(bo_all[:, :], b_out.unsqueeze(0).to_broadcast([P, D])).then_inc(s_bout, 16)

            @block.gpsimd
            def _(pool):
                pool.memset(upto[:, :], 1.0).then_inc(s_c, 1)
                pool.memset(block_mask[:, :, :], 1.0).then_inc(s_c, 1)
                pool.memset(ones[:, :], 1.0).then_inc(s_const, 1)
                for k in range(U):
                    pool.memset(v1[k][:, :, DL:DL + 1], 1.0).then_inc(s_const, 1)
                    pool.memset(state[k][:, :], 0.0).then_inc(s_const, 1)
                pool.wait_ge(s_c, 2)
                pool.affine_select(out=upto[:, :], in_=upto[:, :], compare_op=ALU.is_ge, fill=0.0, base=0,
                                   pattern=[[1, P]], channel_multiplier=-1).then_inc(s_const, 1)
                pool.affine_select(out=block_mask[:, :, :], in_=block_mask[:, :, :], compare_op=ALU.is_ge, fill=0.0, base=0,
                                   pattern=[[-DL, HL], [0, DL + 1]], channel_multiplier=1).then_inc(s_c, 1)
                pool.wait_ge(s_c, 3)
                pool.affine_select(out=block_mask[:, :, :], in_=block_mask[:, :, :], compare_op=ALU.is_ge, fill=0.0, base=DL - 1,
                                   pattern=[[DL, HL], [0, DL + 1]], channel_multiplier=-1).then_inc(s_const, 1)
                pool.wait_ge(s_const, 2 * U + 3)
                pool.wait_ge(s_bout, 16)

                def emit(stage, turn, c):
                    t, k = U * turn + c, c % U
                    if stage == "bias":
                        pool.wait_ge(s_xn, t + 1)
                        rows = x[:, bass.ds(t, 1), :].rearrange("p a d -> p (a d)")
                        pool.tensor_tensor(rows, rows, bo_all[:, :], ALU.add).then_inc(s_xb, 1)
                    elif stage == "state":
                        pool.wait_ge(s_fresh, t + 1)
                        if not first(turn, c):
                            pool.wait_ge(s_state, t)
                        pool.tensor_tensor(state[k][:, :], state[1 - k][:, :], fresh[k][:, :], ALU.add).then_inc(s_state, 1)
                    else:
                        pool.wait_ge(s_qk, t + 1)
                        pool.wait_ge(s_v, t + 1)
                        kk = qk[k][:, D:2 * D].rearrange("p (h d) -> p h d", d=DL).unsqueeze(3).to_broadcast([P, HL, DL, DL + 1])
                        vv = v1[k][:, :, :].unsqueeze(2).to_broadcast([P, HL, DL, DL + 1])
                        pool.tensor_tensor(outer[k][:, :, :, :], kk, vv, ALU.mult).then_inc(s_outer, 1)

                skewed(pool, NT, U, {"bias": 0, "outer": 1, "state": 2}, emit)

            @block.vector
            def _(dve):
                ln_vector(dve)
                dve.wait_ge(s_const, 2 * U + 3)

                def emit(stage, turn, c):
                    t, k = U * turn + c, c % U
                    if stage == "norm":
                        rows = x[:, bass.ds(t, 1), :].rearrange("p a d -> p (a d)")
                        mean = mv[:, bass.ds(t, 1), 0:1].rearrange("p a b -> p (a b)")
                        dve.tensor_scalar(xn[k][:, :], rows, mean, rstd[:, bass.ds(t, 1)], ALU.subtract, ALU.mult).then_inc(s_xn, 1)
                    elif stage == "y":
                        dve.wait_ge(s_out, t + 1)
                        dve.wait_ge(s_xb, t + 1)
                        rows = x[:, bass.ds(t, 1), :].rearrange("p a d -> p (a d)")
                        dve.tensor_tensor(rows, out_ps, rows, ALU.add).then_inc(s_x, 1)
                    elif stage == "sums":
                        dve.wait_ge(s_delta, t + 1)
                        dve.tensor_tensor(fresh[k][:, :], delta, block_mask[:, :, :].rearrange("p h e -> p (h e)"), ALU.mult).then_inc(s_fresh, 1)
                        dve.wait_ge(s_sums, t + 1)
                        dve.tensor_tensor(prod[:, :, :], sums_ps[:, 0:OUTER].rearrange("p (c e) -> p c e", e=DL + 1),
                                          qk[k][:, 0:D].unsqueeze(2).to_broadcast([P, D, DL + 1]), ALU.mult).then_inc(s_prod, 1)
                    elif stage == "features":
                        dve.wait_ge(s_ex, t + 1)
                        dve.scalar_tensor_tensor(qk[k][:, :], z_ps[:, 0:2 * D], 0.0, ex[k][:, :], ALU.max, ALU.add).then_inc(s_qk, 1)
                    else:
                        dve.wait_ge(s_prod, t + 1)
                        dve.tensor_reduce(own[:, :, :], prod[:, :, :].rearrange("p (h d) e -> p h e d", d=DL), AX.X, ALU.add).then_inc(s_own, 1)
                        dve.wait_ge(s_inter, t + 1)
                        dve.wait_ge(s_own, t + 1)
                        dve.tensor_tensor(tot[:, :, :], inter.rearrange("p (h e) -> p h e", e=DL + 1), own[:, :, :], ALU.add).then_inc(s_tot, 1)
                        dve.wait_ge(s_tot, t + 1)
                        dve.tensor_scalar(den[:, :].unsqueeze(2), tot[:, :, DL:DL + 1], EPS, None, ALU.add).then_inc(s_den, 1)
                        dve.wait_ge(s_den, t + 1)
                        dve.reciprocal(den[:, :], den[:, :]).then_inc(s_rden, 1)
                        dve.wait_ge(s_rden, t + 1)
                        dve.tensor_tensor(o[k][:, :, :], tot[:, :, 0:DL], den[:, :].unsqueeze(2).to_broadcast([P, HL, DL]), ALU.mult).then_inc(s_o, 1)

                skewed(dve, NT, U, {"norm": 0, "y": 5, "heads": 3, "features": 1, "sums": 2}, emit)

            @block.scalar
            def _(act):
                act.wait_ge(s_const, 2 * U + 3)
                ln_scalar(act)
                act.wait_ge(s_wTp, 1)
                act.activation(wT[:, :, :].rearrange("p a f -> p (a f)"), sums_ps[:, 0:BANK], ACT.Copy).then_inc(s_wT, 1)

                def emit(stage, turn, c):
                    t, k = U * turn + c, c % U
                    if stage == "qT":
                        act.wait_ge(s_qTp, t + 1)
                        act.activation(qT[k][:, :], qT_ps[:, 0:P], ACT.Copy).then_inc(s_qT, 1)
                    elif stage == "xT":
                        act.wait_ge(s_xTp, t + 1)
                        act.activation(xT[k][:, :], xT_ps[:, 0:P], ACT.Copy).then_inc(s_xT, 1)
                    elif stage == "z":
                        act.wait_ge(s_z, t + 1)
                        act.activation(neg[k][:, :], z_ps[:, 0:2 * D], ACT.Relu, scale=-1.0).then_inc(s_neg, 1)
                        act.activation(v1[k][:, :, 0:DL], z_ps[:, 2 * D:3 * D].rearrange("p (h e) -> p h e", e=DL), ACT.Copy).then_inc(s_v, 1)
                        act.wait_ge(s_neg, t + 1)
                        act.activation(ex[k][:, :], neg[k][:, :], ACT.Exp, scale=-1.0).then_inc(s_ex, 1)
                    else:
                        act.wait_ge(s_oTp, t + 1)
                        act.activation(oT[k][:, :], oT_ps, ACT.Copy).then_inc(s_oT, 1)

                skewed(act, NT, U, {"qT": 2, "z": 1, "xT": 0, "oT": 4}, emit)

            @block.tensor
            def _(pe):
                pe.wait_ge(s_in, 32)
                for a in range(3):
                    pe.transpose(sums_ps[:, a * P:(a + 1) * P], w_nat[:, a, :], ident[:, :])
                pe.transpose(sums_ps[:, 3 * P:4 * P], wo_nat[:, :], ident[:, :]).then_inc(s_wTp, 1)
                pe.wait_ge(s_const, 2 * U + 3)
                pe.wait_ge(s_bias, 16)
                pe.wait_ge(s_wT, 1)

                def emit(stage, turn, c):
                    t, k = U * turn + c, c % U
                    if stage == "y":
                        pe.wait_ge(s_oT, t + 1)
                        pe.matmul(out_ps, oT[k][:, :], wT[:, 3, :], start=True, stop=True).then_inc(s_out, 1)
                    elif stage == "qT":
                        pe.wait_ge(s_qk, t + 1)
                        if not first(turn, c):
                            pe.wait_ge(s_fresh, t)
                        pe.transpose(qT_ps[:, 0:P], qk[k][:, 0:D], ident[:, :]).then_inc(s_qTp, 1)
                    elif stage == "sums":
                        pe.wait_ge(s_v, t + 1)
                        pe.wait_ge(s_qT, t + 1)
                        pe.matmul(delta, qk[k][:, D:2 * D], v1[k][:, :, :].rearrange("p h e -> p (h e)"),
                                  start=True, stop=True).then_inc(s_delta, 1)
                        pe.wait_ge(s_outer, t + 1)
                        if not first(turn, c):
                            pe.wait_ge(s_prod, t)
                        flat = outer[k][:, :, :, :].rearrange("p h d e -> p (h d e)")
                        for a in range(0, OUTER, BANK):
                            b = min(a + BANK, OUTER)
                            last = pe.matmul(sums_ps[:, a:b], upto[:, :], flat[:, a:b], start=True, stop=True)
                        last.then_inc(s_sums, 1)
                        if not first(turn, c):
                            pe.wait_ge(s_tot, t)
                            pe.wait_ge(s_state, t)
                        pe.matmul(inter, qT[k][:, :], state[1 - k][:, :], start=True, stop=True).then_inc(s_inter, 1)
                    elif stage == "xT":
                        pe.wait_ge(s_xn, t + 1)
                        if not first(turn, c):
                            pe.wait_ge(s_xT, t)
                        pe.transpose(xT_ps[:, 0:P], xn[k][:, :], ident[:, :]).then_inc(s_xTp, 1)
                    elif stage == "z":
                        pe.wait_ge(s_xT, t + 1)
                        if not first(turn, c):
                            pe.wait_ge(s_qk, t)
                            pe.wait_ge(s_v, t)
                        pe.matmul(z_ps[:, 0:3 * D], xT[k][:, :], wT[:, 0:3, :].rearrange("p a f -> p (a f)"), start=True, stop=False)
                        pe.matmul(z_ps[:, 0:3 * D], ones[:, :], b_row[:, :], start=False, stop=True).then_inc(s_z, 1)
                    else:
                        pe.wait_ge(s_o, t + 1)
                        if not first(turn, c):
                            pe.wait_ge(s_x, t)
                        pe.transpose(oT_ps, o[k][:, :, :].rearrange("p h e -> p (h e)"), ident[:, :]).then_inc(s_oTp, 1)

                skewed(pe, NT, U, {"y": 5, "qT": 2, "z": 1, "xT": 0, "sums": 2, "oT": 4}, emit)

        nc.clear_and_free_semaphores(sems)
        nc.all_engine_barrier()


def prepare(nc, shp, keep, f_w1, f_b1, f_w2, f_b2, scratch_in):
    E, FCH, D, NT, SLOTS = shp.E, shp.FCH, shp.D, shp.NT, shp.SLOTS
    W1, W2, B1, B2 = keep["wall_cols"]
    wall = keep["wall"]
    s_z, s_c = keep["s_z"], keep["s_c"]
    with nc.Block() as block:

        @block.vector
        def _(dve):
            dve.memset(keep["eps"][:, :], LN_EPS)
            dve.memset(keep["zeros"][:, :], 0.0).then_inc(s_z, 1)
            dve.memset(keep["ones8"][:, :], 1.0)
            dve.memset(keep["all"][:, :], 1.0)
            dve.wait_ge(s_c, 1)
            dve.tensor_scalar(keep["restart"][:, :, :], keep["restart"][:, :, :], 1.0, None, ALU.min)

        @block.gpsimd
        def _(pool):
            pool.iota(keep["restart"][:, :, :], pattern=[[0, E], [1, NT]], base=0, channel_multiplier=0,
                      allow_small_or_imprecise_dtypes=True).then_inc(s_c, 1)
            pool.iota(keep["full"][:, :, :], pattern=[[0, E], [P, NT]], base=0, channel_multiplier=0,
                      allow_small_or_imprecise_dtypes=True)
            pool.iota(keep["prio"][:, :, :], pattern=[[0, NT], [-1, E]], base=E, channel_multiplier=0,
                      allow_small_or_imprecise_dtypes=True)
            pool.iota(keep["slots"][:, :, :], pattern=[[1, SLOTS], [0, E]], base=0, channel_multiplier=0,
                      allow_small_or_imprecise_dtypes=True)
            pool.memset(keep["before"][:, :], 1.0).then_inc(s_c, 1)
            pool.wait_ge(s_c, 2)
            pool.affine_select(out=keep["before"][:, :], in_=keep["before"][:, :], compare_op=ALU.is_gt, fill=0.0, base=0,
                               pattern=[[1, P]], channel_multiplier=-1)

    def fetch(sp):
        sp.wait_ge(s_z, 1)
        sp.dma_start(scratch_in.rearrange("(s p) d -> p s d", p=P),
                     keep["zeros"][:, :].unsqueeze(1).to_broadcast([P, SLOTS, D])).then_inc(keep["s_scratch"], 16)
        sp.dma_start(wall[:, :, W1], f_w1.rearrange("e d f -> d e f")).then_inc(keep["s_wall"], 16)
        for f in range(FCH):
            sp.dma_start(wall[:, :, W2.start + f * D:W2.start + (f + 1) * D],
                         f_w2[:, f * P:(f + 1) * P, :].rearrange("e p d -> p e d")).then_inc(keep["s_wall"], 16)
            sp.dma_start(wall[:, :, B1.start + f:B1.start + f + 1],
                         f_b1[:, f * P:(f + 1) * P].rearrange("e (p a) -> p e a", a=1), allow_slow_non_contiguous=True).then_inc(keep["s_wall"], 16)
        sp.dma_start(wall[:, :, B2], f_b2.unsqueeze(0).to_broadcast([P, E, D])).then_inc(keep["s_wall"], 16)

    return fetch


def bass_hybrid_layers(nc, a_x, w_k, w_q, w_v, w_o, b_wqkv, b_bqkv, b_wout, b_bout,
                       f_wred, f_wg, f_w1, f_b1, f_w2, f_b2, out):
    shp = Shapes(a_x, w_k, f_wg, f_w1)
    NT, D, E = shp.NT, shp.D, shp.E
    hid = shp.FCH * P
    scratch_in = nc.dram_tensor("slots_in", (shp.SLOTS * P, D), F32).ap()
    scratch_out = nc.dram_tensor("slots_out", (shp.SLOTS * P, D), F32).ap()
    with ExitStack() as ctx:
        def sb(name, shape, dt=F32):
            return ctx.enter_context(nc.sbuf_tensor(name, shape, dt))

        keep = {
            "x": sb("x", [P, NT, D]), "ident": sb("ident", [P, P]), "eps": sb("eps", [P, 1]), "zeros": sb("zeros", [P, D]),
            "wall": sb("wall", [P, E, 2 * hid + shp.FCH + D]),
            "wall_cols": (slice(0, hid), slice(hid, 2 * hid), slice(2 * hid, 2 * hid + shp.FCH),
                          slice(2 * hid + shp.FCH, 2 * hid + shp.FCH + D)),
            "restart": sb("restart", [P, E, NT]), "full": sb("full", [P, E, NT]), "prio": sb("prio", [P, NT, E]),
            "slots": sb("slots", [1, shp.SLOTS, E]), "ones8": sb("ones8", [P, E]),
            "before": sb("before", [P, P], BF16), "all": sb("all", [P, P], BF16),
        }
        for n in ("s_z", "s_c", "s_scratch", "s_wall"):
            keep[n] = ctx.enter_context(nc.semaphore(n))
        s_out = ctx.enter_context(nc.semaphore("s_out"))
        fetch = prepare(nc, shp, keep, f_w1, f_b1, f_w2, f_b2, scratch_in)
        attention(nc, shp, keep, a_x, w_k, w_q, w_v, w_o, fetch)
        ffn(nc, shp, keep, "f0_", f_wred, f_wg, scratch_in, scratch_out)
        linear_attention(nc, shp, keep, b_wqkv, b_bqkv, b_wout, b_bout)
        ffn(nc, shp, keep, "f1_", f_wred, f_wg, scratch_in, scratch_out)

        with nc.Block() as block:
            @block.sync
            def _(sp):
                sp.dma_start(out[0].rearrange("(t p) d -> p t d", p=P), keep["x"][:, :, :]).then_inc(s_out, 16)
                sp.wait_ge(s_out, 16)


_INS = ['L0_attn_a_x', 'L0_attn_a_W_K', 'L0_attn_a_W_Q', 'L0_attn_a_W_V', 'L0_attn_a_W_O',
        'L0_attn_b_w_qkv', 'L0_attn_b_b_qkv', 'L0_attn_b_w_out', 'L0_attn_b_b_out',
        'L0_ffn_w_red', 'L0_ffn_wg', 'L0_ffn_w1', 'L0_ffn_b1', 'L0_ffn_w2', 'L0_ffn_b2']
_OUTS = [((1, 2048, 128), 'float32')]


def kernel(**inputs):
    import numpy as _np
    import concourse.bacc as _bacc
    from concourse import mybir as _mybir
    from concourse.bass_utils import run_bass_kernel_spmd as _run

    nc = _bacc.Bacc("TRN2", target_bir_lowering=False, num_devices=1)
    arrays, args = {}, []
    for name in _INS:
        a = _np.ascontiguousarray(inputs[name])
        arrays[f"in_{name}_dram"] = a
        args.append(nc.dram_tensor(f"in_{name}_dram", a.shape, _mybir.dt.from_np(a.dtype), kind="ExternalInput").ap())
    for i, (shape, dtype) in enumerate(_OUTS):
        dt = _mybir.dt.from_np(_np.dtype(dtype))
        args.append(nc.dram_tensor(f"out_{i}_dram", shape, dt, kind="ExternalOutput").ap())
    bass_hybrid_layers(nc, *args)
    r = _run(nc, [arrays], core_ids=[0])
    got = tuple(r.results[0][f"out_{i}_dram"] for i in range(len(_OUTS)))
    return got[0]
```

```python
from contextlib import ExitStack

import concourse.bass as bass
from concourse import mybir

F32 = mybir.dt.float32
F32R = mybir.dt.float32r
BF16 = mybir.dt.bfloat16
I32 = mybir.dt.int32
U32 = mybir.dt.uint32
ALU = mybir.AluOpType
ACT = mybir.ActivationFunctionType
AX = mybir.AxisListType

P = 128
BANK = 512
MASKED = -1e30
LN_EPS = 1e-5


class Shapes:

    def __init__(self, x, w_k, w_g, w_1):
        self.T, self.D = x.shape[1], x.shape[2]
        self.H, self.DH = w_k.shape[0], w_k.shape[1]
        self.NT = self.T // P
        self.NC = self.T // BANK
        self.TPC = BANK // P
        self.PAIRS = self.H * self.DH // P
        self.HL = 16
        self.E, self.GD = w_g.shape
        self.FCH = w_1.shape[2] // P
        self.SLOTS = -(-(self.NT + self.E - 1) // 4) * 4


def make_identity(pool, tile, done, ready):
    pool.memset(tile, 0.0).then_inc(done, 1)
    pool.wait_ge(done, 1)
    pool.affine_select(out=tile, in_=tile, compare_op=ALU.not_equal, fill=1.0, base=0,
                       pattern=[[-1, P]], channel_multiplier=1).then_inc(ready, 1)


def attention(nc, shp, keep, x_in, w_k, w_q, w_v, w_o, fetch):
    T, D, DH, NT, NC, TPC, PAIRS = shp.T, shp.D, shp.DH, shp.NT, shp.NC, shp.TPC, shp.PAIRS
    x, ident = keep["x"], keep["ident"]
    SCALE = float(DH) ** -0.5
    RING = 5
    STEPS = NT // 2
    UNITS = 4 * STEPS
    SLOTS = 8

    def row(u):
        return u // 4 * 2 + u % 4 // 2

    def chunks(u):
        return row(u) // TPC + 1

    def width(u, c):
        return min(BANK, (row(u) + 1) * P - c * BANK)

    first_chunk = [sum(chunks(b) for b in range(u)) for u in range(UNITS + 1)]
    N_SC = first_chunk[UNITS]
    first_group = [j * (j + 1) // 2 for j in range(STEPS + 1)]
    N_GR = first_group[STEPS]
    N_PJ = 2 * NC
    N_V = NC
    V_FIRST = N_SC + N_PJ
    V_BANKS = [RING - 2, RING - 1] * (N_V // 2)
    BANKS = [use % RING for use in range(V_FIRST)] + V_BANKS

    def back_of(j):
        items = []
        for g in range(j + 1):
            items += [("turn", j, 0, g), ("turn", j, 1, g)]
            if g:
                items += [("value", j, g - 1), None]
        return items + [("value", j, j), None, ("leave", j)]

    def spread(items, weights):
        ends = [round(len(items) * sum(weights[:i]) / sum(weights)) for i in range(len(weights) + 1)]
        return [items[a:b] for a, b in zip(ends, ends[1:])]

    def slot_weights(n, opens):
        w = [1] * n
        return [0] * ((n + 1) // 2) + w[(n + 1) // 2:] if opens and n > 1 else w

    def exp_slot(c, ne):
        return max(c - 1, 0)

    LATE = 4

    def issue_order(projections):
        order, rest = [], []
        for w in range(UNITS + 1):
            ns = chunks(w) if w < UNITS else 0
            ne = chunks(w - 1) if w else 0
            opens = w % 4 == 1 and w > 4
            fill = []
            if opens:
                j = w // 4 - 1
                lens = [max(chunks(u) if u < UNITS else 0, chunks(u - 1)) for u in range(w, w + 4)]
                items = back_of(j)
                fill = [rest[:2], rest[2:3], rest[3:4], rest[4:]] if len(rest) > 2 else [rest]
                if j < STEPS - 2 and chunks(4 * (j + 2)) == NC:
                    items, rest = items[:-LATE], items[-LATE:]
                else:
                    rest = []
                rest = rest + [("out", j), ("add", j)]
                dealt = spread(items, [v for i, n in enumerate(lens) for v in slot_weights(n, i == 0)])
            for k in range(max(ns, ne)):
                if k < ns:
                    order.append(("score", w, k))
                if opens and k == 0:
                    order.append(("sums", j))
                order += fill.pop(0) if fill else []
                order += dealt.pop(0) if w > 4 else []
                order += [("exp", w - 1, c) for c in range(ne) if exp_slot(c, ne) == k]
        j = STEPS - 1
        if not projections:
            order += [("sums", j), ("out", j - 1), ("add", j - 1)] + back_of(j) + [("out", j), ("add", j)]
            return [it for item in order for it in ([item, ("stats", item[1])] if item and item[0] == "add" else [item])]
        order += [("project", 0), ("sums", j), ("project", 1), ("out", j - 1), ("add", j - 1), ("low", 0)]
        for i, items in enumerate(spread(back_of(j), [1] * (N_PJ - 2))):
            order += [("project", i + 2)] + items + [("low", i + 1)]
        values = [("vproject", m) for m in range(N_V)]
        return order + values[:1] + [("low", N_PJ - 1)] + values[1:2] + [("out", j), ("add", j)] + values[2:]

    order, last_order = ([it for it in issue_order(projections) if it] for projections in (True, False))
    opening = [(step, i) for i in range(N_PJ) for step in ("project", "low")] + [("vproject", m) for m in range(N_V)]

    with ExitStack() as ctx:
        def sb(name, shape, dt=F32):
            return ctx.enter_context(nc.sbuf_tensor("at_" + name, shape, dt))

        sems = []

        def sem(name):
            sems.append(nc.alloc_semaphore("at_" + name))
            return sems[-1]

        ps = [ctx.enter_context(nc.psum_tensor(f"at_ps{i}", [P, BANK], F32)) for i in range(8)]
        ring = ps[:RING]
        turn_ps = ps[RING:RING + 2]
        z_ps = ps[RING + 2][:, 0:2 * P]
        o_ps = [ps[RING + 2][:, 2 * D:4 * D], ps[RING + 2][:, 0:2 * D]]

        stats = sb("stats", [P, NT, 6])
        mv = keep["mv"]
        rstd = sb("rstd", [P, NT])
        xnT = sb("xnT", [D, T])
        wT = {n: sb("wT_" + n, [P, PAIRS, P]) for n in "qkv"}
        wo_bd = sb("wo_bd", [P, PAIRS, 2, D])
        wq_fix, wk_fix = sb("wq_fix", [D, P]), sb("wk_fix", [D, P])
        k_st = [sb(f"k_st{h}", [P, T], F32R) for h in range(2)]
        q_parts = [sb(f"q_parts{h}", [P, 2, T], F32R) for h in range(2)]
        q_hi, q_lo = ([q[:, i, :] for q in q_parts] for i in range(2))
        v = sb("v", [P, NT, P])
        prob = [[sb(f"prob{k}{i}", [P, T - P * (i < 2)]) for i in range(4)] for k in range(2)]
        wnat = {n: prob[0][i][:, 0:PAIRS * P].rearrange("p (a f) -> p a f", f=P) for i, n in enumerate("qkv")}
        wnat_o = prob[0][3][:, 0:PAIRS * P]
        xn = prob[1][2][:, 0:NT * D].rearrange("p (t d) -> p t d", d=D)
        probT = [[sb(f"probT{h}{k}", [P, BANK]) for k in range(2)] for h in range(2)]
        zT = [sb(f"zT{k}", [P, 2 * P]) for k in range(2)]
        cmax = sb("cmax", [P, SLOTS, NC])
        nmax = sb("nmax", [P, SLOTS])
        esum = sb("esum", [P, 2, 4, NC])
        rsum, rinv = sb("rsum", [P, 2, 4]), sb("rinv", [P, 2, 4])
        identb = sb("identb", [P, P], BF16)
        maskb = sb("maskb", [P, P], BF16)

        s_xin, s_win = sem("s_xin"), [sem(f"s_win{i}") for i in range(4)]
        s_c0, s_c1, s_c2, s_const = sem("s_c0"), sem("s_c1"), sem("s_c2"), sem("s_const")
        s_stat, s_aggr, s_std, s_rstd, s_xn = (sem(n) for n in ("s_stat", "s_aggr", "s_std", "s_rstd", "s_xn"))
        s_setT, s_setcp = sem("s_setT"), sem("s_setcp")
        s_wfix = sem("s_wfix")
        s_second = [sem(f"s_second{c}") for c in range(NC)]
        s_proj, s_hi, s_lo = sem("s_proj"), sem("s_hi"), sem("s_lo")
        s_vproj, s_v = sem("s_vproj"), sem("s_v")
        s_score, s_cmax, s_nmax, s_exp = sem("s_score"), sem("s_cmax"), sem("s_nmax"), sem("s_exp")
        s_turn = [sem(f"s_turn{h}") for h in range(2)]
        s_probT = [sem(f"s_probT{h}") for h in range(2)]
        s_z, s_zT, s_o = sem("s_z"), sem("s_zT"), sem("s_o")
        s_rsum, s_rinv, s_acc1, s_acc2 = sem("s_rsum"), sem("s_rinv"), sem("s_acc1"), sem("s_acc2")

        N_SET = 4 * PAIRS // TPC + NC
        FIRST_MANY = next(u for u in range(UNITS) if chunks(u) > 1)
        N_CMAX = N_SC - first_chunk[FIRST_MANY]
        FIRST_SUMS = FIRST_MANY // 4
        N_RSUM = STEPS - FIRST_SUMS

        with nc.Block() as block:

            @block.sync
            def _(sp):
                sp.dma_start(x[:, :, :], x_in[0].rearrange("(t p) d -> p t d", p=P)).then_inc(s_xin, 16)
                for i, (n, w) in enumerate((("q", w_q), ("k", w_k), ("v", w_v))):
                    sp.dma_start(wnat[n], w.rearrange("h f d -> (h f) d").rearrange("(a p) d -> p a d", p=P)).then_inc(s_win[i], 16)
                sp.dma_start(wnat_o, w_o).then_inc(s_win[3], 16)

                def second_copies(made):
                    for c in range(NC):
                        cols = slice(c * BANK, (c + 1) * BANK)
                        sp.wait_ge(s_lo, N_PJ * made + NC + c + 1)
                        for h in range(2):
                            here, there = slice(DH * h, DH * (h + 1)), slice(DH * (1 - h), DH * (2 - h))
                            sp.dma_start(q_parts[h][there, :, cols].bitcast(F32), q_parts[h][here, :, cols].bitcast(F32)).then_inc(s_second[c], 16)

                second_copies(0)
                fetch(sp)
                with sp.Fori(0, PAIRS - 1) as pair:
                    second_copies(pair + 1)

            @block.gpsimd
            def _(pool):
                pool.sem_inc(s_probT[0], 1)
                pool.sem_inc(s_probT[1], 1)
                pool.sem_inc(s_acc2, 1)
                make_identity(pool, ident[:, :], s_c0, s_const)
                make_identity(pool, identb[:, :], s_c1, s_const)
                pool.memset(maskb[:, :], 0.0).then_inc(s_c2, 1)
                pool.wait_ge(s_c2, 1)
                pool.affine_select(out=maskb[:, :], in_=maskb[:, :], compare_op=ALU.is_ge, fill=MASKED, base=0,
                                   pattern=[[-1, P]], channel_multiplier=1).then_inc(s_const, 1)
                pool.memset(wo_bd[:, :, :, :], 0.0).then_inc(s_const, 1)
                pool.wait_ge(s_setcp, N_SET - NC)

                def projection_weights(pair):
                    for fix, n in ((wk_fix, "k"), (wq_fix, "q")):
                        last = pool.tensor_copy(fix[:, :], wT[n][:, bass.ds(pair, 1), :].rearrange("d a f -> d (a f)"))
                    last.then_inc(s_wfix, 1)

                projection_weights(0)
                with pool.Fori(0, PAIRS - 1) as pair:
                    pool.wait_ge(s_proj, N_PJ * (pair + 1))
                    projection_weights(pair + 1)

            @block.vector
            def _(dve):
                dve.wait_ge(s_xin, 16)
                for t in range(NT):
                    dve.bn_stats(stats[:, t, :], x[:, t, :]).then_inc(s_stat, 1)
                for t in range(NT):
                    dve.wait_ge(s_stat, t + 1)
                    dve.bn_aggr(mv[:, t, :], stats[:, t, :]).then_inc(s_aggr, 1)
                dve.wait_ge(s_std, 1)
                dve.reciprocal(rstd[:, :], rstd[:, :]).then_inc(s_rstd, 1)
                dve.wait_ge(s_rstd, 1)
                for t in range(NT):
                    dve.tensor_scalar(xn[:, t, :], x[:, t, :], mv[:, t, 0:1], rstd[:, t:t + 1],
                                      ALU.subtract, ALU.mult).then_inc(s_xn, 1)

                def run(items, pair, made):
                    for it in items:
                        if it[0] == "score":
                            _, u, c = it
                            k = first_chunk[u] + c
                            bank = ring[k % RING][:, 0:width(u, c)]
                            dve.wait_ge(s_score, N_SC * pair + k + 1)
                            if chunks(u) == 1:
                                dve.tensor_reduce(nmax[:, u % SLOTS:u % SLOTS + 1], bank, AX.X, ALU.max, negate=True).then_inc(s_nmax, 1)
                                continue
                            dve.tensor_reduce(cmax[:, u % SLOTS, c:c + 1], bank, AX.X, ALU.max).then_inc(s_cmax, 1)
                            if c == chunks(u) - 1:
                                dve.wait_ge(s_cmax, N_CMAX * pair + k + 1 - first_chunk[FIRST_MANY])
                                dve.tensor_reduce(nmax[:, u % SLOTS:u % SLOTS + 1], cmax[:, u % SLOTS, 0:c + 1], AX.X, ALU.max,
                                                  negate=True).then_inc(s_nmax, 1)
                        elif it[0] == "turn" and it[2] == 1:
                            _, j, h, g = it
                            n, w = first_group[j] + g, (4 if g < j else 3) * P
                            dve.wait_ge(s_turn[1], N_GR * pair + n + 1)
                            dve.tensor_copy(probT[1][n % 2][:, 0:w], turn_ps[1][:, 0:w]).then_inc(s_probT[1], 1)
                        elif it[0] == "sums":
                            j = it[1]
                            n, k = chunks(4 * j), j % 2
                            dve.wait_ge(s_exp, N_SC * pair + first_chunk[4 * j + 4])
                            if n == 1:
                                dve.reciprocal(rinv[:, k, :].unsqueeze(2), esum[:, k, :, 0:1]).then_inc(s_rinv, 1)
                                continue
                            dve.tensor_reduce(rsum[:, k, :], esum[:, k, :, 0:n], AX.X, ALU.add).then_inc(s_rsum, 1)
                            dve.wait_ge(s_rsum, N_RSUM * pair + j + 1 - FIRST_SUMS)
                            dve.reciprocal(rinv[:, k, :], rsum[:, k, :]).then_inc(s_rinv, 1)
                        elif it[0] == "add":
                            j = it[1]
                            dve.wait_ge(s_rinv, STEPS * pair + j + 1)
                            dve.wait_ge(s_o, STEPS * pair + j + 1)
                            for h, done in enumerate((s_acc1, s_acc2)):
                                if h:
                                    dve.wait_ge(s_acc1, STEPS * pair + j + 1)
                                for i in range(2):
                                    last = dve.scalar_tensor_tensor(x[:, 2 * j + i, :], o_ps[i][:, h * D:(h + 1) * D],
                                                                    rinv[:, j % 2, 2 * i + h:2 * i + h + 1], x[:, 2 * j + i, :],
                                                                    ALU.mult, ALU.add)
                                last.then_inc(done, 1)
                        elif it[0] == "stats":
                            j = it[1]
                            dve.wait_ge(s_acc2, STEPS * pair + j + 2)
                            for t in (2 * j, 2 * j + 1):
                                last = dve.bn_stats(stats[:, t, :], x[:, t, :])
                            last.then_inc(s_stat, 1)
                            dve.wait_ge(s_stat, NT + j + 1)
                            for t in (2 * j, 2 * j + 1):
                                dve.bn_aggr(mv[:, t, :], stats[:, t, :])
                        elif it[0] == "low":
                            kind, c = divmod(it[1], NC)
                            cols = slice(c * BANK, (c + 1) * BANK)
                            bank = ring[(N_SC + it[1]) % RING]
                            dve.wait_ge(s_hi, N_PJ * made + it[1] + 1)
                            for h in range(2):
                                here, there = slice(DH * h, DH * (h + 1)), slice(DH * (1 - h), DH * (2 - h))
                                if kind == 0:
                                    last = dve.tensor_tensor(k_st[h][there, cols], bank[here, :],
                                                             k_st[h][here, cols].bitcast(F32), ALU.subtract)
                                    continue
                                last = dve.scalar_tensor_tensor(q_lo[h][here, cols], bank[here, :], SCALE,
                                                                q_hi[h][here, cols].bitcast(F32), ALU.mult, ALU.subtract)
                            last.then_inc(s_lo, 1)

                run(opening, 0, 0)
                with dve.Fori(0, PAIRS - 1) as pair:
                    run(order, pair, pair + 1)
                run(last_order, PAIRS - 1, PAIRS)

            @block.scalar
            def _(act):
                act.wait_ge(s_aggr, NT)
                act.activation(rstd[:, :], mv[:, :, 1], ACT.Sqrt, bias=keep["eps"][:, 0:1]).then_inc(s_std, 1)
                W_GROUPS = PAIRS // TPC
                dst = [wT[n][:, TPC * i:TPC * (i + 1), :] for n in "qkv" for i in range(W_GROUPS)]
                dst = [d.rearrange("p a f -> p (a f)") for d in dst]
                act.wait_ge(s_const, 4)
                for i in range(N_SET):
                    act.wait_ge(s_setT, i + 1)
                    if i < 3 * W_GROUPS:
                        last = act.activation(dst[i], ps[i % 8][:, :], ACT.Copy)
                    elif i < 4 * W_GROUPS:
                        pairs = slice(TPC * (i - 3 * W_GROUPS), TPC * (i - 3 * W_GROUPS + 1))
                        for h in range(2):
                            rows = slice(DH * h, DH * (h + 1))
                            last = act.activation(wo_bd[rows, pairs, h, :],
                                                  ps[i % 8][rows, :].rearrange("p (a d) -> p a d", d=D), ACT.Copy)
                    else:
                        c = i - 4 * W_GROUPS
                        last = act.activation(xnT[:, c * BANK:(c + 1) * BANK], ps[i % 8][:, :], ACT.Copy)
                    last.then_inc(s_setcp, 1)

                def run(items, pair, made):
                    for it in items:
                        if it[0] == "exp":
                            _, u, c = it
                            j, h, k, w = u // 4, u % 2, first_chunk[u] + c, width(u, c)
                            if c == 0:
                                act.wait_ge(s_nmax, UNITS * pair + u + 1)
                                if j >= 2 and u % 4 < 2:
                                    act.wait_ge(s_turn[h], N_GR * pair + first_group[j - 1])
                            act.activation(prob[j % 2][u % 4][:, c * BANK:c * BANK + w], ring[k % RING][:, 0:w], ACT.Exp,
                                           bias=nmax[:, u % SLOTS:u % SLOTS + 1],
                                           accum_out=esum[:, j % 2, u % 4, c:c + 1]).then_inc(s_exp, 1)
                        elif it[0] == "turn" and it[2] == 0:
                            _, j, h, g = it
                            n, w = first_group[j] + g, (4 if g < j else 3) * P
                            act.wait_ge(s_turn[0], N_GR * pair + n + 1)
                            act.activation(probT[0][n % 2][:, 0:w], turn_ps[0][:, 0:w], ACT.Copy).then_inc(s_probT[0], 1)
                        elif it[0] == "leave":
                            j = it[1]
                            act.wait_ge(s_z, STEPS * pair + j + 1)
                            act.activation(zT[j % 2][:, :], z_ps, ACT.Copy).then_inc(s_zT, 1)
                        elif it[0] == "project":
                            kind, c = divmod(it[1], NC)
                            cols = slice(c * BANK, (c + 1) * BANK)
                            bank = ring[(N_SC + it[1]) % RING]
                            act.wait_ge(s_proj, N_PJ * made + it[1] + 1)
                            for h in range(2):
                                here, there = slice(DH * h, DH * (h + 1)), slice(DH * (1 - h), DH * (2 - h))
                                if kind == 0:
                                    last = act.activation(k_st[h][here, cols], bank[here, :], ACT.Copy)
                                    continue
                                last = act.activation(q_hi[h][here, cols], bank[here, :], ACT.Copy, scale=SCALE)
                            last.then_inc(s_hi, 1)
                        elif it[0] == "vproject":
                            m = it[1]
                            act.wait_ge(s_vproj, N_V * made + m + 1)
                            act.activation(v[:, TPC * m:TPC * (m + 1), :].rearrange("p t f -> p (t f)"),
                                           ring[BANKS[V_FIRST + m]][:, :], ACT.Copy).then_inc(s_v, 1)

                act.activation(zT[0][:, 0:1], keep["eps"][:, 0:1], ACT.Exp)
                run(opening, 0, 0)
                with act.Fori(0, PAIRS - 1) as pair:
                    run(order, pair, pair + 1)
                run(last_order, PAIRS - 1, PAIRS)

            @block.tensor
            def _(pe):
                pe.wait_ge(s_const, 3)
                src = []
                for i, n in enumerate("qkv"):
                    src += [(s_win[i], 16, wnat[n][:, a, :]) for a in range(PAIRS)]
                src += [(s_win[3], 16, wnat_o[:, a * P:(a + 1) * P]) for a in range(PAIRS)]
                src += [(s_xn, t + 1, xn[:, t, :]) for t in range(NT)]
                for i, (ready, count, tile) in enumerate(src):
                    grp, k = divmod(i, TPC)
                    if k == 0 and grp >= 8:
                        pe.wait_ge(s_setcp, grp - 7)
                    pe.wait_ge(ready, count)
                    last = pe.transpose(ps[grp % 8][:, k * P:(k + 1) * P], tile, ident[:, :])
                    if k == TPC - 1:
                        last.then_inc(s_setT, 1)
                pe.wait_ge(s_setcp, N_SET)

                def free_bank(use, pair, made):
                    same = [u for u in range(len(BANKS)) if BANKS[u] == BANKS[use]]
                    before = max([u for u in same if u < use], default=None)
                    if before is None:
                        before, made = max(same), made - 1
                    if before >= V_FIRST:
                        pe.wait_ge(s_v, N_V * made + before - V_FIRST + 1)
                    elif before >= N_SC:
                        pe.wait_ge(s_lo, N_PJ * made + before - N_SC + 1)
                    else:
                        pe.wait_ge(s_exp, N_SC * pair + before + 1)

                def run(items, pair, made, first):
                    for it in items:
                        if it[0] == "score":
                            _, u, c = it
                            r, h = row(u), u % 2
                            if r % TPC == 0 and u % 4 == 0:
                                pe.wait_ge(s_lo, N_PJ * (made - 1) + r // TPC + 1)
                                pe.wait_ge(s_second[r // TPC], 32 * made)
                            k, w = first_chunk[u] + c, width(u, c)
                            free_bank(k, pair, made)
                            bank = ring[k % RING]
                            keys = k_st[h][:, c * BANK:c * BANK + w]
                            pe.matmul(bank[:, 0:w], q_hi[h][:, r * P:(r + 1) * P], keys, start=True, stop=False)
                            if c == chunks(u) - 1:
                                pe.matmul(bank[:, w - P:w], identb[:, :], maskb[:, :], start=False, stop=False)
                            last = pe.matmul(bank[:, 0:w], q_lo[h][:, r * P:(r + 1) * P], keys, start=False, stop=True)
                            last.then_inc(s_score, 1)
                        elif it[0] == "turn":
                            _, j, h, g = it
                            n = first_group[j] + g
                            if g == 0:
                                pe.wait_ge(s_exp, N_SC * pair + first_chunk[4 * j + 3 + h])
                            pe.wait_ge(s_probT[h], N_GR * pair + n + 1)
                            tiles = [(t, i) for t in (2 * g, 2 * g + 1) for i in range(2) if t <= 2 * j + i]
                            for b, (t, i) in enumerate(tiles):
                                last = pe.transpose(turn_ps[h][:, b * P:(b + 1) * P],
                                                    prob[j % 2][2 * i + h][:, t * P:(t + 1) * P], ident[:, :])
                            last.then_inc(s_turn[h], 1)
                        elif it[0] == "value":
                            _, j, g = it
                            n = first_group[j] + g
                            if j == 0:
                                pe.wait_ge(s_v, N_V * made)
                            if g == 0:
                                pe.wait_ge(s_acc2, STEPS * pair + j + 1)
                            for h in range(2):
                                pe.wait_ge(s_probT[h], N_GR * pair + n + 2)
                            for h, b in ((0, 0), (1, 0), (1, 1), (0, 1)):
                                t = 2 * g + b
                                last_tile = t == 2 * j + 1
                                to, w = (P, P) if last_tile else (0, 2 * P)
                                rows = slice(DH * h, DH * (h + 1))
                                last = pe.matmul(z_ps[rows, to:to + w], v[:, t, rows], probT[h][n % 2][:, 2 * P * b:2 * P * b + w],
                                                 start=t == 0, stop=last_tile)
                            if g == j:
                                last.then_inc(s_z, 1)
                        elif it[0] == "out":
                            j = it[1]
                            pe.wait_ge(s_zT, STEPS * pair + j + 1)
                            for i in range(2):
                                last = pe.matmul(o_ps[i], zT[j % 2][:, i * P:(i + 1) * P],
                                                 wo_bd[:, bass.ds(pair, 1), :, :].rearrange("f a h d -> f (a h d)"),
                                                 start=True, stop=True)
                            last.then_inc(s_o, 1)
                        elif it[0] == "project":
                            i = it[1]
                            kind, c = divmod(i, NC)
                            if i == 0:
                                pe.wait_ge(s_wfix, made + 1)
                            if not first or i >= RING:
                                free_bank(N_SC + i, pair, made)
                            pe.matmul(ring[(N_SC + i) % RING][:, :], (wk_fix, wq_fix)[kind][:, :], xnT[:, c * BANK:(c + 1) * BANK],
                                      start=True, stop=True).then_inc(s_proj, 1)
                        elif it[0] == "vproject":
                            m = it[1]
                            free_bank(V_FIRST + m, pair, made)
                            bank = ring[BANKS[V_FIRST + m]]
                            wv = wT["v"][:, bass.ds(made, 1), :].rearrange("d a f -> d (a f)")
                            for b in range(TPC):
                                t = m * TPC + b
                                last = pe.matmul(bank[:, b * P:(b + 1) * P], xnT[:, t * P:(t + 1) * P], wv, start=True, stop=True)
                            last.then_inc(s_vproj, 1)

                run(opening, 0, 0, True)
                with pe.Fori(0, PAIRS - 1) as pair:
                    run(order, pair, pair + 1, False)
                run(last_order, PAIRS - 1, PAIRS, False)

        nc.clear_and_free_semaphores(sems)
        nc.all_engine_barrier()


def layernorm_steps(keep, shp, stats, mv, rstd, s_stat, s_aggr, s_std, s_rstd):
    x = keep["x"]

    def on_vector(dve):
        for t in range(shp.NT):
            dve.bn_stats(stats[:, t, :], x[:, t, :]).then_inc(s_stat, 1)
        for t in range(shp.NT):
            dve.wait_ge(s_stat, t + 1)
            dve.bn_aggr(mv[:, t, :], stats[:, t, :]).then_inc(s_aggr, 1)
        dve.wait_ge(s_std, 1)
        dve.reciprocal(rstd[:, :], rstd[:, :]).then_inc(s_rstd, 1)
        dve.wait_ge(s_rstd, 1)

    def on_scalar(act):
        act.wait_ge(s_aggr, shp.NT)
        act.activation(rstd[:, :], mv[:, :, 1], ACT.Sqrt, bias=keep["eps"][:, 0:1]).then_inc(s_std, 1)

    return on_vector, on_scalar


def skewed(eng, tiles, ring, offsets, emit):
    deepest = max(offsets.values())
    head = -(-(deepest + ring) // ring) * ring

    def peeled(steps):
        for n in steps:
            for stage, off in offsets.items():
                if 0 <= n - off < tiles:
                    emit(stage, 0, n - off)

    peeled(range(head))
    with eng.Fori(head // ring, tiles // ring) as turn:
        for phase in range(ring):
            for stage, off in offsets.items():
                emit(stage, turn, phase - off)
    peeled(range(tiles, tiles + deepest))


def static_tile(turn, c):
    return c if isinstance(turn, int) else None


def ffn(nc, shp, keep, tag, w_red, w_g, scratch_in, scratch_out, has_stats, out=None):
    T, D, NT, NC, TPC = shp.T, shp.D, shp.NT, shp.NC, shp.TPC
    E, GD, FCH, SLOTS = shp.E, shp.GD, shp.FCH, shp.SLOTS
    x, ident, wall = keep["x"], keep["ident"], keep["wall"]
    W1, W2, B1, B2 = keep["wall_cols"]
    WCOLS = keep["wall"].shape[2]
    U = 4

    with ExitStack() as ctx:
        def sb(name, shape, dt=F32):
            return ctx.enter_context(nc.sbuf_tensor(tag + name, shape, dt))

        sems = []

        def sem(name):
            sems.append(nc.alloc_semaphore(tag + name))
            return sems[-1]

        ps = [ctx.enter_context(nc.psum_tensor(f"{tag}ps{i}", [P, BANK], F32)) for i in range(8)]
        stats, rstd, mv = sb("stats", [P, NT, 6]), sb("rstd", [P, NT]), keep["mv"]
        xn, xnT = sb("xn", [P, NT, D + 1]), sb("xnT", [D, T])
        wred, wg = sb("wred", [D, GD]), sb("wg", [E, GD])
        wg2, wgs, wgr, wgn, wgnT = sb("wg2", [E, GD]), sb("wgs", [E, 1]), sb("wgr", [E, 1]), sb("wgn", [E, GD]), sb("wgnT", [GD, E])
        wredT, gate = sb("wredT", [GD, D]), sb("gate", [D, E])
        lmax, sub, ex = sb("lmax", [P, NT]), sb("sub", [P, NT, E]), sb("ex", [P, NT, E])
        prio, best = sb("prio", [P, NT, E]), sb("best", [P, NT])
        onehot = sb("onehot", [P, E, NT], BF16)
        den, score = sb("den", [P, NT]), sb("score", [P, NT])
        cnt, incl, excl = sb("cnt", [P, E, NT]), sb("incl", [P, E, NT]), sb("excl", [P, E, NT])
        over, tiles, ends, starts = sb("over", [P, E, NT]), sb("tiles", [P, E]), sb("ends", [P, E]), sb("starts", [P, E])
        place, pos, pos_u = sb("place", [P, E, NT]), sb("pos", [P, NT]), sb("pos_u", [P, NT], U32)
        passed, slot_f, slot_e = sb("passed", [1, SLOTS, E]), sb("slot_f", [1, SLOTS]), sb("slot_e", [1, SLOTS], I32)
        xs = [sb(f"xs{k}", [P, D + 1]) for k in range(U)]
        xsT = [sb(f"xsT{k}", [D, P]) for k in range(U)]
        wfix = [sb(f"wfix{k}", [P, WCOLS]) for k in range(U)]
        hT = [sb(f"hT{k}", [P, FCH, P]) for k in range(U)]
        ys = [sb(f"ys{k}", [P, D]) for k in range(U)]
        token, back = ([sb(f"{n}{k}", [P, 1], U32) for k in range(U)] for n in ("token", "back"))
        got = sb("got", [P, NT, D])

        s_stat, s_aggr, s_std, s_rstd = sem("s_stat"), sem("s_aggr"), sem("s_std"), sem("s_rstd")
        s_gin, s_xn, s_xnTp, s_xnT = sem("s_gin"), sem("s_xn"), sem("s_xnTp"), sem("s_xnT")
        s_wg, s_wgsq, s_wgn, s_wgTp, s_wgT = sem("s_wg"), sem("s_wgsq"), sem("s_wgn"), sem("s_wgTp"), sem("s_wgT")
        s_gateP, s_gate, s_lg, s_sub, s_ex = sem("s_gateP"), sem("s_gate"), sem("s_lg"), sem("s_sub"), sem("s_ex")
        s_hot, s_rank, s_chain, s_pos, s_slot = sem("s_hot"), sem("s_rank"), sem("s_chain"), sem("s_pos"), sem("s_slot")
        s_ids, s_ready, s_scat, s_wgr, s_sum, s_out = sem("s_ids"), sem("s_ready"), sem("s_scat"), sem("s_wgr"), sem("s_sum"), sem("s_out")
        s_xs = [sem(f"s_xs{k}") for k in range(U)]
        s_xsTp, s_xsT, s_w, s_h, s_gelu, s_y, s_ys = (sem(n) for n in ("s_xsTp", "s_xsT", "s_w", "s_h", "s_gelu", "s_y", "s_ys"))
        s_store = [sem(f"s_store{k}") for k in range(U)]
        s_got = [sem(f"s_got{c}") for c in range(NC)]

        lg_ps, rank_ps = ps[6], ps[7]
        lg = lg_ps[:, 0:NT * E].rearrange("p (t e) -> p t e", e=E)
        gateT_ps, gate_ps = ps[5][0:GD, 0:D + E], ps[4][:, 0:E]
        rank = rank_ps[:, 0:E * NT].rearrange("p (e t) -> p e t", t=NT)
        count = rank_ps[:, E * NT:2 * E * NT].rearrange("p (e t) -> p e t", t=NT)

        def by_tile(ap):
            return ap.rearrange("p e t -> p t e")

        with nc.Block() as block:

            @block.sync
            def _(sp):
                sp.dma_start(wred[:, :], w_red).then_inc(s_gin, 16)
                sp.dma_start(wg[:, :], w_g).then_inc(s_wg, 16)
                sp.wait_ge(s_scat, 16 * NT)

                def emit(stage, turn, c):
                    s, k = U * turn + c, c % U
                    if static_tile(turn, c) is None or c >= U:
                        sp.wait_ge(s_xsT, s - U + 1)
                    sp.dma_start(xs[k][:, :], scratch_in[bass.ds(s * P, P), :]).then_inc(s_xs[k], 16)

                skewed(sp, SLOTS, U, {"load": 0}, emit)
                for k in range(U):
                    sp.wait_ge(s_store[k], 16 * (SLOTS // U))
                by_chunk = [ap.rearrange("(c t p) d -> c p t d", p=P, t=TPC) for ap in [scratch_out[0:T, :]] + ([] if out is None else [out])]
                for c in range(NC):
                    sp.dma_start(got[:, c * TPC:(c + 1) * TPC, :], by_chunk[0][c]).then_inc(s_got[c], 16)
                if out is not None:
                    for c in range(NC):
                        sp.wait_ge(s_sum, c + 1)
                        sp.dma_start(by_chunk[1][c], x[:, c * TPC:(c + 1) * TPC, :]).then_inc(s_out, 16)
                    sp.wait_ge(s_out, 16 * NC)

            @block.gpsimd
            def _(pool):
                pool.iota(xn[:, :, D:D + 1].bitcast(U32), pattern=[[P, NT], [0, 1]], base=0, channel_multiplier=1).then_inc(s_ids, 1)
                pool.wait_ge(s_ids, 1)
                pool.wait_ge(keep["s_scratch"], 64)
                pool.wait_ge(s_pos, 1)
                for t in range(NT):
                    pool.indirect_dma_start(scratch_in[:, :], bass.IndirectOffsetOnAxis(ap=pos_u[:, t:t + 1], axis=0),
                                            xn[:, t, :], None).then_inc(s_scat, 16)

                def emit(stage, turn, c):
                    s, k = U * turn + c, c % U
                    pool.wait_ge(s_ys, s + 1)
                    pool.sem_inc(s_ready, 1)
                    pool.indirect_dma_start(scratch_out[:, :], bass.IndirectOffsetOnAxis(ap=back[k][:, :], axis=0),
                                            ys[k][:, :], None).then_inc(s_store[k], 16)

                skewed(pool, SLOTS, U, {"store": 0}, emit)

            @block.vector
            def _(dve):
                links = [0]

                def link(ins):
                    links[0] += 1
                    ins.then_inc(s_chain, 1)
                    dve.wait_ge(s_chain, links[0])

                def gate_weights(c):
                    if c == 0:
                        dve.wait_ge(s_wg, 16)
                        link(dve.tensor_tensor(wg2[:, :], wg[:, :], wg[:, :], ALU.mult))
                        dve.tensor_reduce(wgs[:, :], wg2[:, :], AX.X, ALU.add).then_inc(s_wgsq, 1)
                    elif c == 1:
                        dve.wait_ge(s_wgr, 1)
                        link(dve.tensor_scalar(wgr[:, :], wgr[:, :], 1e-4, None, ALU.max))
                        link(dve.reciprocal(wgr[:, :], wgr[:, :]))
                        dve.tensor_scalar(wgn[:, :], wg[:, :], wgr[:, 0:1], None, ALU.mult).then_inc(s_wgn, 1)
                    elif c == 2:
                        dve.wait_ge(s_wgTp, 1)
                        dve.tensor_copy(wredT[:, :], gateT_ps[:, 0:D])
                        dve.tensor_copy(wgnT[:, :], gateT_ps[:, D:D + E]).then_inc(s_wgT, 1)
                    else:
                        dve.wait_ge(s_gateP, 1)
                        dve.tensor_copy(gate[:, :], gate_ps).then_inc(s_gate, 1)

                def statistics(c):
                    rows = range(c * TPC, (c + 1) * TPC)
                    for t in rows:
                        dve.bn_stats(stats[:, t, :], x[:, t, :]).then_inc(s_stat, 1)
                    for t in rows:
                        dve.wait_ge(s_stat, t + 1)
                        dve.bn_aggr(mv[:, t, :], stats[:, t, :]).then_inc(s_aggr, 1)

                if not has_stats:
                    statistics(0)
                for c in range(NC):
                    if not has_stats and c + 1 < NC:
                        statistics(c + 1)
                    rows = slice(c * TPC, (c + 1) * TPC)
                    dve.wait_ge(s_std, c + 1)
                    dve.reciprocal(rstd[:, rows], rstd[:, rows]).then_inc(s_rstd, 1)
                    dve.wait_ge(s_rstd, c + 1)
                    for t in range(c * TPC, (c + 1) * TPC):
                        dve.tensor_scalar(xn[:, t, 0:D], x[:, t, :], mv[:, t, 0:1], rstd[:, t:t + 1],
                                          ALU.subtract, ALU.mult).then_inc(s_xn, 1)
                    gate_weights(c)

                dve.wait_ge(s_lg, 1)
                link(dve.tensor_reduce(lmax[:, :], lg, AX.X, ALU.max))
                dve.tensor_tensor(sub[:, :, :], lg, lmax[:, :].unsqueeze(2).to_broadcast([P, NT, E]), ALU.subtract).then_inc(s_sub, 1)
                dve.wait_ge(s_sub, 1)
                link(dve.scalar_tensor_tensor(prio[:, :, :], sub[:, :, :], 0.0, keep["prio"][:, :, :], ALU.is_ge, ALU.mult))
                link(dve.tensor_reduce(best[:, :], prio[:, :, :], AX.X, ALU.max))
                dve.tensor_tensor(by_tile(onehot[:, :, :]), prio[:, :, :], best[:, :].unsqueeze(2).to_broadcast([P, NT, E]),
                                  ALU.is_equal).then_inc(s_hot, 1)
                dve.wait_ge(s_ex, 1)
                link(dve.tensor_reduce(den[:, :], ex[:, :, :], AX.X, ALU.add))
                link(dve.reciprocal(score[:, :], den[:, :]))

                dve.wait_ge(s_rank, 1)
                link(dve.tensor_copy(cnt[:, :, :], count))
                flat = [a[:, :, :].rearrange("p e t -> p (e t)") for a in (incl, keep["restart"], cnt)]
                link(dve.tensor_tensor_scan(flat[0], flat[1], flat[2], 0.0, ALU.mult, ALU.add))
                dve.tensor_tensor(excl[:, :, :], incl[:, :, :], cnt[:, :, :], ALU.subtract)
                link(dve.tensor_tensor(over[:, :, :], incl[:, :, NT - 1:NT].to_broadcast([P, E, NT]), keep["full"][:, :, :], ALU.is_gt))
                link(dve.tensor_reduce(tiles[:, :], over[:, :, :], AX.X, ALU.add))
                link(dve.tensor_tensor_scan(ends[:, :], keep["ones8"][:, :], tiles[:, :], 0.0, ALU.mult, ALU.add))
                link(dve.tensor_tensor(starts[:, :], ends[:, :], tiles[:, :], ALU.subtract))
                link(dve.scalar_tensor_tensor(place[:, :, :], starts[:, :].unsqueeze(2).to_broadcast([P, E, NT]), float(P), excl[:, :, :],
                                              ALU.mult, ALU.add))
                link(dve.tensor_tensor(place[:, :, :], rank, place[:, :, :], ALU.add))
                link(dve.tensor_tensor(place[:, :, :], place[:, :, :], onehot[:, :, :], ALU.mult))
                link(dve.tensor_reduce(pos[:, :], by_tile(place[:, :, :]), AX.X, ALU.add))
                dve.tensor_copy(pos_u[:, :], pos[:, :]).then_inc(s_pos, 1)
                link(dve.tensor_tensor(passed[:, :, :], keep["slots"][:, :, :], ends[0:1, :].unsqueeze(1).to_broadcast([1, SLOTS, E]), ALU.is_ge))
                link(dve.tensor_reduce(slot_f[:, :], passed[:, :, :], AX.X, ALU.add))
                dve.tensor_scalar(slot_e[:, :], slot_f[:, :], float(E - 1), None, ALU.min).then_inc(s_slot, 1)

                dve.wait_ge(keep["s_wall"], 16 * (2 * FCH + 2))
                dve.wait_ge(s_slot, 1)

                def emit(stage, turn, c):
                    s, k = U * turn + c, c % U
                    if stage == "weights":
                        if static_tile(turn, c) is None or c >= U:
                            dve.wait_ge(s_ys, s - U + 1)
                        e = dve.value_load(slot_e[0:1, bass.ds(s, 1)], min_val=0, max_val=E - 1)
                        dve.tensor_copy(wfix[k][:, :], wall[:, bass.ds(e, 1), :].rearrange("p a n -> p (a n)")).then_inc(s_w, 1)
                    elif stage == "xT":
                        dve.wait_ge(s_xsTp, s + 1)
                        dve.tensor_copy(token[k][:, :], xs[k][:, D:D + 1].bitcast(U32))
                        dve.tensor_copy(xsT[k][:, :], ps[c % 2][:, 0:P]).then_inc(s_xsT, 1)
                    else:
                        dve.wait_ge(s_y, s + 1)
                        if static_tile(turn, c) is None or c >= U:
                            dve.wait_ge(s_store[k], 16 * (turn + c // U))
                        dve.tensor_copy(back[k][:, :], token[k][:, :])
                        dve.tensor_tensor(ys[k][:, :], ps[4 + c % 2][:, 0:D], wfix[k][:, B2], ALU.add).then_inc(s_ys, 1)

                skewed(dve, SLOTS, U, {"xT": 1, "weights": 0, "y": 3}, emit)
                for c in range(NC):
                    dve.wait_ge(s_got[c], 16)
                    for t in range(c * TPC, (c + 1) * TPC):
                        last = dve.scalar_tensor_tensor(x[:, t, :], got[:, t, :], score[:, t:t + 1], x[:, t, :], ALU.mult, ALU.add)
                    last.then_inc(s_sum, 1)

            @block.scalar
            def _(act):
                for c in range(NC):
                    if not has_stats:
                        act.wait_ge(s_aggr, (c + 1) * TPC)
                    rows = slice(c * TPC, (c + 1) * TPC)
                    act.activation(rstd[:, rows], mv[:, rows, 1], ACT.Sqrt, bias=keep["eps"][:, 0:1]).then_inc(s_std, 1)
                    if c == 1:
                        act.wait_ge(s_wgsq, 1)
                        act.activation(wgr[:, :], wgs[:, :], ACT.Sqrt).then_inc(s_wgr, 1)
                for c in range(NC):
                    act.wait_ge(s_xnTp, c + 1)
                    act.activation(xnT[:, c * BANK:(c + 1) * BANK], ps[c][:, :], ACT.Copy).then_inc(s_xnT, 1)
                act.wait_ge(s_sub, 1)
                act.activation(ex[:, :, :], sub[:, :, :], ACT.Exp).then_inc(s_ex, 1)

                def emit(stage, turn, c):
                    s, k = U * turn + c, c % U
                    act.wait_ge(s_w, s + 1)
                    act.wait_ge(s_h, s + 1)
                    for f in range(FCH):
                        last = act.activation(hT[k][:, f, :], ps[2 + c % 2][:, f * P:(f + 1) * P], ACT.Gelu,
                                              bias=wfix[k][:, B1.start + f:B1.start + f + 1])
                    last.then_inc(s_gelu, 1)

                skewed(act, SLOTS, U, {"gelu": 2}, emit)

            @block.tensor
            def _(pe):
                for t in range(NT):
                    pe.wait_ge(s_xn, t + 1)
                    last = pe.transpose(ps[t // TPC][:, t % TPC * P:(t % TPC + 1) * P], xn[:, t, 0:D], ident[:, :])
                    if t % TPC == TPC - 1:
                        last.then_inc(s_xnTp, 1)
                    if t == 2 * TPC - 1:
                        pe.wait_ge(s_gin, 16)
                        pe.transpose(gateT_ps[:, 0:D], wred[:, :], ident[:, :])
                        pe.wait_ge(s_wgn, 1)
                        pe.transpose(gateT_ps[:, D:D + E], wgn[:, :], ident[0:E, 0:E]).then_inc(s_wgTp, 1)
                    elif t == 3 * TPC - 1:
                        pe.wait_ge(s_wgT, 1)
                        pe.matmul(gate_ps, wredT[:, :], wgnT[:, :], start=True, stop=True).then_inc(s_gateP, 1)
                pe.wait_ge(s_gate, 1)
                for t in range(NT):
                    pe.wait_ge(s_xnT, t // TPC + 1)
                    last = pe.matmul(lg[:, t, :], xnT[:, t * P:(t + 1) * P], gate[:, :], start=True, stop=True)
                last.then_inc(s_lg, 1)
                pe.wait_ge(s_hot, 1)
                hot = onehot[:, :, :].rearrange("p e t -> p (e t)")
                pe.matmul(rank_ps[:, 0:E * NT], keep["before"][:, :], hot, start=True, stop=True)
                pe.matmul(rank_ps[:, E * NT:2 * E * NT], keep["all"][:, :], hot, start=True, stop=True).then_inc(s_rank, 1)

                def emit(stage, turn, c):
                    s, k = U * turn + c, c % U
                    first = static_tile(turn, c) is not None and c < 2
                    if stage == "xT":
                        pe.wait_ge(s_xs[k], 16 * (turn + c // U + 1))
                        if not first:
                            pe.wait_ge(s_xsT, s - 1)
                        pe.transpose(ps[c % 2][:, 0:P], xs[k][:, 0:D], ident[:, :]).then_inc(s_xsTp, 1)
                    elif stage == "h":
                        pe.wait_ge(s_xsT, s + 1)
                        pe.wait_ge(s_w, s + 1)
                        if not first:
                            pe.wait_ge(s_gelu, s - 1)
                        for f in range(FCH):
                            last = pe.matmul(ps[2 + c % 2][:, f * P:(f + 1) * P], wfix[k][:, f * P:(f + 1) * P], xsT[k][:, :],
                                             start=True, stop=True)
                        last.then_inc(s_h, 1)
                    else:
                        pe.wait_ge(s_gelu, s + 1)
                        if not first:
                            pe.wait_ge(s_ys, s - 1)
                        for f in range(FCH):
                            last = pe.matmul(ps[4 + c % 2][:, 0:D], hT[k][:, f, :], wfix[k][:, W2.start + f * D:W2.start + (f + 1) * D],
                                             start=f == 0, stop=f == FCH - 1)
                        last.then_inc(s_y, 1)

                skewed(pe, SLOTS, U, {"xT": 1, "h": 2, "y": 3}, emit)

        nc.clear_and_free_semaphores(sems)
        nc.all_engine_barrier()


def linear_attention(nc, shp, keep, w_qkv, b_qkv, w_out, b_out):
    D, NT = shp.D, shp.NT
    HL, DL = shp.HL, D // shp.HL
    VX = HL * (DL + 1)
    OUTER = D * (DL + 1)
    EPS = 1e-6
    U = 2
    x, ident = keep["x"], keep["ident"]

    with ExitStack() as ctx:
        def sb(name, shape, dt=F32):
            return ctx.enter_context(nc.sbuf_tensor("li_" + name, shape, dt))

        def pair(name, shape):
            return [sb(f"{name}{k}", shape) for k in range(U)]

        sems = []

        def sem(name):
            sems.append(nc.alloc_semaphore("li_" + name))
            return sems[-1]

        sums_ps = ctx.enter_context(nc.psum_tensor("li_sums", [P, 3 * BANK], F32))
        xT_ps, z_ps, qT_ps, st_ps, y_ps = (ctx.enter_context(nc.psum_tensor("li_" + n, [P, BANK], F32))
                                           for n in ("xTp", "zp", "qTp", "stp", "yp"))
        delta, inter = qT_ps[:, P:P + VX], st_ps[:, 0:VX]
        oT_ps, out_ps = y_ps[:, 0:P], y_ps[:, P:P + D]

        stats, mv, rstd = sb("stats", [P, NT, 6]), sb("mv", [P, NT, 2]), sb("rstd", [P, NT])
        w_nat, wo_nat = sb("w_nat", [P, 3, D]), sb("wo_nat", [P, D])
        wT = sb("wT", [P, 4, P])
        b_row, bo_all = sb("b_row", [1, 3 * D]), sb("bo_all", [P, D])
        ones = sb("ones", [1, P])
        table = sb("table", [P, 2])
        upto = sb("upto", [P, P])
        block_mask = sb("block_mask", [P, HL, DL + 1])
        xn, xT = pair("xn", [P, D]), pair("xT", [D, P])
        neg, ex = pair("neg", [P, 2 * D]), pair("ex", [P, 2 * D])
        qk, v1 = pair("qk", [P, 2 * D]), pair("v1", [P, HL, DL + 1])
        outer, prod = pair("outer", [P, HL, DL, DL + 1]), sb("prod", [P, D, DL + 1])
        qT, mine, fresh, state = pair("qT", [D, P]), pair("mine", [P, VX]), pair("fresh", [P, VX]), pair("state", [P, VX])
        own, tot = sb("own", [P, HL, DL + 1]), sb("tot", [P, HL, DL + 1])
        den, o, oT = sb("den", [P, HL]), pair("o", [P, HL, DL]), pair("oT", [P, P])

        s_in, s_bias, s_bout = sem("s_in"), sem("s_bias"), sem("s_bout")
        s_c, s_const, s_init = sem("s_c"), sem("s_const"), sem("s_init")
        s_stat, s_aggr, s_std, s_rstd = sem("s_stat"), sem("s_aggr"), sem("s_std"), sem("s_rstd")
        s_wTp, s_wT, s_dcopy = sem("s_wTp"), sem("s_wT"), sem("s_dcopy")
        s_xn, s_xTp, s_xT, s_z, s_neg, s_ex, s_v, s_qk = (sem(n) for n in ("s_xn", "s_xTp", "s_xT", "s_z", "s_neg", "s_ex", "s_v", "s_qk"))
        s_outer, s_sums, s_prod, s_delta, s_fresh, s_state, s_inter = (
            sem(n) for n in ("s_outer", "s_sums", "s_prod", "s_delta", "s_fresh", "s_state", "s_inter"))
        s_qTp, s_qT, s_own, s_tot, s_den, s_rden, s_o, s_oTp, s_oT, s_out, s_xb, s_x = (
            sem(n) for n in ("s_qTp", "s_qT", "s_own", "s_tot", "s_den", "s_rden", "s_o", "s_oTp", "s_oT", "s_out", "s_xb", "s_x"))
        ln_vector, ln_scalar = layernorm_steps(keep, shp, stats, mv, rstd, s_stat, s_aggr, s_std, s_rstd)

        def first(turn, c):
            return static_tile(turn, c) == 0

        with nc.Block() as block:

            @block.sync
            def _(sp):
                sp.dma_start(w_nat[:, :, :], w_qkv.rearrange("(a p) d -> p a d", p=P)).then_inc(s_in, 16)
                sp.dma_start(wo_nat[:, :], w_out).then_inc(s_in, 16)
                sp.dma_start(b_row[:, :], b_qkv.unsqueeze(0)).then_inc(s_bias, 16)
                sp.dma_start(bo_all[:, :], b_out.unsqueeze(0).to_broadcast([P, D])).then_inc(s_bout, 16)

            @block.gpsimd
            def _(pool):
                pool.memset(upto[:, :], 1.0).then_inc(s_c, 1)
                pool.memset(block_mask[:, :, :], 1.0).then_inc(s_c, 1)
                pool.memset(ones[:, :], 1.0).then_inc(s_const, 1)
                for k in range(U):
                    pool.memset(v1[k][:, :, DL:DL + 1], 1.0).then_inc(s_const, 1)
                    pool.memset(state[k][:, :], 0.0).then_inc(s_const, 1)
                pool.wait_ge(s_c, 2)
                pool.affine_select(out=upto[:, :], in_=upto[:, :], compare_op=ALU.is_ge, fill=0.0, base=0,
                                   pattern=[[1, P]], channel_multiplier=-1).then_inc(s_const, 1)
                pool.affine_select(out=block_mask[:, :, :], in_=block_mask[:, :, :], compare_op=ALU.is_ge, fill=0.0, base=0,
                                   pattern=[[-DL, HL], [0, DL + 1]], channel_multiplier=1).then_inc(s_c, 1)
                pool.wait_ge(s_c, 3)
                pool.affine_select(out=block_mask[:, :, :], in_=block_mask[:, :, :], compare_op=ALU.is_ge, fill=0.0, base=DL - 1,
                                   pattern=[[DL, HL], [0, DL + 1]], channel_multiplier=-1).then_inc(s_const, 1)
                pool.wait_ge(s_const, 2 * U + 3)
                pool.wait_ge(s_bout, 16)

                def emit(stage, turn, c):
                    t, k = U * turn + c, c % U
                    if stage == "bias":
                        pool.wait_ge(s_xn, t + 1)
                        rows = x[:, bass.ds(t, 1), :].rearrange("p a d -> p (a d)")
                        pool.tensor_tensor(rows, rows, bo_all[:, :], ALU.add).then_inc(s_xb, 1)
                    elif stage == "state":
                        pool.wait_ge(s_dcopy, t + 1)
                        pool.tensor_tensor(fresh[k][:, :], mine[k][:, :], block_mask[:, :, :].rearrange("p h e -> p (h e)"), ALU.mult).then_inc(s_fresh, 1)
                        pool.wait_ge(s_fresh, t + 1)
                        if not first(turn, c):
                            pool.wait_ge(s_state, t)
                        pool.tensor_tensor(state[k][:, :], state[1 - k][:, :], fresh[k][:, :], ALU.add).then_inc(s_state, 1)
                    else:
                        pool.wait_ge(s_qk, t + 1)
                        pool.wait_ge(s_v, t + 1)
                        kk = qk[k][:, D:2 * D].rearrange("p (h d) -> p h d", d=DL).unsqueeze(3).to_broadcast([P, HL, DL, DL + 1])
                        vv = v1[k][:, :, :].unsqueeze(2).to_broadcast([P, HL, DL, DL + 1])
                        pool.tensor_tensor(outer[k][:, :, :, :], kk, vv, ALU.mult).then_inc(s_outer, 1)

                skewed(pool, NT, U, {"bias": 0, "outer": 1, "state": 2}, emit)

            @block.vector
            def _(dve):
                ln_vector(dve)
                dve.wait_ge(s_const, 2 * U + 3)

                def emit(stage, turn, c):
                    t, k = U * turn + c, c % U
                    if stage == "norm":
                        rows = x[:, bass.ds(t, 1), :].rearrange("p a d -> p (a d)")
                        mean = mv[:, bass.ds(t, 1), 0:1].rearrange("p a b -> p (a b)")
                        dve.tensor_scalar(xn[k][:, :], rows, mean, rstd[:, bass.ds(t, 1)], ALU.subtract, ALU.mult).then_inc(s_xn, 1)
                    elif stage == "y":
                        dve.wait_ge(s_out, t + 1)
                        dve.wait_ge(s_xb, t + 1)
                        rows = x[:, bass.ds(t, 1), :].rearrange("p a d -> p (a d)")
                        dve.tensor_tensor(rows, out_ps, rows, ALU.add).then_inc(s_x, 1)
                    elif stage == "sums":
                        dve.wait_ge(s_sums, t + 1)
                        dve.tensor_tensor(prod[:, :, :], sums_ps[:, 0:OUTER].rearrange("p (c e) -> p c e", e=DL + 1),
                                          qk[k][:, 0:D].unsqueeze(2).to_broadcast([P, D, DL + 1]), ALU.mult).then_inc(s_prod, 1)
                    elif stage == "features":
                        dve.wait_ge(s_ex, t + 1)
                        dve.scalar_tensor_tensor(qk[k][:, :], z_ps[:, 0:2 * D], 0.0, ex[k][:, :], ALU.max, ALU.add).then_inc(s_qk, 1)
                    else:
                        dve.wait_ge(s_prod, t + 1)
                        dve.tensor_reduce(own[:, :, :], prod[:, :, :].rearrange("p (h d) e -> p h e d", d=DL), AX.X, ALU.add).then_inc(s_own, 1)
                        dve.wait_ge(s_inter, t + 1)
                        dve.wait_ge(s_own, t + 1)
                        dve.tensor_tensor(tot[:, :, :], inter.rearrange("p (h e) -> p h e", e=DL + 1), own[:, :, :], ALU.add).then_inc(s_tot, 1)
                        dve.wait_ge(s_tot, t + 1)
                        dve.tensor_scalar(den[:, :].unsqueeze(2), tot[:, :, DL:DL + 1], EPS, None, ALU.add).then_inc(s_den, 1)
                        dve.wait_ge(s_den, t + 1)
                        dve.reciprocal(den[:, :], den[:, :]).then_inc(s_rden, 1)
                        dve.wait_ge(s_rden, t + 1)
                        dve.tensor_tensor(o[k][:, :, :], tot[:, :, 0:DL], den[:, :].unsqueeze(2).to_broadcast([P, HL, DL]), ALU.mult).then_inc(s_o, 1)

                skewed(dve, NT, U, {"norm": 0, "y": 5, "heads": 3, "features": 1, "sums": 2}, emit)

            @block.scalar
            def _(act):
                act.activation(table[:, 0:1], keep["eps"][:, 0:1], ACT.Sqrt)
                act.wait_ge(s_const, 2 * U + 3)
                ln_scalar(act)
                act.activation(table[:, 1:2], keep["eps"][:, 0:1], ACT.Exp)
                act.wait_ge(s_wTp, 1)
                act.activation(wT[:, :, :].rearrange("p a f -> p (a f)"), sums_ps[:, 0:BANK], ACT.Copy).then_inc(s_wT, 1)

                def emit(stage, turn, c):
                    t, k = U * turn + c, c % U
                    if stage == "qT":
                        act.wait_ge(s_qTp, t + 1)
                        act.activation(qT[k][:, :], qT_ps[:, 0:P], ACT.Copy).then_inc(s_qT, 1)
                    elif stage == "delta":
                        act.wait_ge(s_delta, t + 1)
                        act.activation(mine[k][:, :], delta, ACT.Copy).then_inc(s_dcopy, 1)
                    elif stage == "xT":
                        act.wait_ge(s_xTp, t + 1)
                        act.activation(xT[k][:, :], xT_ps[:, 0:P], ACT.Copy).then_inc(s_xT, 1)
                    elif stage == "z":
                        act.wait_ge(s_z, t + 1)
                        act.activation(neg[k][:, :], z_ps[:, 0:2 * D], ACT.Relu, scale=-1.0).then_inc(s_neg, 1)
                        act.activation(v1[k][:, :, 0:DL], z_ps[:, 2 * D:3 * D].rearrange("p (h e) -> p h e", e=DL), ACT.Copy).then_inc(s_v, 1)
                        act.wait_ge(s_neg, t + 1)
                        act.activation(ex[k][:, :], neg[k][:, :], ACT.Exp, scale=-1.0).then_inc(s_ex, 1)
                    else:
                        act.wait_ge(s_oTp, t + 1)
                        act.activation(oT[k][:, :], oT_ps, ACT.Copy).then_inc(s_oT, 1)

                skewed(act, NT, U, {"qT": 2, "z": 1, "xT": 0, "delta": 2, "oT": 4}, emit)

            @block.tensor
            def _(pe):
                pe.wait_ge(s_in, 32)
                for a in range(3):
                    pe.transpose(sums_ps[:, a * P:(a + 1) * P], w_nat[:, a, :], ident[:, :])
                pe.transpose(sums_ps[:, 3 * P:4 * P], wo_nat[:, :], ident[:, :]).then_inc(s_wTp, 1)
                pe.wait_ge(s_const, 2 * U + 3)
                pe.wait_ge(s_bias, 16)
                pe.wait_ge(s_wT, 1)

                def emit(stage, turn, c):
                    t, k = U * turn + c, c % U
                    if stage == "y":
                        pe.wait_ge(s_oT, t + 1)
                        pe.matmul(out_ps, oT[k][:, :], wT[:, 3, :], start=True, stop=True).then_inc(s_out, 1)
                    elif stage == "qT":
                        pe.wait_ge(s_qk, t + 1)
                        if not first(turn, c):
                            pe.wait_ge(s_dcopy, t)
                        pe.transpose(qT_ps[:, 0:P], qk[k][:, 0:D], ident[:, :]).then_inc(s_qTp, 1)
                    elif stage == "sums":
                        pe.wait_ge(s_v, t + 1)
                        pe.wait_ge(s_qT, t + 1)
                        pe.matmul(delta, qk[k][:, D:2 * D], v1[k][:, :, :].rearrange("p h e -> p (h e)"),
                                  start=True, stop=True).then_inc(s_delta, 1)
                        pe.wait_ge(s_outer, t + 1)
                        if not first(turn, c):
                            pe.wait_ge(s_prod, t)
                        flat = outer[k][:, :, :, :].rearrange("p h d e -> p (h d e)")
                        for a in range(0, OUTER, BANK):
                            b = min(a + BANK, OUTER)
                            last = pe.matmul(sums_ps[:, a:b], upto[:, :], flat[:, a:b], start=True, stop=True)
                        last.then_inc(s_sums, 1)
                        if not first(turn, c):
                            pe.wait_ge(s_tot, t)
                            pe.wait_ge(s_state, t)
                        pe.matmul(inter, qT[k][:, :], state[1 - k][:, :], start=True, stop=True).then_inc(s_inter, 1)
                    elif stage == "xT":
                        pe.wait_ge(s_xn, t + 1)
                        if not first(turn, c):
                            pe.wait_ge(s_xT, t)
                        pe.transpose(xT_ps[:, 0:P], xn[k][:, :], ident[:, :]).then_inc(s_xTp, 1)
                    elif stage == "z":
                        pe.wait_ge(s_xT, t + 1)
                        if not first(turn, c):
                            pe.wait_ge(s_qk, t)
                            pe.wait_ge(s_v, t)
                        pe.matmul(z_ps[:, 0:3 * D], xT[k][:, :], wT[:, 0:3, :].rearrange("p a f -> p (a f)"), start=True, stop=False)
                        pe.matmul(z_ps[:, 0:3 * D], ones[:, :], b_row[:, :], start=False, stop=True).then_inc(s_z, 1)
                    else:
                        pe.wait_ge(s_o, t + 1)
                        if not first(turn, c):
                            pe.wait_ge(s_x, t)
                        pe.transpose(oT_ps, o[k][:, :, :].rearrange("p h e -> p (h e)"), ident[:, :]).then_inc(s_oTp, 1)

                skewed(pe, NT, U, {"y": 5, "qT": 2, "z": 1, "xT": 0, "sums": 2, "oT": 4}, emit)

        nc.clear_and_free_semaphores(sems)
        nc.all_engine_barrier()


def prepare(nc, shp, keep, f_w1, f_b1, f_w2, f_b2, scratch_ins):
    E, FCH, D, NT, SLOTS = shp.E, shp.FCH, shp.D, shp.NT, shp.SLOTS
    W1, W2, B1, B2 = keep["wall_cols"]
    wall = keep["wall"]
    s_z, s_c = keep["s_z"], keep["s_c"]
    with nc.Block() as block:

        @block.vector
        def _(dve):
            dve.memset(keep["eps"][:, :], LN_EPS)
            dve.memset(keep["zeros"][:, :], 0.0).then_inc(s_z, 1)
            dve.memset(keep["ones8"][:, :], 1.0)
            dve.memset(keep["all"][:, :], 1.0)
            dve.wait_ge(s_c, 1)
            dve.tensor_scalar(keep["restart"][:, :, :], keep["restart"][:, :, :], 1.0, None, ALU.min)

        @block.gpsimd
        def _(pool):
            pool.iota(keep["restart"][:, :, :], pattern=[[0, E], [1, NT]], base=0, channel_multiplier=0,
                      allow_small_or_imprecise_dtypes=True).then_inc(s_c, 1)
            pool.iota(keep["full"][:, :, :], pattern=[[0, E], [P, NT]], base=0, channel_multiplier=0,
                      allow_small_or_imprecise_dtypes=True)
            pool.iota(keep["prio"][:, :, :], pattern=[[0, NT], [-1, E]], base=E, channel_multiplier=0,
                      allow_small_or_imprecise_dtypes=True)
            pool.iota(keep["slots"][:, :, :], pattern=[[1, SLOTS], [0, E]], base=0, channel_multiplier=0,
                      allow_small_or_imprecise_dtypes=True)
            pool.iota(keep["unused"][:, :], pattern=[[P, SLOTS]], base=shp.T, channel_multiplier=1).then_inc(s_z, 1)
            pool.memset(keep["before"][:, :], 1.0).then_inc(s_c, 1)
            pool.wait_ge(s_c, 2)
            pool.affine_select(out=keep["before"][:, :], in_=keep["before"][:, :], compare_op=ALU.is_gt, fill=0.0, base=0,
                               pattern=[[1, P]], channel_multiplier=-1)

    def fetch(sp):
        sp.wait_ge(s_z, 2)
        for scratch in scratch_ins:
            rows = scratch.rearrange("(s p) d -> p s d", p=P)
            sp.dma_start(rows[:, :, 0:D], keep["zeros"][:, :].unsqueeze(1).to_broadcast([P, SLOTS, D])).then_inc(keep["s_scratch"], 16)
            sp.dma_start(rows[:, :, D:D + 1], keep["unused"][:, :].bitcast(F32).unsqueeze(2),
                         allow_slow_non_contiguous=True).then_inc(keep["s_scratch"], 16)
        sp.dma_start(wall[:, :, W1], f_w1.rearrange("e d f -> d e f")).then_inc(keep["s_wall"], 16)
        for f in range(FCH):
            sp.dma_start(wall[:, :, W2.start + f * D:W2.start + (f + 1) * D],
                         f_w2[:, f * P:(f + 1) * P, :].rearrange("e p d -> p e d")).then_inc(keep["s_wall"], 16)
            sp.dma_start(wall[:, :, B1.start + f:B1.start + f + 1],
                         f_b1[:, f * P:(f + 1) * P].rearrange("e (p a) -> p e a", a=1), allow_slow_non_contiguous=True).then_inc(keep["s_wall"], 16)
        sp.dma_start(wall[:, :, B2], f_b2.unsqueeze(0).to_broadcast([P, E, D])).then_inc(keep["s_wall"], 16)

    return fetch


def bass_hybrid_layers(nc, a_x, w_k, w_q, w_v, w_o, b_wqkv, b_bqkv, b_wout, b_bout,
                       f_wred, f_wg, f_w1, f_b1, f_w2, f_b2, out):
    shp = Shapes(a_x, w_k, f_wg, f_w1)
    NT, D, E = shp.NT, shp.D, shp.E
    hid = shp.FCH * P
    scratch_in = [nc.dram_tensor(f"slots_in{i}", (shp.SLOTS * P, D + 1), F32).ap() for i in range(2)]
    scratch_out = [nc.dram_tensor(f"slots_out{i}", (shp.T + shp.SLOTS * P, D), F32).ap() for i in range(2)]
    with ExitStack() as ctx:
        def sb(name, shape, dt=F32):
            return ctx.enter_context(nc.sbuf_tensor(name, shape, dt))

        keep = {
            "x": sb("x", [P, NT, D]), "ident": sb("ident", [P, P]), "eps": sb("eps", [P, 1]), "zeros": sb("zeros", [P, D]),
            "wall": sb("wall", [P, E, 2 * hid + shp.FCH + D]),
            "wall_cols": (slice(0, hid), slice(hid, 2 * hid), slice(2 * hid, 2 * hid + shp.FCH),
                          slice(2 * hid + shp.FCH, 2 * hid + shp.FCH + D)),
            "restart": sb("restart", [P, E, NT]), "full": sb("full", [P, E, NT]), "prio": sb("prio", [P, NT, E]),
            "slots": sb("slots", [1, shp.SLOTS, E]), "unused": sb("unused", [P, shp.SLOTS], U32), "mv": sb("mv", [P, NT, 2]), "ones8": sb("ones8", [P, E]),
            "before": sb("before", [P, P], BF16), "all": sb("all", [P, P], BF16),
        }
        for n in ("s_z", "s_c", "s_scratch", "s_wall"):
            keep[n] = ctx.enter_context(nc.semaphore(n))
        fetch = prepare(nc, shp, keep, f_w1, f_b1, f_w2, f_b2, scratch_in)
        attention(nc, shp, keep, a_x, w_k, w_q, w_v, w_o, fetch)
        ffn(nc, shp, keep, "f0_", f_wred, f_wg, scratch_in[0], scratch_out[0], True)
        linear_attention(nc, shp, keep, b_wqkv, b_bqkv, b_wout, b_bout)
        ffn(nc, shp, keep, "f1_", f_wred, f_wg, scratch_in[1], scratch_out[1], False, out[0])


_INS = ['L0_attn_a_x', 'L0_attn_a_W_K', 'L0_attn_a_W_Q', 'L0_attn_a_W_V', 'L0_attn_a_W_O',
        'L0_attn_b_w_qkv', 'L0_attn_b_b_qkv', 'L0_attn_b_w_out', 'L0_attn_b_b_out',
        'L0_ffn_w_red', 'L0_ffn_wg', 'L0_ffn_w1', 'L0_ffn_b1', 'L0_ffn_w2', 'L0_ffn_b2']
_OUTS = [((1, 2048, 128), 'float32')]


def kernel(**inputs):
    import numpy as _np
    import concourse.bacc as _bacc
    from concourse import mybir as _mybir
    from concourse.bass_utils import run_bass_kernel_spmd as _run

    nc = _bacc.Bacc("TRN2", target_bir_lowering=False, num_devices=1)
    arrays, args = {}, []
    for name in _INS:
        a = _np.ascontiguousarray(inputs[name])
        arrays[f"in_{name}_dram"] = a
        args.append(nc.dram_tensor(f"in_{name}_dram", a.shape, _mybir.dt.from_np(a.dtype), kind="ExternalInput").ap())
    for i, (shape, dtype) in enumerate(_OUTS):
        dt = _mybir.dt.from_np(_np.dtype(dtype))
        args.append(nc.dram_tensor(f"out_{i}_dram", shape, dt, kind="ExternalOutput").ap())
    bass_hybrid_layers(nc, *args)
    r = _run(nc, [arrays], core_ids=[0])
    got = tuple(r.results[0][f"out_{i}_dram"] for i in range(len(_OUTS)))
    return got[0]
```
